# Optimizing a Trainium2 kernel written in Bass

```python
import numpy as np
import jax
import jax.numpy as jnp

def _softmax(x, axis=-1):
    return jax.nn.softmax(x, axis=axis)

def _gelu(x):
    return jax.nn.gelu(x, approximate=True)

def _silu(x):
    return jax.nn.silu(x)

def _sigmoid(x):
    return jax.nn.sigmoid(x)

def _layernorm(x, axis=-1, eps=1e-05):
    m = jnp.mean(x, axis=axis, keepdims=True)
    v = jnp.var(x, axis=axis, keepdims=True)
    return (x - m) / jnp.sqrt(v + eps)

def _scatter_add(tgt, idx, src, axis=0):
    return tgt.at[idx].add(src)

def _segment_sum(src, seg, n):
    return jax.ops.segment_sum(src, seg, n)
kernel_name = 'mk_seq_preln_d1_jaxref_r8_b81445'

def setup_inputs(seed: int=0):
    np.random.seed(seed)
    _w = jnp.asarray

    def _L0_attn_setup():
        import jax, jax.numpy as jnp
        import numpy as np
        B, S, D, H = (2, 256, 128, 16)
        HD = D // H
        key = jax.random.key(seed)
        ks = jax.random.split(key, 16)
        sc = 0.02
        return {'hidden_states': jax.random.normal(ks[0], (B, S, D), jnp.float32), 'Wq': jax.random.normal(ks[1], (D, D), jnp.float32) * sc, 'bq': jnp.zeros((D,), jnp.float32), 'Wk': jax.random.normal(ks[2], (D, D), jnp.float32) * sc, 'bk': jnp.zeros((D,), jnp.float32), 'Wv': jax.random.normal(ks[3], (D, D), jnp.float32) * sc, 'bv': jnp.zeros((D,), jnp.float32), 'Wo': jax.random.normal(ks[4], (D, D), jnp.float32) * sc, 'bo': jnp.zeros((D,), jnp.float32), 'rel_W': jax.random.normal(ks[5], (3, 2 * D), jnp.float32) * sc, 'rel_b': jnp.zeros((3,), jnp.float32), 'logical_bias': jax.random.normal(ks[6], (H, 3), jnp.float32) * sc, 'gate_W': jax.random.normal(ks[7], (H, D), jnp.float32) * sc, 'gate_b': jnp.zeros((H,), jnp.float32)}
    _L0_attn_in = _L0_attn_setup()

    def _L0_ffn_setup():
        import jax, jax.numpy as jnp
        import numpy as np
        SQRT_2_PI = 0.7978845608028654
        GELU_COEF = 0.044715
        LN_EPS = 1e-06
        TOP_K = 2

        def gelu_kernel(x):
            inner = SQRT_2_PI * (x + GELU_COEF * x ** 3)
            return 0.5 * x * (1.0 + jnp.tanh(inner))
        key = jax.random.key(seed)
        ks = jax.random.split(key, 8)
        B, S, D, F, E = (2, 256, 128, 512, 8)
        s = lambda d: 1.0 / np.sqrt(d)
        return {'x': jax.random.normal(ks[0], (B, S, D), jnp.float32), 'Wr1': jax.random.normal(ks[1], (D, D // 2), jnp.float32) * s(D), 'br1': jnp.zeros((D // 2,), jnp.float32), 'ln_scale': jnp.ones((D // 2,), jnp.float32), 'ln_bias': jnp.zeros((D // 2,), jnp.float32), 'Wr2': jax.random.normal(ks[2], (D // 2, E), jnp.float32) * s(D // 2), 'br2': jnp.zeros((E,), jnp.float32), 'W1': jax.random.normal(ks[3], (E, D, 2 * F), jnp.float32) * s(D), 'b1': jnp.zeros((E, 2 * F), jnp.float32), 'W2': jax.random.normal(ks[4], (E, F, D), jnp.float32) * s(F), 'b2': jnp.zeros((E, D), jnp.float32)}
    _L0_ffn_in = _L0_ffn_setup()
    _d = {'L0_attn_hidden_states': _L0_attn_in['hidden_states'], 'L0_attn_Wq': _L0_attn_in['Wq'], 'L0_attn_bq': _L0_attn_in['bq'], 'L0_attn_Wk': _L0_attn_in['Wk'], 'L0_attn_bk': _L0_attn_in['bk'], 'L0_attn_Wv': _L0_attn_in['Wv'], 'L0_attn_bv': _L0_attn_in['bv'], 'L0_attn_Wo': _L0_attn_in['Wo'], 'L0_attn_bo': _L0_attn_in['bo'], 'L0_attn_rel_W': _L0_attn_in['rel_W'], 'L0_attn_rel_b': _L0_attn_in['rel_b'], 'L0_attn_logical_bias': _L0_attn_in['logical_bias'], 'L0_attn_gate_W': _L0_attn_in['gate_W'], 'L0_attn_gate_b': _L0_attn_in['gate_b'], 'L0_ffn_Wr1': _L0_ffn_in['Wr1'], 'L0_ffn_br1': _L0_ffn_in['br1'], 'L0_ffn_ln_scale': _L0_ffn_in['ln_scale'], 'L0_ffn_ln_bias': _L0_ffn_in['ln_bias'], 'L0_ffn_Wr2': _L0_ffn_in['Wr2'], 'L0_ffn_br2': _L0_ffn_in['br2'], 'L0_ffn_W1': _L0_ffn_in['W1'], 'L0_ffn_b1': _L0_ffn_in['b1'], 'L0_ffn_W2': _L0_ffn_in['W2'], 'L0_ffn_b2': _L0_ffn_in['b2']}
    _x0 = _d['L0_attn_hidden_states']
    _d['L0_attn_hidden_states'] = jax.random.normal(jax.random.fold_in(jax.random.key(seed), 1), (1, 2048, 128), dtype=_x0.dtype)
    del _x0
    return _d

def reference(L0_attn_hidden_states, L0_attn_Wq, L0_attn_bq, L0_attn_Wk, L0_attn_bk, L0_attn_Wv, L0_attn_bv, L0_attn_Wo, L0_attn_bo, L0_attn_rel_W, L0_attn_rel_b, L0_attn_logical_bias, L0_attn_gate_W, L0_attn_gate_b, L0_ffn_Wr1, L0_ffn_br1, L0_ffn_ln_scale, L0_ffn_ln_bias, L0_ffn_Wr2, L0_ffn_br2, L0_ffn_W1, L0_ffn_b1, L0_ffn_W2, L0_ffn_b2):

    def _L0_attn_ref(hidden_states, Wq, bq, Wk, bk, Wv, bv, Wo, bo, rel_W, rel_b, logical_bias, gate_W, gate_b):
        import jax, jax.numpy as jnp
        import numpy as np
        B, S, D, H = (2, 256, 128, 16)
        HD = D // H
        x = hidden_states
        b, s, d = x.shape
        h = gate_W.shape[0]
        hd = d // h
        scale = hd ** 0.5
        q = (x @ Wq.T + bq).reshape(b, s, h, hd)
        k = (x @ Wk.T + bk).reshape(b, s, h, hd)
        v = (x @ Wv.T + bv).reshape(b, s, h, hd)
        attn_scores = jnp.einsum('bihd,bjhd->bhij', q, k) / scale
        li = x @ rel_W[:, :d].T
        lj = x @ rel_W[:, d:].T
        logits = li[:, :, None, :] + lj[:, None, :, :] + rel_b
        relation_probs = jax.nn.softmax(logits, axis=-1)
        bias = jnp.einsum('bijk,hk->bhij', relation_probs, logical_bias)
        gate = jax.nn.sigmoid(x @ gate_W.T + gate_b)
        gate = jnp.transpose(gate, (0, 2, 1))[..., None]
        attn_scores = attn_scores + gate * bias
        attn_weights = jax.nn.softmax(attn_scores, axis=-1)
        out = jnp.einsum('bhij,bjhd->bihd', attn_weights, v).reshape(b, s, d)
        return out @ Wo.T + bo

    def _L0_ffn_ref(x, Wr1, br1, ln_scale, ln_bias, Wr2, br2, W1, b1, W2, b2):
        import jax, jax.numpy as jnp
        import numpy as np
        SQRT_2_PI = 0.7978845608028654
        GELU_COEF = 0.044715
        LN_EPS = 1e-06
        TOP_K = 2

        def gelu_kernel(x):
            inner = SQRT_2_PI * (x + GELU_COEF * x ** 3)
            return 0.5 * x * (1.0 + jnp.tanh(inner))
        E = W1.shape[0]
        h = jnp.einsum('bsd,dk->bsk', x, Wr1) + br1
        mu = jnp.mean(h, axis=-1, keepdims=True)
        var = jnp.mean((h - mu) ** 2, axis=-1, keepdims=True)
        h = (h - mu) * jax.lax.rsqrt(var + LN_EPS) * ln_scale + ln_bias
        h = gelu_kernel(h)
        router_logits = jnp.einsum('bsk,ke->bse', h, Wr2) + br2
        routing_probs = jax.nn.softmax(router_logits, axis=-1)
        top_k_probs, top_k_indices = jax.lax.top_k(routing_probs, TOP_K)
        top_k_probs = top_k_probs / jnp.sum(top_k_probs, axis=-1, keepdims=True)
        expert_mask = jnp.sum(jax.nn.one_hot(top_k_indices, E, dtype=x.dtype) * top_k_probs[..., None], axis=-2)
        output = jnp.zeros_like(x)
        for e in range(E):
            x12 = jnp.einsum('bsd,df->bsf', x, W1[e]) + b1[e]
            x1, x2 = jnp.split(x12, 2, axis=-1)
            g = x1 * gelu_kernel(x2)
            y = jnp.einsum('bsf,fd->bsd', g, W2[e]) + b2[e]
            output = output + y * expert_mask[:, :, e][:, :, None]
        return output
    x = L0_attn_hidden_states
    x = x + _L0_attn_ref(_layernorm(x, axis=-1), L0_attn_Wq, L0_attn_bq, L0_attn_Wk, L0_attn_bk, L0_attn_Wv, L0_attn_bv, L0_attn_Wo, L0_attn_bo, L0_attn_rel_W, L0_attn_rel_b, L0_attn_logical_bias, L0_attn_gate_W, L0_attn_gate_b)
    x = x + _L0_ffn_ref(_layernorm(x, axis=-1), L0_ffn_Wr1, L0_ffn_br1, L0_ffn_ln_scale, L0_ffn_ln_bias, L0_ffn_Wr2, L0_ffn_br2, L0_ffn_W1, L0_ffn_b1, L0_ffn_W2, L0_ffn_b2)
    return x

_drawn_inputs = setup_inputs


def setup_inputs(seed=0):
    import zlib

    import numpy as np

    out = dict(_drawn_inputs(seed))
    spreads = {'L0_attn_bq': (0.0, 0.8),
     'L0_attn_bk': (0.0, 2.0),
     'L0_attn_bv': (0.0, 0.1),
     'L0_attn_bo': (0.0, 0.1),
     'L0_attn_rel_b': (0.0, 2.0),
     'L0_attn_gate_b': (0.0, 2.0),
     'L0_ffn_br1': (0.0, 0.1),
     'L0_ffn_ln_scale': (1.0, 0.2),
     'L0_ffn_ln_bias': (0.0, 0.1),
     'L0_ffn_br2': (0.0, 0.1),
     'L0_ffn_b1': (0.0, 0.1),
     'L0_ffn_b2': (0.0, 0.1)}
    factors = {'L0_attn_Wq': 8.0,
     'L0_attn_Wk': 8.0,
     'L0_attn_Wv': 8.0,
     'L0_attn_rel_W': 27.233,
     'L0_attn_logical_bias': 23.649,
     'L0_attn_gate_W': 29.699}
    for name, (base, spread) in spreads.items():
        noise = np.random.default_rng([zlib.crc32(name.encode()), seed]).standard_normal(out[name].shape)
        drawn = base * np.exp(spread * noise) if base else spread * noise
        out[name] = jnp.asarray(drawn.astype(out[name].dtype))
    for name, factor in factors.items():
        out[name] = (out[name] * factor).astype(out[name].dtype)
    return out
```

```python
from contextlib import ExitStack

import concourse.bass as bass
from concourse import mybir

F32 = mybir.dt.float32
F16 = mybir.dt.float16
BF16 = mybir.dt.bfloat16
ALU = mybir.AluOpType
ACT = mybir.ActivationFunctionType
AX_X = mybir.AxisListType.X

P = 128
S, D = 2048, 128
H, HD = 16, 8
T = S // P
PAIRS = H // 2
SLOTS = 6
QPART = [0, 0, 1, 0, 2, 1]
KPART = [0, 1, 0, 2, 0, 1]
ROWS = 2 * SLOTS * HD
SROWS = ROWS + 2 * 3
IB = 16
BLOCKS = P // IB
CHUNKS = 2
CW = S // CHUNKS
JC = CW // P
VW = HD + 1
NS = 512
MAXS = S // NS * H
E, F = 8, 512
FT = F // P
R1 = 64
FC = S // NS
LN_EPS, ROUTER_EPS = 1e-5, 1e-6

CONST = [("wqT", D), ("wkT", D), ("wvT", D), ("woT", D), ("relI", 3), ("relJ", 3), ("gateT", H),
         ("bq", 1), ("bk", 1), ("bv", D), ("bo", D), ("relb", 3), ("gateb", H), ("bias", 3 * H),
         ("ident", P), ("diag", IB), ("wr1", R1), ("br1", R1), ("lns", R1), ("lnb", R1), ("wr2", E),
         ("br2", E), ("b2", D), ("own", T), ("before", E * E), ("b1", E * 2 * FT)]
AT, n = {}, 0
for _name, _w in CONST:
    AT[_name] = slice(n, n + _w)
    n += _w
CW_ALL = n


def build(nc, x, consts, w1, w2, out):
    q_dram = nc.dram_tensor("q_parts", [3, P, S], BF16, kind="Internal").ap()
    k_dram = nc.dram_tensor("k_parts", [3, P, S], BF16, kind="Internal").ap()
    a_dram = nc.dram_tensor("a_parts", [S, 4, H], F16, kind="Internal").ap()

    ctx = ExitStack()
    with ctx:
        def sb(name, shape, dt, c=ctx):
            return c.enter_context(nc.sbuf_tensor(name, shape, dt))

        def sem(name, c=ctx):
            return c.enter_context(nc.semaphore(name))

        psS = ctx.enter_context(nc.psum_tensor("psS", [P, 2, 2 * NS], F32))
        psO = ctx.enter_context(nc.psum_tensor("psO", [P, NS], F32))
        psM = ctx.enter_context(nc.psum_tensor("psM", [P, 2, NS], F32))
        psX = ctx.enter_context(nc.psum_tensor("psX", [P, NS], F32))
        banks = [psS[:, 0, 0:NS], psS[:, 0, NS:], psS[:, 1, 0:NS], psS[:, 1, NS:],
                 psO[:, :], psM[:, 0, :], psM[:, 1, :], psX[:, :]]

        cst = sb("cst", [P, CW_ALL], F32)

        def C(name):
            return cst[:, AT[name]]

        xs = sb("xs", [P, T, D], F32)
        stats = sb("stats", [P, T, 6], F32)
        mv = sb("mv", [P, T, 2], F32)
        rstd = sb("rstd", [P, T], F32)
        var = sb("var", [P, T], F32)
        newton = sb("newton", [P, T], F32)

        attention(nc, ctx, sb, sem, locals())
        experts(nc, sb, sem, locals())


RSTD = 7


def rstd_first(nc, pool, done, eps, g):
    nc.gpsimd.tensor_scalar(g["var"][:, :], g["mv"][:, :, 1], eps, None, ALU.add).then_inc(done, 1)


def rstd_reciprocal(nc, dve, done, g):
    dve.wait_ge(done, 1)
    nc.vector.reciprocal(g["rstd"][:, :], g["var"][:, :]).then_inc(done, 1)


def rstd_root(nc, act, done, g):
    act.wait_ge(done, 2)
    nc.scalar.activation(g["rstd"][:, :], g["rstd"][:, :], ACT.Sqrt).then_inc(done, 1)


def rstd_step(nc, pool, done, g):
    rstd, var, newton = g["rstd"][:, :], g["var"][:, :], g["newton"][:, :]
    pool.wait_ge(done, 3)
    nc.gpsimd.tensor_tensor(newton, rstd, rstd, ALU.mult).then_inc(done, 1)
    pool.wait_ge(done, 4)
    nc.gpsimd.tensor_tensor(newton, newton, var, ALU.mult).then_inc(done, 1)
    pool.wait_ge(done, 5)
    nc.gpsimd.tensor_scalar(newton, newton, -0.5, 1.5, ALU.mult, ALU.add).then_inc(done, 1)
    pool.wait_ge(done, 6)
    nc.gpsimd.tensor_tensor(rstd, rstd, newton, ALU.mult).then_inc(done, 1)


def attention(nc, outer, sb, sem, g):
    C, xs, banks = g["C"], g["xs"], g["banks"]
    psS, psO, psM, psX = g["psS"], g["psO"], g["psM"], g["psX"]
    stats, mv, rstd, cst = g["stats"], g["mv"], g["rstd"], g["cst"]
    q_dram, k_dram, a_dram = g["q_dram"], g["k_dram"], g["a_dram"]
    with ExitStack() as ctx:
        kst = sb("kst", [SROWS, PAIRS, S], BF16, ctx)
        V = sb("V", [P, T, H, VW], F32, ctx)
        beta = sb("beta", [P, 2, S], F32, ctx)
        alpha = sb("alpha", [P, T, 2], F32, ctx)
        gtop = sb("gtop", [P, T, H], F32, ctx)
        ast = sb("ast", [P, T * BLOCKS, H], F16, ctx)
        diag = sb("diag", [P, IB], F16, ctx)
        prepare(nc, sb, sem, {**g, **locals()})
        attend(nc, sb, sem, {**g, **locals()})


def prepare(nc, sb, sem, g):
    C, xs, banks, x = g["C"], g["xs"], g["banks"], g["x"]
    stats, mv, rstd, cst, consts = g["stats"], g["mv"], g["rstd"], g["cst"], g["consts"]
    q_dram, k_dram, a_dram = g["q_dram"], g["k_dram"], g["a_dram"]
    kst, V, beta, alpha, gtop, ast, diag = (g[n] for n in ("kst", "V", "beta", "alpha", "gtop", "ast", "diag"))
    with ExitStack() as ctx:
        xn = sb("xn", [P, T, D], F32, ctx)
        xT = sb("xT", [P, S], F32, ctx)
        proj = sb("proj", [P, 2, S], F32, ctx)
        rest = sb("rest", [P, S], F32, ctx)
        parts = sb("parts", [P, 2, 3, S], BF16, ctx)
        ones = sb("ones", [P, P], F32, ctx)
        dJ = sb("dJ", [P, 2], F32, ctx)
        dJb = sb("dJb", [P, 2, P], F32, ctx)
        wnat = sb("wnat", [P, 2 + H], F32, ctx)
        drb = sb("drb", [P, 2], F32, ctx)
        dL = sb("dL", [P, 3, H], F32, ctx)
        gate = sb("gate", [P, T, H], F32, ctx)
        gated = sb("gated", [P, T, 2, H], F32, ctx)
        gparts = sb("gparts", [P, T, 4, H], F16, ctx)

        names = ["load", "loadx", "kone", "chain", "dv", "rs", "xn_ready", "xt_ps", "xt_ready", "w_ready",
                 "mm_q", "mm_k", "mm_v", "mm_b", "mm_n", "q_parts", "k_parts", "a_parts", "gsum", "gexp",
                 "v_copied", "b_copied", "q_out", "k_out", "a_out", "k_in", "a_in"]
        s = {n: sem("p_" + n, ctx) for n in names}
        with nc.Block() as block:

            @block.sync
            def _(sp):
                sp.dma_start(xs[:, :, :], x.rearrange("(t p) d -> p t d", p=P)).then_inc(s["loadx"], 16)
                sp.dma_start(cst[:, :], consts).then_inc(s["load"], 16)
                sp.wait_ge(s["k_parts"], 3)
                sp.dma_start(k_dram.rearrange("a p s -> p a s"), parts[:, 1, :, :]).then_inc(s["k_out"], 16)
                sp.wait_ge(s["k_out"], 16)
                sp.wait_ge(s["kone"], 1)
                for z in range(2):
                    for n in range(SLOTS):
                        src = k_dram[KPART[n], :, :].rearrange("(a z d) s -> z d a s", z=2, d=HD)[z]
                        r = (z * SLOTS + n) * HD
                        sp.dma_start(kst[r:r + HD, :, :], src).then_inc(s["k_in"], 16)
                sp.wait_ge(s["q_parts"], 3)
                sp.dma_start(q_dram.rearrange("a p s -> p a s"), parts[:, 0, :, :]).then_inc(s["q_out"], 16)
                sp.wait_ge(s["a_parts"], 2)
                sp.dma_start(a_dram.rearrange("(t p) a h -> p t (a h)", p=P),
                             gparts[:, :, :, :].rearrange("p t a h -> p t (a h)")).then_inc(s["a_out"], 16)
                sp.wait_ge(s["a_out"], 16)
                for n in range(8):
                    part = (n % 4) // 2 + 2 * (n // 4)
                    src = a_dram[:, part, :].rearrange("(b i) h -> i b h", i=IB)
                    sp.dma_start(ast[n * IB:(n + 1) * IB, :, :], src).then_inc(s["a_in"], 16)
                sp.wait_ge(s["k_in"], 16 * 2 * SLOTS)
                sp.wait_ge(s["a_in"], 16 * 8)
                sp.wait_ge(s["q_out"], 16)

            @block.gpsimd
            def _(pool):
                nc.gpsimd.memset(kst[:, :, :], 1.0).then_inc(s["kone"], 1)
                nc.gpsimd.memset(V[:, :, :, HD:VW], 1.0).then_inc(s["v_copied"], 1)
                pool.wait_ge(s["dv"], 2 * T)
                rstd_first(nc, pool, s["rs"], LN_EPS, g)
                rstd_step(nc, pool, s["rs"], g)

            @block.vector
            def _(dve):
                dve.wait_ge(s["load"], 16)
                L = C("bias").rearrange("p (r h) -> p r h", h=H)
                nc.vector.tensor_tensor(dL[:, 2, :], L[:, 0, :], L[:, 1, :], ALU.max).then_inc(s["w_ready"], 1)
                dve.wait_ge(s["w_ready"], 1)
                nc.vector.tensor_tensor(dL[:, 2, :], dL[:, 2, :], L[:, 2, :], ALU.max).then_inc(s["w_ready"], 1)
                dve.wait_ge(s["w_ready"], 2)
                nc.vector.tensor_tensor(dL[:, 2, :], dL[:, 2, :], L[:, 2, :], ALU.subtract).then_inc(s["w_ready"], 1)
                for r in range(2):
                    nc.vector.tensor_tensor(dL[:, r, :], L[:, r, :], L[:, 2, :], ALU.subtract).then_inc(s["w_ready"], 1)
                nc.vector.tensor_tensor(drb[:, :], C("relb")[:, 0:2], C("relb")[:, 2:3].to_broadcast([P, 2]),
                                        ALU.subtract).then_inc(s["w_ready"], 1)
                nc.vector.tensor_tensor(wnat[:, 0:2], C("relI")[:, 0:2], C("relI")[:, 2:3].to_broadcast([P, 2]),
                                        ALU.subtract).then_inc(s["w_ready"], 1)
                nc.vector.tensor_copy(wnat[:, 2:2 + H], C("gateT")).then_inc(s["w_ready"], 1)
                nc.vector.tensor_copy(diag[:, :], C("diag")).then_inc(s["w_ready"], 1)
                nc.vector.memset(ones[:, :], 1.0).then_inc(s["w_ready"], 1)
                nc.vector.tensor_tensor(dJ[:, :], C("relJ")[:, 0:2], C("relJ")[:, 2:3].to_broadcast([P, 2]),
                                        ALU.subtract).then_inc(s["w_ready"], 1)
                dve.wait_ge(s["w_ready"], 11)
                for r in range(2):
                    nc.vector.tensor_scalar(dJb[:, r, :], ones[:, :], dJ[:, r:r + 1], None,
                                            ALU.mult).then_inc(s["w_ready"], 1)
                dve.wait_ge(s["loadx"], 16)
                for t in range(T):
                    nc.vector.bn_stats(stats[:, t, :], xs[:, t, :]).then_inc(s["dv"], 1)
                for t in range(T):
                    dve.wait_ge(s["dv"], t + 1)
                    nc.vector.bn_aggr(mv[:, t, :], stats[:, t, :]).then_inc(s["dv"], 1)
                dve.wait_ge(s["dv"], 2 * T)
                rstd_reciprocal(nc, dve, s["rs"], g)
                dve.wait_ge(s["rs"], RSTD)
                for t in range(T):
                    nc.vector.tensor_scalar(xn[:, t, :], xs[:, t, :], mv[:, t, 0:1], rstd[:, t:t + 1],
                                            ALU.subtract, ALU.mult).then_inc(s["xn_ready"], 1)
                dve.wait_ge(s["xn_ready"], T)
                dve.wait_ge(s["load"], 16)
                nc.vector.tensor_tensor(xs[:, :, :], xs[:, :, :],
                                        C("bo").rearrange("p (a d) -> p a d", a=1).to_broadcast([P, T, D]),
                                        ALU.add).then_inc(s["chain"], 1)

                def split(which, bias, scale, mm, done):
                    p32 = proj[:, which, :]
                    dve.wait_ge(s[mm], FC)
                    for c in range(FC):
                        nc.vector.tensor_scalar(proj[:, which, c * NS:(c + 1) * NS], banks[4 * which + c], bias,
                                                scale, ALU.add, ALU.mult).then_inc(s["chain"], 1)
                    dve.wait_ge(s["chain"], 1 + FC + which * (FC + 1))
                    nc.vector.tensor_copy(parts[:, which, 0, :], p32).then_inc(s[done], 1)
                    dve.wait_ge(s[done], 1)
                    nc.vector.tensor_tensor(rest[:, :], p32, parts[:, which, 0, :], ALU.subtract).then_inc(s["chain"], 1)
                    dve.wait_ge(s["chain"], 2 + FC + which * (FC + 1))
                    nc.vector.tensor_copy(parts[:, which, 1, :], rest[:, :]).then_inc(s[done], 1)
                    dve.wait_ge(s[done], 2)
                    nc.vector.tensor_tensor(parts[:, which, 2, :], rest[:, :], parts[:, which, 1, :],
                                            ALU.subtract).then_inc(s[done], 1)
                    dve.wait_ge(s[done], 3)

                split(0, C("bq"), float(HD) ** -0.5, "mm_q", "q_parts")
                split(1, C("bk"), 1.0, "mm_k", "k_parts")
                dve.wait_ge(s["mm_n"], 1)
                dve.wait_ge(s["w_ready"], 13)
                nat = banks[0][:, 0:T * (2 + H)].rearrange("p (t n) -> p t n", t=T)
                nc.vector.tensor_tensor(alpha[:, :, :], nat[:, :, 0:2],
                                        drb[:, :].rearrange("p (a n) -> p a n", a=1).to_broadcast([P, T, 2]),
                                        ALU.add).then_inc(s["gsum"], 1)
                nc.vector.tensor_tensor(gate[:, :, :], nat[:, :, 2:2 + H],
                                        C("gateb").rearrange("p (a n) -> p a n", a=1).to_broadcast([P, T, H]),
                                        ALU.add).then_inc(s["gsum"], 1)
                dve.wait_ge(s["gexp"], 1)
                nc.vector.tensor_scalar(gate[:, :, :], gate[:, :, :], 1.0, None, ALU.add).then_inc(s["gsum"], 1)
                dve.wait_ge(s["gsum"], 3)
                nc.vector.reciprocal(gate[:, :, :], gate[:, :, :]).then_inc(s["gsum"], 1)
                dve.wait_ge(s["gsum"], 4)
                for r in range(3):
                    dst = gated[:, :, r, :] if r < 2 else gtop[:, :, :]
                    nc.vector.tensor_tensor(dst, gate[:, :, :], dL[:, r:r + 1, :].to_broadcast([P, T, H]),
                                            ALU.mult).then_inc(s["gsum"], 1)
                dve.wait_ge(s["gsum"], 7)
                nc.vector.tensor_copy(gparts[:, :, 0:2, :], gated[:, :, :, :]).then_inc(s["a_parts"], 1)
                dve.wait_ge(s["a_parts"], 1)
                nc.vector.tensor_tensor(gparts[:, :, 2:4, :], gated[:, :, :, :], gparts[:, :, 0:2, :],
                                        ALU.subtract).then_inc(s["a_parts"], 1)
                for c in range(4):
                    dve.wait_ge(s["mm_v"], c + 1)
                    src = banks[4 + c].rearrange("p (t h d) -> p t h d", t=4, d=HD)
                    for t in range(4):
                        nc.vector.tensor_tensor(V[:, 4 * c + t, :, 0:HD], src[:, t],
                                                C("bv").rearrange("p (h d) -> p h d", d=HD),
                                                ALU.add).then_inc(s["v_copied"], 1)

            @block.scalar
            def _(act):
                rstd_root(nc, act, s["rs"], g)
                for c in range(FC):
                    act.wait_ge(s["xt_ps"], c + 1)
                    nc.scalar.copy(xT[:, c * NS:(c + 1) * NS], banks[c]).then_inc(s["xt_ready"], 1)
                act.wait_ge(s["gsum"], 2)
                nc.scalar.activation(gate[:, :, :], gate[:, :, :], ACT.Exp, scale=-1.0).then_inc(s["gexp"], 1)
                for r in range(2):
                    for c in range(FC):
                        n = r * FC + c
                        act.wait_ge(s["mm_b"], n + 1)
                        nc.scalar.copy(beta[:, r, c * NS:(c + 1) * NS], banks[1 + n % 3]).then_inc(s["b_copied"], 1)

            @block.tensor
            def _(pe):
                pe.wait_ge(s["load"], 16)
                for t in range(T):
                    pe.wait_ge(s["xn_ready"], t + 1)
                    ins = nc.tensor.transpose(banks[t // 4][:, (t % 4) * P:(t % 4 + 1) * P], xn[:, t, :], C("ident"))
                    if t % 4 == 3:
                        ins.then_inc(s["xt_ps"], 1)
                pe.wait_ge(s["xt_ready"], FC)
                for w, mm, first in (("wqT", "mm_q", 0), ("wkT", "mm_k", 4)):
                    for c in range(FC):
                        nc.tensor.matmul(banks[first + c], C(w), xT[:, c * NS:(c + 1) * NS],
                                         start=True, stop=True).then_inc(s[mm], 1)
                pe.wait_ge(s["w_ready"], 13)
                pe.wait_ge(s["chain"], 1 + FC)
                for t in range(T):
                    ins = nc.tensor.matmul(banks[0][:, t * (2 + H):(t + 1) * (2 + H)], xT[:, t * P:(t + 1) * P],
                                           wnat[:, :], start=True, stop=True)
                ins.then_inc(s["mm_n"], 1)
                pe.wait_ge(s["chain"], 1 + FC + FC + 1)
                for t in range(T):
                    ins = nc.tensor.matmul(banks[4 + t // 4][:, (t % 4) * P:(t % 4 + 1) * P],
                                           xT[:, t * P:(t + 1) * P], C("wvT"), start=True, stop=True)
                    if t % 4 == 3:
                        ins.then_inc(s["mm_v"], 1)
                for r in range(2):
                    for c in range(FC):
                        n = r * FC + c
                        if n >= 3:
                            pe.wait_ge(s["b_copied"], n - 2)
                        nc.tensor.matmul(banks[1 + n % 3], dJb[:, r, :], xT[:, c * NS:(c + 1) * NS],
                                         start=True, stop=True).then_inc(s["mm_b"], 1)


def attend(nc, sb, sem, g):
    C, xs = g["C"], g["xs"]
    psS, psO, psM, psX = g["psS"], g["psO"], g["psM"], g["psX"]
    q_dram = g["q_dram"]
    kst, V, beta, alpha, gtop, ast, diag = (g[n] for n in ("kst", "V", "beta", "alpha", "gtop", "ast", "diag"))
    with ExitStack() as ctx:
        qnext = sb("qnext", [SROWS, PAIRS, 2, P], BF16, ctx)
        qcur = sb("qcur", [SROWS, PAIRS, 2, P], BF16, ctx)
        anext = sb("anext", [P, BLOCKS * H, IB], F16, ctx)
        acur = sb("acur", [P, BLOCKS * H, IB], F16, ctx)
        pst = sb("pst", [P, CHUNKS, BLOCKS, CW], F16, ctx)
        pp = sb("pp", [P, CHUNKS, 4, CW], F16, ctx)
        top = sb("top", [P, CW], F32, ctx)
        low = sb("low", [P, CW], F32, ctx)
        l0 = sb("l0", [P, CW], F32, ctx)
        l1 = sb("l1", [P, CW], F32, ctx)
        tot = sb("tot", [P, CW], F32, ctx)
        ET = sb("ET", [P, 2, H, P], F32, ctx)
        mx = sb("mx", [P, H, S // NS], F32, ctx)
        mrow = sb("mrow", [P, H], F32, ctx)
        sh = sb("sh", [P, P], F32, ctx)
        shh = sb("shh", [P, 2, H], BF16, ctx)
        shT = sb("shT", [2 * 3 * PAIRS, P], BF16, ctx)
        osb = sb("osb", [P, NS], F32, ctx)
        den = sb("den", [P, H], F32, ctx)
        att = sb("att", [P, H, HD], F32, ctx)
        attT = sb("attT", [P, P], F32, ctx)

        names = ["zero_q", "zero_sh", "zero_o", "q_in", "sh_in", "st_in0", "st_in1", "scores", "exps", "av", "cur", "anext", "mxs",
                 "mxused", "lg", "ex", "sm", "rc", "pr", "hi0", "hi1", "pd0", "pd1", "sh", "shps", "shT",
                 "o_sb", "o_ps", "den", "att", "aT_ps", "aT", "y_ps", "y"]
        s = {n: sem("a_" + n, ctx) for n in names}

        shv = sh[:, 0:2 * 3 * PAIRS].rearrange("p (z a n) -> p z a n", z=2, a=3)

        def by_pair(ap):
            return ap.rearrange("p (n z) -> p z n", z=2)

        def wait(eng, name, per, tile, more):
            if isinstance(tile, int) and per * tile + more <= 0:
                return
            eng.wait_ge(s[name], tile * per + more)

        with nc.Block() as block:

            @block.sync
            def _(sp):
                def load_q(t):
                    wait(sp, "cur", 2, t, 0)
                    for z in range(2):
                        for n in range(SLOTS):
                            r = (z * SLOTS + n) * HD
                            src = q_dram[QPART[n], :, :].rearrange("(a z d) s -> z d a s", z=2, d=HD)[z]
                            sp.dma_start(qnext[r:r + HD, :, z, :], src[:, :, bass.ds(t * P, P)]).then_inc(s["q_in"], 16)

                def load_shift(t):
                    wait(sp, "shT", 1, t, 1)
                    for z in range(2):
                        sp.dma_start(qnext[ROWS + 3 * z:ROWS + 3 * z + 3, :, z, :],
                                     shT[z * 3 * PAIRS:(z + 1) * 3 * PAIRS, :]).then_inc(s["sh_in"], 16)

                def load_stack(t, c):
                    wait(sp, f"pd{c}", 2, t, 2)
                    wait(sp, "scores", 2 * T, t, -2 * T + 2 * JC * (c + 1))
                    for n in range(8):
                        for b in range(BLOCKS):
                            sp.dma_start(pst[n * IB:(n + 1) * IB, c, b, :],
                                         pp[b * IB:(b + 1) * IB, c, n % 4, :]).then_inc(s[f"st_in{c}"], 16)

                sp.wait_ge(s["zero_q"], 1)
                load_q(0)
                load_stack(0, 0)
                load_shift(0)
                load_stack(0, 1)

                def ahead(t):
                    load_q(t + 1)
                    load_stack(t + 1, 0)
                    load_shift(t + 1)
                    load_stack(t + 1, 1)

                with sp.Fori(0, T - 1) as t:
                    ahead(t)

            @block.gpsimd
            def _(pool):
                nc.gpsimd.memset(qnext[:, :, :, :], 0.0).then_inc(s["zero_q"], 1)
                nc.gpsimd.memset(sh[:, :], 0.0).then_inc(s["zero_sh"], 1)

                def chunk(t, c):
                    wait(pool, "ex", 6, t, 3 * c + 3)
                    wait(pool, "rc", 2, t, c)
                    nc.gpsimd.tensor_tensor(tot[:, :], l0[:, :], l1[:, :], ALU.add).then_inc(s["sm"], 1)
                    wait(pool, "sm", 4, t, 2 * c + 1)
                    nc.gpsimd.tensor_tensor(tot[:, :], tot[:, :], low[:, :], ALU.add).then_inc(s["sm"], 1)
                    for r, l in ((0, l0), (1, l1)):
                        wait(pool, f"hi{c}", 2, t, r + 1)
                        nc.gpsimd.tensor_tensor(pp[:, c, 2 * r + 1, :], l[:, :], pp[:, c, 2 * r, :],
                                                ALU.subtract).then_inc(s[f"pd{c}"], 1)

                def diagonal(t):
                    wait(pool, "cur", 2, t, 0)
                    nc.gpsimd.tensor_tensor(
                        anext[:, :, :],
                        ast[:, bass.ds(t * BLOCKS, BLOCKS), :].rearrange("p b (h a) -> p (b h) a", a=1)
                        .to_broadcast([P, BLOCKS * H, IB]),
                        diag[:, :].rearrange("p (a i) -> p a i", a=1).to_broadcast([P, BLOCKS * H, IB]),
                        ALU.mult).then_inc(s["anext"], 1)

                def ahead(t):
                    chunk(t, 0)
                    diagonal(t)
                    chunk(t, 1)

                ahead(0)
                with pool.Fori(0, T - 1) as t:
                    ahead(t + 1)

            @block.scalar
            def _(act):
                def exps(t, j):
                    for u in range(2):
                        wait(act, "scores", 2 * T, t, 2 * j + u + 1)
                        if u == 0:
                            wait(act, "av", T, t, j - 1)
                        nc.scalar.activation(
                            ET[:, j % 2, 8 * u:8 * u + 8, :].rearrange("p h (v i) -> p v h i", v=2),
                            psS[:, u, :].rearrange("p (v h i) -> p v h i", v=2, h=8),
                            ACT.Exp).then_inc(s["exps"], 1)

                def rel_exps(t, c):
                    for n, (dst, src, sc) in enumerate(((l0, l0, 1.0), (l1, l1, 1.0), (low, top, -1.0))):
                        wait(act, "lg", 8, t, 4 * c + (3 if n == 0 else 4))
                        if n == 2:
                            wait(act, "sm", 4, t, 2 * c)
                        nc.scalar.activation(dst[:, :], src[:, :], ACT.Exp, scale=sc).then_inc(s["ex"], 1)

                def high(t, c):
                    for r, l in ((0, l0), (1, l1)):
                        wait(act, "pr", 4, t, 2 * c + r + 1)
                        wait(act, f"st_in{c}", 16 * 8 * BLOCKS, t, 0)
                        nc.scalar.copy(pp[:, c, 2 * r, :], l[:, :]).then_inc(s[f"hi{c}"], 1)

                def tile(t, first, last):
                    for j in range(T):
                        exps(t, j)
                        if not last and j % JC == 2:
                            rel_exps(t + 1, j // JC)
                        if not last and j % JC == 5:
                            high(t + 1, j // JC)
                        if not first and j == 4:
                            wait(act, "aT_ps", 1, t, 0)
                            nc.scalar.copy(attT[:, :], psX[:, 0:P]).then_inc(s["aT"], 1)
                    wait(act, "av", T, t, T)
                    if not first:
                        wait(act, "o_ps", 1, t, 0)
                    nc.scalar.copy(osb[:, :], psO[:, :]).then_inc(s["o_sb"], 1)

                for c in range(CHUNKS):
                    rel_exps(0, c)
                    high(0, c)
                tile(0, True, False)
                with act.Fori(1, T - 1) as t:
                    tile(t, False, False)
                tile(T - 1, False, True)
                act.wait_ge(s["aT_ps"], T)
                nc.scalar.copy(attT[:, :], psX[:, 0:P]).then_inc(s["aT"], 1)

            @block.vector
            def _(dve):
                nc.vector.memset(psO[:, :], 0.0).then_inc(s["zero_o"], 1)

                def a(t, r):
                    return alpha[:, bass.ds(t, 1), r]

                def logits(t, c, part):
                    b0, b1 = (beta[:, r, c * CW:(c + 1) * CW] for r in range(2))
                    if part == 0:
                        wait(dve, "pr", 4, t, 2 * c)
                        nc.vector.tensor_scalar(top[:, :], b1, a(t, 1), 0.0, ALU.add, ALU.max).then_inc(s["lg"], 1)
                        wait(dve, "lg", 8, t, 4 * c + 1)
                        nc.vector.scalar_tensor_tensor(top[:, :], b0, a(t, 0), top[:, :], ALU.add,
                                                       ALU.max).then_inc(s["lg"], 1)
                    else:
                        wait(dve, "lg", 8, t, 4 * c + 2)
                        for r, (b, l) in enumerate(((b0, l0), (b1, l1))):
                            if c == 1:
                                wait(dve, "pd0", 2, t, r + 1)
                            else:
                                wait(dve, "pd1", 2, t, r - 1)
                            nc.vector.scalar_tensor_tensor(l[:, :], b, a(t, r), top[:, :], ALU.add,
                                                           ALU.subtract).then_inc(s["lg"], 1)

                def recip(t, c):
                    wait(dve, "sm", 4, t, 2 * c + 2)
                    nc.vector.reciprocal(top[:, :], tot[:, :]).then_inc(s["rc"], 1)

                def products(t, c):
                    wait(dve, "rc", 2, t, c + 1)
                    for l in (l0, l1):
                        nc.vector.tensor_tensor(l[:, :], l[:, :], top[:, :], ALU.mult).then_inc(s["pr"], 1)

                def maxima(t, lo, hi):
                    for m in range(lo, hi):
                        wait(dve, "mxs", MAXS, t, m + 1)
                        h, c = divmod(m, S // NS)
                        nc.vector.reduce_max(mx[:, h, c:c + 1], psM[:, m % 2, :], AX_X).then_inc(s["mxused"], 1)

                def shift(t):
                    wait(dve, "mxused", MAXS, t, MAXS)
                    wait(dve, "shps", 1, t, 0)
                    nc.vector.reduce_max(mrow[:, :], mx[:, :, :], AX_X).then_inc(s["sh"], 1)
                    wait(dve, "sh", 6, t, 1)
                    nc.vector.scalar_tensor_tensor(
                        shv[:, :, 0, :], by_pair(mrow[:, :]), -1.0,
                        gtop[:, bass.ds(t, 1), :].rearrange("p a (n z) -> p z (a n)", z=2),
                        ALU.mult, ALU.subtract).then_inc(s["sh"], 1)
                    wait(dve, "sh", 6, t, 2)
                    hv = [shh[:, n, :].rearrange("p (z n) -> p z n", z=2) for n in range(2)]
                    for n in range(2):
                        nc.vector.tensor_copy(hv[n], shv[:, :, n, :]).then_inc(s["sh"], 1)
                        wait(dve, "sh", 6, t, 3 + 2 * n)
                        nc.vector.tensor_tensor(shv[:, :, n + 1, :], shv[:, :, n, :], hv[n],
                                                ALU.subtract).then_inc(s["sh"], 1)
                        if n == 0:
                            wait(dve, "sh", 6, t, 4)

                def shift_rows(t):
                    wait(dve, "shps", 1, t, 1)
                    wait(dve, "sh_in", 32, t, 0)
                    nc.vector.tensor_copy(shT[:, :], psX[0:2 * 3 * PAIRS, 0:P]).then_inc(s["shT"], 1)

                def to_current(t):
                    wait(dve, "scores", 2 * T, t, 0)
                    wait(dve, "q_in", 16 * 2 * SLOTS, t, 16 * 2 * SLOTS)
                    wait(dve, "sh_in", 32, t, 32)
                    nc.vector.tensor_copy(qcur[:, :, :, :], qnext[:, :, :, :]).then_inc(s["cur"], 1)
                    wait(dve, "anext", 1, t, 1)
                    nc.vector.tensor_copy(acur[:, :, :], anext[:, :, :]).then_inc(s["cur"], 1)

                def normalize(t):
                    v = psX[:, :].rearrange("p (h w) -> p h w", w=32)
                    wait(dve, "o_ps", 1, t, 1)
                    wait(dve, "aT_ps", 1, t, 0)
                    nc.vector.reciprocal(den[:, :], v[:, :, HD]).then_inc(s["den"], 1)
                    wait(dve, "den", 1, t, 1)
                    nc.vector.tensor_tensor(att[:, :, :], v[:, :, 0:HD],
                                            den[:, :].rearrange("p (h a) -> p h a", a=1).to_broadcast([P, H, HD]),
                                            ALU.mult).then_inc(s["att"], 1)

                def residual(t):
                    wait(dve, "y_ps", 1, t, 1)
                    nc.vector.tensor_tensor(xs[:, bass.ds(t, 1), :], xs[:, bass.ds(t, 1), :],
                                            psX[:, P:2 * P].rearrange("p (a d) -> p a d", a=1),
                                            ALU.add).then_inc(s["y"], 1)

                def tile(t, first, last):
                    for j in range(T):
                        if not last:
                            if 2 <= j <= 12:
                                maxima(t + 1, 6 * (j - 2), min(6 * (j - 1), MAXS))
                            if j % JC in (0, 1):
                                logits(t + 1, j // JC, j % JC)
                            if j % JC == 4:
                                recip(t + 1, j // JC)
                                products(t + 1, j // JC)
                            if j == 13:
                                shift(t + 1)
                            if j == 14:
                                shift_rows(t + 1)
                        if not first:
                            if j == 3:
                                normalize(t - 1)
                            if j == 7:
                                residual(t - 1)
                    if not last:
                        to_current(t + 1)

                for c in range(CHUNKS):
                    logits(0, c, 0)
                    logits(0, c, 1)
                    recip(0, c)
                    products(0, c)
                maxima(0, 0, MAXS)
                dve.wait_ge(s["zero_sh"], 1)
                shift(0)
                shift_rows(0)
                to_current(0)
                tile(0, True, False)
                with dve.Fori(1, T - 1) as t:
                    tile(t, False, False)
                tile(T - 1, False, True)
                normalize(T - 1)
                residual(T - 1)

            @block.tensor
            def _(pe):
                def scores(t, j):
                    c, jj = divmod(j, JC)
                    for u in range(2):
                        wait(pe, "exps", 2 * T, t, 2 * j + u - 1)
                        for v in range(2):
                            out = psS[:, u, v * NS:(v + 1) * NS]
                            for n in range(4):
                                a = 4 * u + n
                                nc.tensor.matmul(out[:, n * P:(n + 1) * P], kst[:, a, j * P:(j + 1) * P],
                                                 qcur[:, a, :, v * 64:(v + 1) * 64], start=n == 0, stop=False,
                                                 skip_group_check=True)
                            for n in range(4):
                                b = 4 * v + n
                                ins = nc.tensor.matmul(
                                    out.rearrange("p (h i) -> p h i", h=8)[:, :, n * IB:(n + 1) * IB],
                                    pst[:, c, b, jj * P:(jj + 1) * P],
                                    acur[:, b * H + 8 * u:b * H + 8 * u + 8, :], start=False, stop=n == 3,
                                    skip_group_check=True)
                        ins.then_inc(s["scores"], 1)

                def times_v(t, j):
                    wait(pe, "exps", 2 * T, t, 2 * j + 2)
                    if j == 0:
                        wait(pe, "o_sb", 1, t, 0)
                    for h in range(H):
                        gr, r = divmod(h, 4)
                        ins = nc.tensor.matmul(psO[32 * r:32 * r + VW, gr * P:(gr + 1) * P], V[:, j, h, :],
                                               ET[:, j % 2, h, :], start=j == 0 and gr == 0, stop=j == T - 1,
                                               skip_group_check=True)
                    ins.then_inc(s["av"], 1)

                def maxima(t, lo, hi):
                    for m in range(lo, hi):
                        h, c = divmod(m, S // NS)
                        wait(pe, "mxused", MAXS, t, m - 1)
                        nc.tensor.matmul(psM[:, m % 2, :], qnext[0:ROWS, h // 2, h % 2, :],
                                         kst[0:ROWS, h // 2, c * NS:(c + 1) * NS], start=True,
                                         stop=True).then_inc(s["mxs"], 1)

                def shift(t):
                    wait(pe, "sh", 6, t, 6)
                    wait(pe, "y", 1, t, -1)
                    nc.tensor.transpose(psX[:, 0:P], sh[:, :], C("ident")).then_inc(s["shps"], 1)

                def outputs(t):
                    wait(pe, "o_sb", 1, t, 1)
                    wait(pe, "shT", 1, t, 2)
                    for gr in range(4):
                        ins = nc.tensor.transpose(psX[:, gr * P:(gr + 1) * P], osb[:, gr * P:(gr + 1) * P], C("ident"))
                    ins.then_inc(s["o_ps"], 1)

                def out_transpose(t):
                    wait(pe, "att", 1, t, 1)
                    nc.tensor.transpose(psX[:, 0:P], att[:, :, :].rearrange("p h d -> p (h d)"),
                                        C("ident")).then_inc(s["aT_ps"], 1)

                def out_project(t):
                    wait(pe, "aT", 1, t, 1)
                    nc.tensor.matmul(psX[:, P:2 * P], attT[:, :], C("woT"), start=True, stop=True).then_inc(s["y_ps"], 1)

                def tile(t, first, last):
                    wait(pe, "cur", 2, t, 2)
                    for j in range(T):
                        if j % JC == 0:
                            wait(pe, f"st_in{j // JC}", 16 * 8 * BLOCKS, t, 16 * 8 * BLOCKS)
                        scores(t, j)
                        if j > 0:
                            times_v(t, j - 1)
                        if not last:
                            if j == 2:
                                wait(pe, "q_in", 16 * 2 * SLOTS, t, 2 * 16 * 2 * SLOTS)
                            if 2 <= j <= 12:
                                maxima(t + 1, 6 * (j - 2), min(6 * (j - 1), MAXS))
                            if j == 14:
                                shift(t + 1)
                        if not first:
                            if j == 2:
                                outputs(t - 1)
                            if j == 4:
                                out_transpose(t - 1)
                            if j == 6:
                                out_project(t - 1)
                    times_v(t, T - 1)

                pe.wait_ge(s["zero_o"], 1)
                pe.wait_ge(s["q_in"], 16 * 2 * SLOTS)
                maxima(0, 0, MAXS)
                shift(0)
                tile(0, True, False)
                with pe.Fori(1, T - 1) as t:
                    tile(t, False, False)
                tile(T - 1, False, True)
                pe.wait_ge(s["o_sb"], T)
                pe.wait_ge(s["y"], T - 1)
                for gr in range(4):
                    ins = nc.tensor.transpose(psX[:, gr * P:(gr + 1) * P], osb[:, gr * P:(gr + 1) * P], C("ident"))
                ins.then_inc(s["o_ps"], 1)
                out_transpose(T - 1)
                out_project(T - 1)


def experts(nc, sb, sem, g):
    C, xs, banks = g["C"], g["xs"], g["banks"]
    stats, mv, rstd, cst = g["stats"], g["mv"], g["rstd"], g["cst"]
    w1, w2, out = g["w1"], g["w2"], g["out"]
    with ExitStack() as ctx:
        xn = sb("xn2", [P, T, D], F32, ctx)
        xT = sb("xT2", [P, S], F32, ctx)
        hr = sb("hr", [P, T, R1], F32, ctx)
        hg = sb("hg", [P, T, R1], F32, ctx)
        hT = sb("hT", [P, T // 2, P], F32, ctx)
        wr2 = sb("wr2", [P, E], F32, ctx)
        lgt = sb("lgt", [P, T, E], F32, ctx)
        row = sb("row", [P, T], F32, ctx)
        pairs = sb("pairs", [P, T, E, E], F32, ctx)
        same = sb("same", [P, T, E, E], F32, ctx)
        wts = sb("wts", [P, T, E], F32, ctx)
        wtT = sb("wtT", [P, P], F32, ctx)
        b2own = sb("b2own", [P, T, D], F32, ctx)
        w1s = sb("w1s", [P, 2, 2 * F], F32, ctx)
        w2s = sb("w2s", [P, 2, FT, D], F32, ctx)
        G = sb("G", [P, 2, NS], F32, ctx)
        hid = sb("hid", [P, 2, FT, NS], F32, ctx)
        b1s = sb("b1s", [P, 2, 2 * FT], F32, ctx)
        b1_dram = g["consts"][:, AT["b1"]]

        names = ["dv", "rs", "xn", "xt_ps", "xt", "h_ps", "h", "hst", "hrs", "hn", "gelu", "hT_ps", "hT",
                 "l_ps", "lg", "ex", "r", "w", "wT_ps", "wT", "own", "b2_ps", "x2",
                 "w_in0", "w_in1", "x2ps", "x1ps", "gl", "hd", "yps", "acc", "out"]
        s = {n: sem("e_" + n, ctx) for n in names}
        UP = FC * FT

        START = {"gl": 3, "hd": 3, "yps": 2, "acc": T}

        def wait(eng, name, per, e, more):
            eng.wait_ge(s[name], e * per + more + START.get(name, 0))

        with nc.Block() as block:

            @block.sync
            def _(sp):
                def load(e, buf):
                    if not isinstance(e, int):
                        wait(sp, "yps", FC, e, -FC)
                    sp.dma_start(w1s[:, buf, :], w1[bass.ds(e, 1), :, :].rearrange("a c f -> c (a f)")).then_inc(s[f"w_in{buf}"], 16)
                    sp.dma_start(w2s[:, buf, :, :],
                                 w2[bass.ds(e, 1), :, :].rearrange("a (n p) d -> p (a n) d", p=P)).then_inc(s[f"w_in{buf}"], 16)
                    sp.dma_start(b1s[:, buf, :], b1_dram[:, bass.ds(e * 2 * FT, 2 * FT)]).then_inc(s[f"w_in{buf}"], 16)

                load(0, 0)
                load(1, 1)
                with sp.Fori(1, E // 2) as p:
                    load(2 * p, 0)
                    load(2 * p + 1, 1)
                wait(sp, "acc", T, E, 0)
                sp.dma_start(out.rearrange("(t p) d -> p t d", p=P), xs[:, :, :]).then_inc(s["out"], 16)
                sp.wait_ge(s["out"], 16)

            @block.gpsimd
            def _(pool):
                nc.gpsimd.tensor_copy(wr2[:, :], C("wr2")).then_inc(s["own"], 1)
                nc.gpsimd.tensor_tensor(b2own[:, :, :], C("b2").rearrange("p (a d) -> p a d", a=1).to_broadcast([P, T, D]),
                                        C("own").rearrange("p (t a) -> p t a", a=1).to_broadcast([P, T, D]),
                                        ALU.mult).then_inc(s["own"], 1)
                pool.wait_ge(s["dv"], 2 * T)
                rstd_first(nc, pool, s["rs"], LN_EPS, g)
                rstd_step(nc, pool, s["rs"], g)
                pool.wait_ge(s["hst"], 2 * T)
                rstd_first(nc, pool, s["hrs"], ROUTER_EPS, g)
                rstd_step(nc, pool, s["hrs"], g)

            @block.vector
            def _(dve):
                for t in range(T):
                    nc.vector.bn_stats(stats[:, t, :], xs[:, t, :]).then_inc(s["dv"], 1)
                for t in range(T):
                    dve.wait_ge(s["dv"], t + 1)
                    nc.vector.bn_aggr(mv[:, t, :], stats[:, t, :]).then_inc(s["dv"], 1)
                dve.wait_ge(s["dv"], 2 * T)
                rstd_reciprocal(nc, dve, s["rs"], g)
                dve.wait_ge(s["rs"], RSTD)
                for t in range(T):
                    nc.vector.tensor_scalar(xn[:, t, :], xs[:, t, :], mv[:, t, 0:1], rstd[:, t:t + 1],
                                            ALU.subtract, ALU.mult).then_inc(s["xn"], 1)
                for c in range(2):
                    dve.wait_ge(s["h_ps"], c + 1)
                    nc.vector.tensor_tensor(hr[:, 8 * c:8 * c + 8, :], banks[4 + c].rearrange("p (t n) -> p t n", n=R1),
                                            C("br1").rearrange("p (a n) -> p a n", a=1).to_broadcast([P, 8, R1]),
                                            ALU.add).then_inc(s["h"], 1)
                dve.wait_ge(s["h"], 2)
                dve.wait_ge(s["xn"], T)
                for t in range(T):
                    nc.vector.bn_stats(stats[:, t, :], hr[:, t, :]).then_inc(s["hst"], 1)
                for t in range(T):
                    dve.wait_ge(s["hst"], t + 1)
                    nc.vector.bn_aggr(mv[:, t, :], stats[:, t, :]).then_inc(s["hst"], 1)
                dve.wait_ge(s["hst"], 2 * T)
                rstd_reciprocal(nc, dve, s["hrs"], g)
                dve.wait_ge(s["hrs"], RSTD)
                for t in range(T):
                    nc.vector.tensor_scalar(hr[:, t, :], hr[:, t, :], mv[:, t, 0:1], rstd[:, t:t + 1],
                                            ALU.subtract, ALU.mult).then_inc(s["hn"], 1)
                dve.wait_ge(s["hn"], T)
                nc.vector.tensor_tensor(hr[:, :, :], hr[:, :, :], C("lns").rearrange("p (a n) -> p a n", a=1).to_broadcast([P, T, R1]),
                                        ALU.mult).then_inc(s["hn"], 1)
                dve.wait_ge(s["hn"], T + 1)
                nc.vector.tensor_tensor(hr[:, :, :], hr[:, :, :], C("lnb").rearrange("p (a n) -> p a n", a=1).to_broadcast([P, T, R1]),
                                        ALU.add).then_inc(s["hn"], 1)
                dve.wait_ge(s["l_ps"], 2)
                for z in range(2):
                    nc.vector.tensor_tensor(lgt[:, z:T:2, :], banks[6 + z][:, 0:T // 2 * E].rearrange("p (t e) -> p t e", e=E),
                                            C("br2").rearrange("p (a e) -> p a e", a=1).to_broadcast([P, T // 2, E]),
                                            ALU.add).then_inc(s["lg"], 1)
                dve.wait_ge(s["lg"], 2)
                nc.vector.reduce_max(row[:, :], lgt[:, :, :], AX_X).then_inc(s["r"], 1)
                dve.wait_ge(s["r"], 1)
                nc.vector.tensor_tensor(lgt[:, :, :], lgt[:, :, :], row[:, :].rearrange("p (t a) -> p t a", a=1).to_broadcast([P, T, E]),
                                        ALU.subtract).then_inc(s["r"], 1)
                dve.wait_ge(s["ex"], 1)
                nc.vector.reduce_sum(row[:, :], lgt[:, :, :], AX_X).then_inc(s["r"], 1)
                dve.wait_ge(s["r"], 3)
                nc.vector.reciprocal(row[:, :], row[:, :]).then_inc(s["r"], 1)
                dve.wait_ge(s["r"], 4)
                nc.vector.tensor_tensor(lgt[:, :, :], lgt[:, :, :], row[:, :].rearrange("p (t a) -> p t a", a=1).to_broadcast([P, T, E]),
                                        ALU.mult).then_inc(s["r"], 1)
                dve.wait_ge(s["r"], 5)
                for t in range(T):
                    mine = lgt[:, t, :].rearrange("p (e a) -> p e a", a=1).to_broadcast([P, E, E])
                    other = lgt[:, t, :].rearrange("p (a e) -> p a e", a=1).to_broadcast([P, E, E])
                    nc.vector.tensor_tensor(pairs[:, t, :, :], other, mine, ALU.is_gt).then_inc(s["r"], 1)
                    nc.vector.tensor_tensor(same[:, t, :, :], other, mine, ALU.is_equal).then_inc(s["r"], 1)
                dve.wait_ge(s["r"], 5 + 2 * T)
                flat = lambda a: a[:, :, :, :].rearrange("p t e f -> p t (e f)")
                nc.vector.tensor_tensor(flat(same), flat(same), C("before").rearrange("p (a n) -> p a n", a=1).to_broadcast([P, T, E * E]),
                                        ALU.mult).then_inc(s["r"], 1)
                dve.wait_ge(s["r"], 6 + 2 * T)
                nc.vector.tensor_tensor(flat(pairs), flat(pairs), flat(same), ALU.add).then_inc(s["r"], 1)
                dve.wait_ge(s["r"], 7 + 2 * T)
                nc.vector.reduce_sum(wts[:, :, :], pairs[:, :, :, :], AX_X).then_inc(s["r"], 1)
                dve.wait_ge(s["r"], 8 + 2 * T)
                nc.vector.tensor_scalar(wts[:, :, :], wts[:, :, :], 1.5, None, ALU.is_lt).then_inc(s["r"], 1)
                dve.wait_ge(s["r"], 9 + 2 * T)
                nc.vector.tensor_tensor(wts[:, :, :], wts[:, :, :], lgt[:, :, :], ALU.mult).then_inc(s["r"], 1)
                dve.wait_ge(s["r"], 10 + 2 * T)
                nc.vector.reduce_sum(row[:, :], wts[:, :, :], AX_X).then_inc(s["r"], 1)
                dve.wait_ge(s["r"], 11 + 2 * T)
                nc.vector.reciprocal(row[:, :], row[:, :]).then_inc(s["r"], 1)
                dve.wait_ge(s["r"], 12 + 2 * T)
                nc.vector.tensor_tensor(wts[:, :, :], wts[:, :, :], row[:, :].rearrange("p (t a) -> p t a", a=1).to_broadcast([P, T, E]),
                                        ALU.mult).then_inc(s["w"], 1)
                dve.wait_ge(s["wT_ps"], 1)
                nc.vector.tensor_copy(wtT[:, :], banks[6][:, P:2 * P]).then_inc(s["wT"], 1)
                for c in range(FC):
                    dve.wait_ge(s["b2_ps"], c + 1)
                    v = xs[:, 4 * c:4 * c + 4, :]
                    nc.vector.tensor_tensor(v, v, banks[c].rearrange("p (t d) -> p t d", t=4), ALU.add).then_inc(s["x2"], 1)
                dve.wait_ge(s["x2"], FC)

                def up(e, buf, n):
                    c, ft = divmod(n, FT)
                    wait(dve, "x1ps", UP, e, n + 1)
                    wait(dve, "gl", UP, e, n + 1)
                    if ft == 0:
                        wait(dve, "yps", FC, e, c - 1)
                    nc.vector.scalar_tensor_tensor(hid[:, c % 2, ft, :], banks[3 + n % 3],
                                                   b1s[:, buf, ft:ft + 1], G[:, n % 2, :],
                                                   ALU.add, ALU.mult).then_inc(s["hd"], 1)

                def gather(e, c):
                    wait(dve, "yps", FC, e, c + 1)
                    for t in range(4):
                        wait(dve, "acc", T, e, 4 * c + t - T + 1)
                        nc.vector.scalar_tensor_tensor(xs[:, 4 * c + t, :], banks[6 + c % 2][:, t * P:(t + 1) * P],
                                                       wts[:, 4 * c + t, bass.ds(e, 1)], xs[:, 4 * c + t, :],
                                                       ALU.mult, ALU.add).then_inc(s["acc"], 1)

                dve.sem_inc(s["hd"], START["hd"])
                dve.sem_inc(s["acc"], START["acc"])
                def expert(e, buf, pair):
                    dve.wait_ge(s[f"w_in{buf}"], pair * 48 + 48)
                    for c in range(FC):
                        for ft in range(FT):
                            up(e, buf, c * FT + ft)
                            if ft == 1 and c > 0:
                                gather(e, c - 1)
                    gather(e, FC - 1)

                with dve.Fori(0, E // 2) as p:
                    expert(2 * p, 0, p)
                    expert(2 * p + 1, 1, p)

            @block.scalar
            def _(act):
                rstd_root(nc, act, s["rs"], g)
                for c in range(FC):
                    act.wait_ge(s["xt_ps"], c + 1)
                    nc.scalar.copy(xT[:, c * NS:(c + 1) * NS], banks[c]).then_inc(s["xt"], 1)
                rstd_root(nc, act, s["hrs"], g)
                act.wait_ge(s["hn"], T + 2)
                nc.scalar.activation(hg[:, :, :], hr[:, :, :], ACT.Gelu_apprx_tanh).then_inc(s["gelu"], 1)
                for c in range(2):
                    act.wait_ge(s["hT_ps"], c + 1)
                    nc.scalar.copy(hT[:, 4 * c:4 * c + 4, :], banks[4 + c].rearrange("p (t n) -> p t n", n=P)).then_inc(s["hT"], 1)
                act.wait_ge(s["r"], 2)
                nc.scalar.activation(lgt[:, :, :], lgt[:, :, :], ACT.Exp).then_inc(s["ex"], 1)

                act.sem_inc(s["gl"], START["gl"])

                def expert(e, buf, pair):
                    act.wait_ge(s[f"w_in{buf}"], pair * 48 + 48)
                    for n in range(UP):
                        wait(act, "x2ps", UP, e, n + 1)
                        wait(act, "hd", UP, e, n - 1)
                        nc.scalar.activation(G[:, n % 2, :], banks[n % 3], ACT.Gelu_apprx_tanh,
                                             bias=b1s[:, buf, FT + n % FT:FT + n % FT + 1]).then_inc(s["gl"], 1)

                with act.Fori(0, E // 2) as p:
                    expert(2 * p, 0, p)
                    expert(2 * p + 1, 1, p)

            @block.tensor
            def _(pe):
                for t in range(T):
                    pe.wait_ge(s["xn"], t + 1)
                    ins = nc.tensor.transpose(banks[t // 4][:, (t % 4) * P:(t % 4 + 1) * P], xn[:, t, :], C("ident"))
                    if t % 4 == 3:
                        ins.then_inc(s["xt_ps"], 1)
                pe.wait_ge(s["xt"], FC)
                for t in range(T):
                    ins = nc.tensor.matmul(banks[4 + t // 8][:, (t % 8) * R1:(t % 8 + 1) * R1], xT[:, t * P:(t + 1) * P],
                                           C("wr1"), start=True, stop=True)
                    if t % 8 == 7:
                        ins.then_inc(s["h_ps"], 1)
                pe.wait_ge(s["gelu"], 1)
                for t in range(T // 2):
                    ins = nc.tensor.transpose(banks[4 + t // 4][:, (t % 4) * P:(t % 4 + 1) * P],
                                              hg[:, 2 * t:2 * t + 2, :].rearrange("p t n -> p (t n)"), C("ident"))
                    if t % 4 == 3:
                        ins.then_inc(s["hT_ps"], 1)
                pe.wait_ge(s["hT"], 2)
                pe.wait_ge(s["own"], 1)
                for t in range(T):
                    z = R1 * (t % 2)
                    ins = nc.tensor.matmul(banks[6 + t % 2][:, t // 2 * E:(t // 2 + 1) * E], hT[z:z + R1, t // 2, :],
                                           wr2[z:z + R1, :], start=True, stop=True)
                    if t >= T - 2:
                        ins.then_inc(s["l_ps"], 1)
                pe.wait_ge(s["w"], 1)
                nc.tensor.transpose(banks[6][:, P:2 * P], wts[:, :, :].rearrange("p t e -> p (t e)"),
                                    C("ident")).then_inc(s["wT_ps"], 1)
                pe.wait_ge(s["wT"], 1)
                pe.wait_ge(s["own"], 2)
                for c in range(FC):
                    nc.tensor.matmul(banks[c], wtT[:, :], b2own[:, 4 * c:4 * c + 4, :].rearrange("p t d -> p (t d)"),
                                     start=True, stop=True).then_inc(s["b2_ps"], 1)
                pe.wait_ge(s["x2"], FC)

                def up(e, buf, n):
                    c, ft = divmod(n, FT)
                    for half, done, used, bank in ((1, "x2ps", "gl", n % 3), (0, "x1ps", "hd", 3 + n % 3)):
                        wait(pe, used, UP, e, n - 2)
                        nc.tensor.matmul(banks[bank], w1s[:, buf, half * F + ft * P:half * F + (ft + 1) * P],
                                         xT[:, c * NS:(c + 1) * NS], start=True, stop=True).then_inc(s[done], 1)

                def down(e, buf, c):
                    wait(pe, "hd", UP, e, FT * (c + 1))
                    wait(pe, "acc", T, e, 4 * (c - 1))
                    for t in range(4):
                        for ft in range(FT):
                            ins = nc.tensor.matmul(banks[6 + c % 2][:, t * P:(t + 1) * P],
                                                   hid[:, c % 2, ft, t * P:(t + 1) * P], w2s[:, buf, ft, :],
                                                   start=ft == 0, stop=ft == FT - 1)
                    ins.then_inc(s["yps"], 1)

                def expert(e, buf, pair):
                    pe.wait_ge(s[f"w_in{buf}"], pair * 48 + 48)
                    for c in range(FC):
                        for ft in range(FT):
                            up(e, buf, c * FT + ft)
                            if ft == 1 and c > 0:
                                down(e, buf, c - 1)
                    down(e, buf, FC - 1)

                pe.sem_inc(s["yps"], START["yps"])
                with pe.Fori(0, E // 2) as p:
                    expert(2 * p, 0, p)
                    expert(2 * p + 1, 1, p)


_NAMES = ["attn_Wq", "attn_bq", "attn_Wk", "attn_bk", "attn_Wv", "attn_bv", "attn_Wo", "attn_bo", "attn_rel_W",
          "attn_rel_b", "attn_logical_bias", "attn_gate_W", "attn_gate_b", "ffn_Wr1", "ffn_br1", "ffn_ln_scale",
          "ffn_ln_bias", "ffn_Wr2", "ffn_br2", "ffn_b1", "ffn_b2"]


def kernel(**inputs):
    import numpy as np
    import concourse.bacc as bacc
    from concourse.bass_utils import run_bass_kernel_spmd

    g = {n: np.asarray(inputs["L0_" + n]) for n in _NAMES}
    packed = np.zeros((P, CW_ALL), np.float32)

    def put(name, a):
        packed[:, AT[name]] = a

    for name, src in (("wqT", "attn_Wq"), ("wkT", "attn_Wk"), ("wvT", "attn_Wv"), ("woT", "attn_Wo"),
                      ("gateT", "attn_gate_W")):
        put(name, g[src].T)
    put("relI", g["attn_rel_W"][:, :D].T)
    put("relJ", g["attn_rel_W"][:, D:].T)
    put("bq", g["attn_bq"][:, None])
    put("bk", g["attn_bk"][:, None])
    for name, src in (("bv", "attn_bv"), ("bo", "attn_bo"), ("relb", "attn_rel_b"), ("gateb", "attn_gate_b"),
                      ("br1", "ffn_br1"), ("lns", "ffn_ln_scale"), ("lnb", "ffn_ln_bias"), ("br2", "ffn_br2")):
        put(name, g[src][None, :])
    put("bias", g["attn_logical_bias"].T.reshape(1, -1))
    put("ident", np.eye(P, dtype=np.float32))
    put("diag", np.tile(np.eye(IB, dtype=np.float32), (P // IB, 1)))
    put("wr1", g["ffn_Wr1"])
    put("wr2", np.tile(g["ffn_Wr2"], (2, 1)))
    put("b2", np.tile(g["ffn_b2"], (T, 1)))
    put("own", np.repeat(np.eye(T, dtype=np.float32), E, axis=0))
    put("before", np.tri(E, E, -1, dtype=np.float32).reshape(1, -1))
    put("b1", g["ffn_b1"].reshape(E, 2 * FT, P).transpose(2, 0, 1).reshape(P, -1))

    nc = bacc.Bacc("TRN2", target_bir_lowering=False, num_devices=1)
    arrays, aps = {}, []
    for name, a in (("x", np.asarray(inputs["L0_attn_hidden_states"])[0]), ("consts", packed),
                    ("w1", np.asarray(inputs["L0_ffn_W1"])), ("w2", np.asarray(inputs["L0_ffn_W2"]))):
        arrays[name] = np.ascontiguousarray(a)
        aps.append(nc.dram_tensor(name, a.shape, F32, kind="ExternalInput").ap())
    out = nc.dram_tensor("out", (S, D), F32, kind="ExternalOutput").ap()
    build(nc, *aps, out)
    r = run_bass_kernel_spmd(nc, [arrays], core_ids=[0])
    return r.results[0]["out"].reshape(1, S, D)
```

```python
from contextlib import ExitStack

import concourse.bass as bass
from concourse import mybir

F32 = mybir.dt.float32
F16 = mybir.dt.float16
BF16 = mybir.dt.bfloat16
ALU = mybir.AluOpType
ACT = mybir.ActivationFunctionType
AX_X = mybir.AxisListType.X

P = 128
S, D = 2048, 128
H, HD = 16, 8
T = S // P
PAIRS = H // 2
SLOTS = 6
QPART = [0, 0, 1, 0, 2, 1]
KPART = [0, 1, 0, 2, 0, 1]
ROWS = 2 * SLOTS * HD
SROWS = ROWS + 2 * 3
IB = 16
BLOCKS = P // IB
CHUNKS = 2
CW = S // CHUNKS
JC = CW // P
VW = HD + 1
NS = 512
MAXS = S // NS * H
E, F = 8, 512
FT = F // P
R1 = 64
FC = S // NS
LN_EPS, ROUTER_EPS = 1e-5, 1e-6

CONST = [("wqT", D), ("wkT", D), ("wvT", D), ("woT", D), ("relI", 3), ("relJ", 3), ("gateT", H),
         ("bq", 1), ("bk", 1), ("bv", D), ("bo", D), ("relb", 3), ("gateb", H), ("bias", 3 * H),
         ("ident", P), ("diag", IB), ("wr1", R1), ("br1", R1), ("lns", R1), ("lnb", R1), ("wr2", E),
         ("br2", E), ("b2", D), ("own", T), ("before", E * E), ("b1", E * 2 * FT)]
AT, n = {}, 0
for _name, _w in CONST:
    AT[_name] = slice(n, n + _w)
    n += _w
CW_ALL = n


def build(nc, x, consts, w1, w2, out):
    q_dram = nc.dram_tensor("q_parts", [2, SLOTS, HD * PAIRS, S], BF16, kind="Internal").ap()
    k_dram = nc.dram_tensor("k_parts", [2, SLOTS, HD * PAIRS, S], BF16, kind="Internal").ap()
    a_dram = nc.dram_tensor("a_parts", [S, 4, H], F16, kind="Internal").ap()

    ctx = ExitStack()
    with ctx:
        def sb(name, shape, dt, c=ctx):
            return c.enter_context(nc.sbuf_tensor(name, shape, dt))

        def sem(name, c=ctx):
            return c.enter_context(nc.semaphore(name))

        psS = ctx.enter_context(nc.psum_tensor("psS", [P, 2, 2 * NS], F32))
        psO = ctx.enter_context(nc.psum_tensor("psO", [P, NS], F32))
        psM = ctx.enter_context(nc.psum_tensor("psM", [P, 2, NS], F32))
        psX = ctx.enter_context(nc.psum_tensor("psX", [P, NS], F32))
        banks = [psS[:, 0, 0:NS], psS[:, 0, NS:], psS[:, 1, 0:NS], psS[:, 1, NS:],
                 psO[:, :], psM[:, 0, :], psM[:, 1, :], psX[:, :]]

        cst = sb("cst", [P, CW_ALL], F32)

        def C(name):
            return cst[:, AT[name]]

        xs = sb("xs", [P, T, D], F32)
        stats = sb("stats", [P, T, 6], F32)
        mv = sb("mv", [P, T, 2], F32)
        rstd = sb("rstd", [P, T], F32)
        var = sb("var", [P, T], F32)
        newton = sb("newton", [P, T], F32)

        attention(nc, ctx, sb, sem, locals())
        experts(nc, sb, sem, locals())


RSTD = 7


def rstd_first(nc, pool, done, eps, g):
    nc.gpsimd.tensor_scalar(g["var"][:, :], g["mv"][:, :, 1], eps, None, ALU.add).then_inc(done, 1)


def rstd_reciprocal(nc, dve, done, g):
    dve.wait_ge(done, 1)
    nc.vector.reciprocal(g["rstd"][:, :], g["var"][:, :]).then_inc(done, 1)


def rstd_root(nc, act, done, g):
    act.wait_ge(done, 2)
    nc.scalar.activation(g["rstd"][:, :], g["rstd"][:, :], ACT.Sqrt).then_inc(done, 1)


def rstd_step(nc, pool, done, g):
    rstd, var, newton = g["rstd"][:, :], g["var"][:, :], g["newton"][:, :]
    pool.wait_ge(done, 3)
    nc.gpsimd.tensor_tensor(newton, rstd, rstd, ALU.mult).then_inc(done, 1)
    pool.wait_ge(done, 4)
    nc.gpsimd.tensor_tensor(newton, newton, var, ALU.mult).then_inc(done, 1)
    pool.wait_ge(done, 5)
    nc.gpsimd.tensor_scalar(newton, newton, -0.5, 1.5, ALU.mult, ALU.add).then_inc(done, 1)
    pool.wait_ge(done, 6)
    nc.gpsimd.tensor_tensor(rstd, rstd, newton, ALU.mult).then_inc(done, 1)


def attention(nc, outer, sb, sem, g):
    C, xs, banks = g["C"], g["xs"], g["banks"]
    psS, psO, psM, psX = g["psS"], g["psO"], g["psM"], g["psX"]
    stats, mv, rstd, cst = g["stats"], g["mv"], g["rstd"], g["cst"]
    q_dram, k_dram, a_dram = g["q_dram"], g["k_dram"], g["a_dram"]
    with ExitStack() as ctx:
        kst = sb("kst", [SROWS, PAIRS, S], BF16, ctx)
        V = sb("V", [P, T, H, VW], F32, ctx)
        beta = sb("beta", [P, 2, S], F32, ctx)
        alpha = sb("alpha", [P, T, 2], F32, ctx)
        gtop = sb("gtop", [P, T, H], F32, ctx)
        ast = sb("ast", [P, T * BLOCKS, H], F16, ctx)
        diag = sb("diag", [P, IB], F16, ctx)
        prepare(nc, sb, sem, {**g, **locals()})
        attend(nc, sb, sem, {**g, **locals()})


def prepare(nc, sb, sem, g):
    C, xs, banks, x = g["C"], g["xs"], g["banks"], g["x"]
    stats, mv, rstd, cst, consts = g["stats"], g["mv"], g["rstd"], g["cst"], g["consts"]
    q_dram, k_dram, a_dram = g["q_dram"], g["k_dram"], g["a_dram"]
    kst, V, beta, alpha, gtop, ast, diag = (g[n] for n in ("kst", "V", "beta", "alpha", "gtop", "ast", "diag"))
    with ExitStack() as ctx:
        xn = sb("xn", [P, T, D], F32, ctx)
        xT = sb("xT", [P, S], F32, ctx)
        proj = sb("proj", [P, 2, S], F32, ctx)
        rest = sb("rest", [P, S], F32, ctx)
        parts = sb("parts", [P, 2, 3, S], BF16, ctx)
        ones = sb("ones", [P, P], F32, ctx)
        dJ = sb("dJ", [P, 2], F32, ctx)
        dJb = sb("dJb", [P, 2, P], F32, ctx)
        wnat = sb("wnat", [P, 2 + H], F32, ctx)
        drb = sb("drb", [P, 2], F32, ctx)
        dL = sb("dL", [P, 3, H], F32, ctx)
        gate = sb("gate", [P, T, H], F32, ctx)
        gated = sb("gated", [P, T, 2, H], F32, ctx)
        gparts = sb("gparts", [P, T, 4, H], F16, ctx)

        names = ["load", "loadx", "kone", "chain", "dv", "rs", "xn_ready", "xt_ps", "xt_ready", "w_ready",
                 "mm_q", "mm_k", "mm_v", "mm_b", "mm_n", "q_parts", "k_parts", "a_parts", "gsum", "gexp",
                 "v_copied", "b_copied", "q_out", "k_out", "a_out", "k_in", "a_in"]
        s = {n: sem("p_" + n, ctx) for n in names}
        with nc.Block() as block:

            @block.sync
            def _(sp):
                sp.dma_start(xs[:, :, :], x.rearrange("(t p) d -> p t d", p=P)).then_inc(s["loadx"], 16)
                sp.dma_start(cst[:, :], consts).then_inc(s["load"], 16)
                sp.wait_ge(s["k_parts"], 3)
                for n in range(SLOTS):
                    sp.dma_start(k_dram[:, n, :, :], parts[:, 1, KPART[n], :]).then_inc(s["k_out"], 16)
                sp.wait_ge(s["k_out"], 16 * SLOTS)
                sp.wait_ge(s["kone"], 1)
                sp.dma_start(kst[0:ROWS, :, :],
                             k_dram.rearrange("z n (d a) s -> (z n d) a s", a=PAIRS)).then_inc(s["k_in"], 16)
                sp.wait_ge(s["q_parts"], 3)
                for n in range(SLOTS):
                    sp.dma_start(q_dram[:, n, :, :], parts[:, 0, QPART[n], :]).then_inc(s["q_out"], 16)
                sp.wait_ge(s["a_parts"], 2)
                sp.dma_start(a_dram.rearrange("(t p) a h -> p t (a h)", p=P),
                             gparts[:, :, :, :].rearrange("p t a h -> p t (a h)")).then_inc(s["a_out"], 16)
                sp.wait_ge(s["a_out"], 16)
                for n in range(8):
                    part = (n % 4) // 2 + 2 * (n // 4)
                    first = n // 4 * (P // 2)
                    src = a_dram[:, part, :].rearrange("(b i) h -> i b h", i=IB)
                    sp.dma_start(ast[first + n % 4:first + P // 2:4, :, :], src).then_inc(s["a_in"], 16)
                sp.wait_ge(s["k_in"], 16)
                sp.wait_ge(s["a_in"], 16 * 8)
                sp.wait_ge(s["q_out"], 16 * SLOTS)

            @block.gpsimd
            def _(pool):
                nc.gpsimd.memset(kst[:, :, :], 1.0).then_inc(s["kone"], 1)
                nc.gpsimd.memset(V[:, :, :, HD:VW], 1.0).then_inc(s["v_copied"], 1)
                pool.wait_ge(s["dv"], 2 * T)
                rstd_first(nc, pool, s["rs"], LN_EPS, g)
                rstd_step(nc, pool, s["rs"], g)

            @block.vector
            def _(dve):
                dve.wait_ge(s["load"], 16)
                L = C("bias").rearrange("p (r h) -> p r h", h=H)
                nc.vector.tensor_tensor(dL[:, 2, :], L[:, 0, :], L[:, 1, :], ALU.max).then_inc(s["w_ready"], 1)
                dve.wait_ge(s["w_ready"], 1)
                nc.vector.tensor_tensor(dL[:, 2, :], dL[:, 2, :], L[:, 2, :], ALU.max).then_inc(s["w_ready"], 1)
                dve.wait_ge(s["w_ready"], 2)
                nc.vector.tensor_tensor(dL[:, 2, :], dL[:, 2, :], L[:, 2, :], ALU.subtract).then_inc(s["w_ready"], 1)
                for r in range(2):
                    nc.vector.tensor_tensor(dL[:, r, :], L[:, 2, :], L[:, r, :], ALU.subtract).then_inc(s["w_ready"], 1)
                nc.vector.tensor_tensor(drb[:, :], C("relb")[:, 0:2], C("relb")[:, 2:3].to_broadcast([P, 2]),
                                        ALU.subtract).then_inc(s["w_ready"], 1)
                nc.vector.tensor_tensor(wnat[:, 0:2], C("relI")[:, 0:2], C("relI")[:, 2:3].to_broadcast([P, 2]),
                                        ALU.subtract).then_inc(s["w_ready"], 1)
                nc.vector.tensor_copy(wnat[:, 2:2 + H], C("gateT")).then_inc(s["w_ready"], 1)
                nc.vector.tensor_copy(diag[:, :], C("diag")).then_inc(s["w_ready"], 1)
                nc.vector.memset(ones[:, :], 1.0).then_inc(s["w_ready"], 1)
                nc.vector.tensor_tensor(dJ[:, :], C("relJ")[:, 0:2], C("relJ")[:, 2:3].to_broadcast([P, 2]),
                                        ALU.subtract).then_inc(s["w_ready"], 1)
                dve.wait_ge(s["w_ready"], 11)
                for r in range(2):
                    nc.vector.tensor_scalar(dJb[:, r, :], ones[:, :], dJ[:, r:r + 1], None,
                                            ALU.mult).then_inc(s["w_ready"], 1)
                dve.wait_ge(s["loadx"], 16)
                for t in range(T):
                    nc.vector.bn_stats(stats[:, t, :], xs[:, t, :]).then_inc(s["dv"], 1)
                for t in range(T):
                    dve.wait_ge(s["dv"], t + 1)
                    nc.vector.bn_aggr(mv[:, t, :], stats[:, t, :]).then_inc(s["dv"], 1)
                dve.wait_ge(s["dv"], 2 * T)
                rstd_reciprocal(nc, dve, s["rs"], g)
                dve.wait_ge(s["rs"], RSTD)
                for t in range(T):
                    nc.vector.tensor_scalar(xn[:, t, :], xs[:, t, :], mv[:, t, 0:1], rstd[:, t:t + 1],
                                            ALU.subtract, ALU.mult).then_inc(s["xn_ready"], 1)
                dve.wait_ge(s["xn_ready"], T)
                dve.wait_ge(s["load"], 16)
                nc.vector.tensor_tensor(xs[:, :, :], xs[:, :, :],
                                        C("bo").rearrange("p (a d) -> p a d", a=1).to_broadcast([P, T, D]),
                                        ALU.add).then_inc(s["chain"], 1)

                def split(which, bias, scale, mm, done):
                    p32 = proj[:, which, :]
                    dve.wait_ge(s[mm], FC)
                    for c in range(FC):
                        nc.vector.tensor_scalar(proj[:, which, c * NS:(c + 1) * NS], banks[4 * which + c], bias,
                                                scale, ALU.add, ALU.mult).then_inc(s["chain"], 1)
                    dve.wait_ge(s["chain"], 1 + FC + which * (FC + 1))
                    nc.vector.tensor_copy(parts[:, which, 0, :], p32).then_inc(s[done], 1)
                    dve.wait_ge(s[done], 1)
                    nc.vector.tensor_tensor(rest[:, :], p32, parts[:, which, 0, :], ALU.subtract).then_inc(s["chain"], 1)
                    dve.wait_ge(s["chain"], 2 + FC + which * (FC + 1))
                    nc.vector.tensor_copy(parts[:, which, 1, :], rest[:, :]).then_inc(s[done], 1)
                    dve.wait_ge(s[done], 2)
                    nc.vector.tensor_tensor(parts[:, which, 2, :], rest[:, :], parts[:, which, 1, :],
                                            ALU.subtract).then_inc(s[done], 1)
                    dve.wait_ge(s[done], 3)

                split(0, C("bq"), float(HD) ** -0.5, "mm_q", "q_parts")
                split(1, C("bk"), 1.0, "mm_k", "k_parts")
                dve.wait_ge(s["mm_n"], 1)
                dve.wait_ge(s["w_ready"], 13)
                nat = banks[0][:, 0:T * (2 + H)].rearrange("p (t n) -> p t n", t=T)
                nc.vector.tensor_tensor(alpha[:, :, :], nat[:, :, 0:2],
                                        drb[:, :].rearrange("p (a n) -> p a n", a=1).to_broadcast([P, T, 2]),
                                        ALU.add).then_inc(s["gsum"], 1)
                nc.vector.tensor_tensor(gate[:, :, :], nat[:, :, 2:2 + H],
                                        C("gateb").rearrange("p (a n) -> p a n", a=1).to_broadcast([P, T, H]),
                                        ALU.add).then_inc(s["gsum"], 1)
                dve.wait_ge(s["gexp"], 1)
                nc.vector.tensor_scalar(gate[:, :, :], gate[:, :, :], 1.0, None, ALU.add).then_inc(s["gsum"], 1)
                dve.wait_ge(s["gsum"], 3)
                nc.vector.reciprocal(gate[:, :, :], gate[:, :, :]).then_inc(s["gsum"], 1)
                dve.wait_ge(s["gsum"], 4)
                for r in range(3):
                    dst = gated[:, :, r, :] if r < 2 else gtop[:, :, :]
                    nc.vector.tensor_tensor(dst, gate[:, :, :], dL[:, r:r + 1, :].to_broadcast([P, T, H]),
                                            ALU.mult).then_inc(s["gsum"], 1)
                dve.wait_ge(s["gsum"], 7)
                nc.vector.tensor_copy(gparts[:, :, 0:2, :], gated[:, :, :, :]).then_inc(s["a_parts"], 1)
                dve.wait_ge(s["a_parts"], 1)
                nc.vector.tensor_tensor(gparts[:, :, 2:4, :], gated[:, :, :, :], gparts[:, :, 0:2, :],
                                        ALU.subtract).then_inc(s["a_parts"], 1)
                for c in range(4):
                    dve.wait_ge(s["mm_v"], c + 1)
                    src = banks[4 + c].rearrange("p (t h d) -> p t h d", t=4, d=HD)
                    for t in range(4):
                        nc.vector.tensor_tensor(V[:, 4 * c + t, :, 0:HD], src[:, t],
                                                C("bv").rearrange("p (h d) -> p h d", d=HD),
                                                ALU.add).then_inc(s["v_copied"], 1)

            @block.scalar
            def _(act):
                rstd_root(nc, act, s["rs"], g)
                for c in range(FC):
                    act.wait_ge(s["xt_ps"], c + 1)
                    nc.scalar.copy(xT[:, c * NS:(c + 1) * NS], banks[c]).then_inc(s["xt_ready"], 1)
                act.wait_ge(s["gsum"], 2)
                nc.scalar.activation(gate[:, :, :], gate[:, :, :], ACT.Exp, scale=-1.0).then_inc(s["gexp"], 1)
                for r in range(2):
                    for c in range(FC):
                        n = r * FC + c
                        act.wait_ge(s["mm_b"], n + 1)
                        nc.scalar.copy(beta[:, r, c * NS:(c + 1) * NS], banks[1 + n % 3]).then_inc(s["b_copied"], 1)

            @block.tensor
            def _(pe):
                pe.wait_ge(s["load"], 16)
                for t in range(T):
                    pe.wait_ge(s["xn_ready"], t + 1)
                    ins = nc.tensor.transpose(banks[t // 4][:, (t % 4) * P:(t % 4 + 1) * P], xn[:, t, :], C("ident"))
                    if t % 4 == 3:
                        ins.then_inc(s["xt_ps"], 1)
                pe.wait_ge(s["xt_ready"], FC)
                for w, mm, first in (("wqT", "mm_q", 0), ("wkT", "mm_k", 4)):
                    for c in range(FC):
                        nc.tensor.matmul(banks[first + c], C(w), xT[:, c * NS:(c + 1) * NS],
                                         start=True, stop=True).then_inc(s[mm], 1)
                pe.wait_ge(s["w_ready"], 13)
                pe.wait_ge(s["chain"], 1 + FC)
                for t in range(T):
                    ins = nc.tensor.matmul(banks[0][:, t * (2 + H):(t + 1) * (2 + H)], xT[:, t * P:(t + 1) * P],
                                           wnat[:, :], start=True, stop=True)
                ins.then_inc(s["mm_n"], 1)
                pe.wait_ge(s["chain"], 1 + FC + FC + 1)
                for t in range(T):
                    ins = nc.tensor.matmul(banks[4 + t // 4][:, (t % 4) * P:(t % 4 + 1) * P],
                                           xT[:, t * P:(t + 1) * P], C("wvT"), start=True, stop=True)
                    if t % 4 == 3:
                        ins.then_inc(s["mm_v"], 1)
                for r in range(2):
                    for c in range(FC):
                        n = r * FC + c
                        if n >= 3:
                            pe.wait_ge(s["b_copied"], n - 2)
                        nc.tensor.matmul(banks[1 + n % 3], dJb[:, r, :], xT[:, c * NS:(c + 1) * NS],
                                         start=True, stop=True).then_inc(s["mm_b"], 1)


def attend(nc, sb, sem, g):
    C, xs = g["C"], g["xs"]
    psS, psO, psM, psX = g["psS"], g["psO"], g["psM"], g["psX"]
    q_dram = g["q_dram"]
    kst, V, beta, alpha, gtop, ast, diag = (g[n] for n in ("kst", "V", "beta", "alpha", "gtop", "ast", "diag"))
    with ExitStack() as ctx:
        qnext = sb("qnext", [SROWS, PAIRS, 2, P], BF16, ctx)
        qcur = sb("qcur", [SROWS, PAIRS, 2, P], BF16, ctx)
        anext = sb("anext", [P, BLOCKS * H, IB], F16, ctx)
        acur = sb("acur", [P, BLOCKS * H, IB], F16, ctx)
        pst = sb("pst", [P, CHUNKS, BLOCKS, CW], F16, ctx)
        pp = sb("pp", [P, CHUNKS, 4, CW], F16, ctx)
        top = [sb(f"top{c}", [P, CW], F32, ctx) for c in range(CHUNKS)]
        low = [sb(f"low{c}", [P, CW], F32, ctx) for c in range(CHUNKS)]
        rel = [[sb(f"rel{c}{r}", [P, CW], F32, ctx) for r in range(2)] for c in range(CHUNKS)]
        tot = [sb(f"tot{c}", [P, CW], F32, ctx) for c in range(CHUNKS)]
        ET = sb("ET", [P, 2, H, P], F32, ctx)
        mx = sb("mx", [P, H, S // NS], F32, ctx)
        mrow = sb("mrow", [P, H], F32, ctx)
        sh = sb("sh", [P, P], F32, ctx)
        shh = sb("shh", [P, 2, H], BF16, ctx)
        shT = sb("shT", [2 * 3 * PAIRS, P], BF16, ctx)
        osb = sb("osb", [P, NS], F32, ctx)
        den = sb("den", [P, H], F32, ctx)
        att = sb("att", [P, H, HD], F32, ctx)
        attT = sb("attT", [P, P], F32, ctx)

        names = ["zero_q", "zero_sh", "zero_o", "q_in", "sh_in", "st_in0", "st_in1", "scores", "exps", "av", "cur", "anext", "mxs",
                 "mxused", "lg0", "lg1", "ex0", "ex1", "sm0", "sm1", "ln0", "ln1", "nt0", "nt1",
                 "rc0", "rc1", "pr0", "pr1", "hi0", "hi1", "pd0", "pd1", "sh", "shps", "shT",
                 "o_sb", "o_ps", "den", "att", "aT_ps", "aT", "y_ps", "y"]
        s = {n: sem("a_" + n, ctx) for n in names}

        shv = sh[:, 0:2 * 3 * PAIRS].rearrange("p (z a n) -> p z a n", z=2, a=3)

        def by_pair(ap):
            return ap.rearrange("p (n z) -> p z n", z=2)

        def wait(eng, name, per, tile, more):
            if isinstance(tile, int) and per * tile + more <= 0:
                return
            eng.wait_ge(s[name], tile * per + more)

        with nc.Block() as block:

            @block.sync
            def _(sp):
                def load_stack(t, c):
                    wait(sp, f"pd{c}", 2, t, 2)
                    wait(sp, "scores", 2 * T, t, -2 * T + 2 * JC * (c + 1))
                    for b in range(BLOCKS):
                        for z in range(2):
                            sp.dma_start(pst[z * (P // 2):(z + 1) * (P // 2), c, b, :],
                                         pp[b * IB:(b + 1) * IB, c, :, :]).then_inc(s[f"st_in{c}"], 16)

                def load_q(t):
                    wait(sp, "cur", 4, t, 0)
                    for z in range(2):
                        src = q_dram[z, :, :, :].rearrange("n (d a) s -> (n d) a s", a=PAIRS)
                        sp.dma_start(qnext[z * SLOTS * HD:(z + 1) * SLOTS * HD, :, z, :],
                                      src[:, :, bass.ds(t * P, P)]).then_inc(s["q_in"], 16)

                def load_shift(t):
                    wait(sp, "shT", 1, t, 1)
                    for z in range(2):
                        sp.dma_start(qnext[ROWS + 3 * z:ROWS + 3 * z + 3, :, z, :],
                                     shT[z * 3 * PAIRS:(z + 1) * 3 * PAIRS, :]).then_inc(s["sh_in"], 16)

                def tile(t, last):
                    load_stack(t, 0)
                    load_shift(t)
                    if not last:
                        load_q(t + 1)
                    load_stack(t, 1)

                sp.wait_ge(s["zero_q"], 1)
                load_q(0)
                tile(0, False)
                with sp.Fori(1, T - 1) as t:
                    tile(t, False)
                tile(T - 1, True)

            @block.gpsimd
            def _(pool):
                nc.gpsimd.memset(qnext[:, :, :, :], 0.0).then_inc(s["zero_q"], 1)
                nc.gpsimd.memset(sh[:, :], 0.0).then_inc(s["zero_sh"], 1)

                def total(t, c):
                    wait(pool, f"ex{c}", 3, t, 2)
                    wait(pool, f"rc{c}", 1, t, 0)
                    nc.gpsimd.tensor_tensor(tot[c][:, :], rel[c][0][:, :], rel[c][1][:, :], ALU.add).then_inc(s[f"sm{c}"], 1)
                    wait(pool, f"ex{c}", 3, t, 3)
                    wait(pool, f"sm{c}", 2, t, 1)
                    nc.gpsimd.tensor_tensor(tot[c][:, :], tot[c][:, :], low[c][:, :], ALU.add).then_inc(s[f"sm{c}"], 1)

                def check(t, c):
                    wait(pool, f"ln{c}", 2, t, 2)
                    nc.gpsimd.tensor_tensor(top[c][:, :], tot[c][:, :], low[c][:, :], ALU.mult).then_inc(s[f"nt{c}"], 1)

                def products(t, c):
                    wait(pool, f"rc{c}", 1, t, 1)
                    for l in rel[c]:
                        nc.gpsimd.tensor_tensor(l[:, :], l[:, :], top[c][:, :], ALU.mult).then_inc(s[f"pr{c}"], 1)

                def lows(t, c):
                    for r, l in enumerate(rel[c]):
                        wait(pool, f"hi{c}", 2, t, r + 1)
                        nc.gpsimd.tensor_tensor(pp[:, c, 2 * r + 1, :], l[:, :], pp[:, c, 2 * r, :],
                                                ALU.subtract).then_inc(s[f"pd{c}"], 1)

                def diagonal(t):
                    wait(pool, "cur", 4, t, 0)
                    nc.gpsimd.tensor_tensor(
                        anext[:, :, :],
                        ast[:, bass.ds(t * BLOCKS, BLOCKS), :].rearrange("p b (h a) -> p (b h) a", a=1)
                        .to_broadcast([P, BLOCKS * H, IB]),
                        diag[:, :].rearrange("p (a i) -> p a i", a=1).to_broadcast([P, BLOCKS * H, IB]),
                        ALU.mult).then_inc(s["anext"], 1)

                def ahead(t):
                    diagonal(t)
                    total(t, 0)
                    check(t, 0)
                    total(t, 1)
                    products(t, 0)
                    lows(t, 0)
                    check(t, 1)
                    products(t, 1)
                    lows(t, 1)

                ahead(0)
                with pool.Fori(0, T - 1) as t:
                    ahead(t + 1)

            @block.scalar
            def _(act):
                def exps(t, j):
                    for u in range(2):
                        wait(act, "scores", 2 * T, t, 2 * j + u + 1)
                        if u == 0:
                            wait(act, "av", T, t, j - 1)
                        nc.scalar.activation(
                            ET[:, j % 2, 8 * u:8 * u + 8, :].rearrange("p h (v i) -> p v h i", v=2),
                            psS[:, u, :].rearrange("p (v h i) -> p v h i", v=2, h=8),
                            ACT.Exp).then_inc(s["exps"], 1)

                def rel_exps(t, c):
                    for n, (dst, src, sc) in enumerate(((rel[c][0], rel[c][0], 1.0), (rel[c][1], rel[c][1], 1.0),
                                                        (low[c], top[c], -1.0))):
                        wait(act, f"lg{c}", 4, t, min(3 + n, 4))
                        if n == 2:
                            wait(act, f"rc{c}", 1, t, 0)
                        nc.scalar.activation(dst[:, :], src[:, :], ACT.Exp, scale=sc).then_inc(s[f"ex{c}"], 1)

                def rough_reciprocal(t, c):
                    wait(act, f"sm{c}", 2, t, 2)
                    nc.scalar.activation(low[c][:, :], tot[c][:, :], ACT.Ln).then_inc(s[f"ln{c}"], 1)
                    wait(act, f"ln{c}", 2, t, 1)
                    nc.scalar.activation(low[c][:, :], low[c][:, :], ACT.Exp, scale=-1.0).then_inc(s[f"ln{c}"], 1)

                def high(t, c):
                    for r, l in enumerate(rel[c]):
                        wait(act, f"pr{c}", 2, t, r + 1)
                        wait(act, f"st_in{c}", 32 * BLOCKS, t, 0)
                        nc.scalar.copy(pp[:, c, 2 * r, :], l[:, :]).then_inc(s[f"hi{c}"], 1)

                def copy_outputs(t):
                    wait(act, "av", T, t, T)
                    wait(act, "o_ps", 1, t, 0)
                    nc.scalar.copy(osb[:, :], psO[:, :]).then_inc(s["o_sb"], 1)

                def copy_transposed(t):
                    wait(act, "aT_ps", 1, t, 1)
                    nc.scalar.copy(attT[:, :], psX[:, 0:P]).then_inc(s["aT"], 1)

                def tile(t, first, last):
                    for j in range(T):
                        exps(t, j)
                        if not first and j == 0:
                            copy_outputs(t - 1)
                        if not first and j == 5:
                            copy_transposed(t - 1)
                        if not last:
                            for c in range(CHUNKS):
                                if j == 3 + 4 * c:
                                    rel_exps(t + 1, c)
                                if j == 5 + 4 * c:
                                    rough_reciprocal(t + 1, c)
                                if j == 9 + 4 * c:
                                    high(t + 1, c)

                act.preload_act_table_set("natural_log_exp_and_others")
                for c in range(CHUNKS):
                    rel_exps(0, c)
                    rough_reciprocal(0, c)
                for c in range(CHUNKS):
                    high(0, c)
                tile(0, True, False)
                with act.Fori(1, T - 1) as t:
                    tile(t, False, False)
                tile(T - 1, False, True)
                copy_outputs(T - 1)
                copy_transposed(T - 1)

            @block.vector
            def _(dve):
                nc.vector.memset(psO[:, :], 0.0).then_inc(s["zero_o"], 1)

                def a(t, r):
                    return alpha[:, bass.ds(t, 1), r]

                def logits_top(t, c, r):
                    b = beta[:, r, c * CW:(c + 1) * CW]
                    if r == 1:
                        wait(dve, f"pr{c}", 2, t, 0)
                        nc.vector.tensor_scalar(top[c][:, :], b, a(t, 1), 0.0, ALU.add, ALU.max).then_inc(s[f"lg{c}"], 1)
                    else:
                        wait(dve, f"lg{c}", 4, t, 1)
                        nc.vector.scalar_tensor_tensor(top[c][:, :], b, a(t, 0), top[c][:, :], ALU.add,
                                                       ALU.max).then_inc(s[f"lg{c}"], 1)

                def logits(t, c, r):
                    wait(dve, f"lg{c}", 4, t, 2)
                    wait(dve, f"pd{c}", 2, t, 0)
                    nc.vector.scalar_tensor_tensor(rel[c][r][:, :], beta[:, r, c * CW:(c + 1) * CW], a(t, r),
                                                   top[c][:, :], ALU.add, ALU.subtract).then_inc(s[f"lg{c}"], 1)

                def newton(t, c):
                    wait(dve, f"nt{c}", 1, t, 1)
                    nc.vector.scalar_tensor_tensor(top[c][:, :], top[c][:, :], -2.0, low[c][:, :], ALU.add,
                                                   ALU.mult).then_inc(s[f"rc{c}"], 1)

                def maxima(t, lo, hi):
                    for m in range(lo, hi):
                        wait(dve, "mxs", MAXS, t, m + 1)
                        h, c = divmod(m, S // NS)
                        nc.vector.reduce_max(mx[:, h, c:c + 1], psM[:, m % 2, :], AX_X).then_inc(s["mxused"], 1)

                def shift(t):
                    wait(dve, "mxused", MAXS, t, MAXS)
                    wait(dve, "shps", 1, t, 0)
                    nc.vector.reduce_max(mrow[:, :], mx[:, :, :], AX_X).then_inc(s["sh"], 1)
                    wait(dve, "sh", 6, t, 1)
                    nc.vector.scalar_tensor_tensor(
                        shv[:, :, 0, :], by_pair(mrow[:, :]), -1.0,
                        gtop[:, bass.ds(t, 1), :].rearrange("p a (n z) -> p z (a n)", z=2),
                        ALU.mult, ALU.subtract).then_inc(s["sh"], 1)
                    wait(dve, "sh", 6, t, 2)
                    hv = [shh[:, n, :].rearrange("p (z n) -> p z n", z=2) for n in range(2)]
                    for n in range(2):
                        nc.vector.tensor_copy(hv[n], shv[:, :, n, :]).then_inc(s["sh"], 1)
                        wait(dve, "sh", 6, t, 3 + 2 * n)
                        nc.vector.tensor_tensor(shv[:, :, n + 1, :], shv[:, :, n, :], hv[n],
                                                ALU.subtract).then_inc(s["sh"], 1)
                        if n == 0:
                            wait(dve, "sh", 6, t, 4)

                def shift_rows(t):
                    wait(dve, "shps", 1, t, 1)
                    wait(dve, "sh_in", 32, t, 0)
                    nc.vector.tensor_copy(shT[:, :], psX[0:2 * 3 * PAIRS, 0:P]).then_inc(s["shT"], 1)

                def to_current(t):
                    wait(dve, "q_in", 32, t, 32)
                    wait(dve, "sh_in", 32, t, 32)
                    wait(dve, "anext", 1, t, 1)
                    for u in range(2):
                        wait(dve, "scores", 2 * T, t, u - 1)
                        nc.vector.tensor_copy(qcur[:, 4 * u:4 * u + 4, :, :],
                                              qnext[:, 4 * u:4 * u + 4, :, :]).then_inc(s["cur"], 1)
                        ac, an = (m[:, :, :].rearrange("p (b h) i -> p b (h i)", h=H)[:, :, u * P:(u + 1) * P]
                                  for m in (acur, anext))
                        nc.vector.tensor_copy(ac, an).then_inc(s["cur"], 1)

                def normalize(t):
                    v = psX[:, :].rearrange("p (h w) -> p h w", w=32)
                    wait(dve, "o_ps", 1, t, 1)
                    wait(dve, "aT_ps", 1, t, 0)
                    nc.vector.reciprocal(den[:, :], v[:, :, HD]).then_inc(s["den"], 1)
                    wait(dve, "den", 1, t, 1)
                    nc.vector.tensor_tensor(att[:, :, :], v[:, :, 0:HD],
                                            den[:, :].rearrange("p (h a) -> p h a", a=1).to_broadcast([P, H, HD]),
                                            ALU.mult).then_inc(s["att"], 1)

                def residual(t):
                    wait(dve, "y_ps", 1, t, 1)
                    nc.vector.tensor_tensor(xs[:, bass.ds(t, 1), :], xs[:, bass.ds(t, 1), :],
                                            psX[:, P:2 * P].rearrange("p (a d) -> p a d", a=1),
                                            ALU.add).then_inc(s["y"], 1)

                def tile(t, first, last):
                    for j in range(T):
                        lo = 6 * (j - 1)
                        for n in range(3):
                            if last:
                                break
                            if 0 <= lo < MAXS:
                                maxima(t + 1, lo + 2 * n, min(lo + 2 * n + 2, MAXS))
                            for c in range(CHUNKS):
                                at = j - 4 * c
                                if (at, n) in ((0, 0), (0, 2)):
                                    logits_top(t + 1, c, (at, n) == (0, 0))
                                if (at, n) in ((1, 1), (2, 1)):
                                    logits(t + 1, c, at - 1)
                                if (at, n) == (7, 1):
                                    newton(t + 1, c)
                        if not last and j == 13:
                            shift(t + 1)
                        if not last and j == 14:
                            shift_rows(t + 1)
                        if not first:
                            if j == 3:
                                normalize(t - 1)
                            if j == 7:
                                residual(t - 1)
                    if not last:
                        to_current(t + 1)

                for c in range(CHUNKS):
                    logits_top(0, c, 1)
                    logits_top(0, c, 0)
                    logits(0, c, 0)
                    logits(0, c, 1)
                for c in range(CHUNKS):
                    newton(0, c)
                maxima(0, 0, MAXS)
                dve.wait_ge(s["zero_sh"], 1)
                shift(0)
                shift_rows(0)
                to_current(0)
                tile(0, True, False)
                with dve.Fori(1, T - 1) as t:
                    tile(t, False, False)
                tile(T - 1, False, True)
                normalize(T - 1)
                residual(T - 1)

            @block.tensor
            def _(pe):
                def scores(t, j, u, v):
                    c, jj = divmod(j, JC)
                    if j == 0 and v == 0:
                        wait(pe, "cur", 4, t, 2 * u + 2)
                    if v == 0:
                        wait(pe, "exps", 2 * T, t, 2 * j + u - 1)
                    out = psS[:, u, v * NS:(v + 1) * NS]
                    for n in range(4):
                        a = 4 * u + n
                        nc.tensor.matmul(out[:, n * P:(n + 1) * P], kst[:, a, j * P:(j + 1) * P],
                                         qcur[:, a, :, v * 64:(v + 1) * 64], start=n == 0, stop=False,
                                         skip_group_check=True)
                    for n in range(4):
                        b = 4 * v + n
                        ins = nc.tensor.matmul(
                            out.rearrange("p (h i) -> p h i", h=8)[:, :, n * IB:(n + 1) * IB],
                            pst[:, c, b, jj * P:(jj + 1) * P],
                            acur[:, b * H + 8 * u:b * H + 8 * u + 8, :], start=False, stop=n == 3,
                            skip_group_check=True)
                    if v == 1:
                        ins.then_inc(s["scores"], 1)

                def times_v(t, j, half):
                    if half == 0:
                        wait(pe, "exps", 2 * T, t, 2 * j + 2)
                    if j == 0 and half == 0:
                        wait(pe, "o_sb", 1, t, 0)
                    for h in range(8 * half, 8 * half + 8):
                        gr, r = divmod(h, 4)
                        ins = nc.tensor.matmul(psO[32 * r:32 * r + VW, gr * P:(gr + 1) * P], V[:, j, h, :],
                                               ET[:, j % 2, h, :], start=j == 0 and gr == 0, stop=j == T - 1,
                                               skip_group_check=True)
                    if half == 1:
                        ins.then_inc(s["av"], 1)

                def maxima(t, lo, hi):
                    for m in range(lo, hi):
                        h, c = divmod(m, S // NS)
                        wait(pe, "mxused", MAXS, t, m - 1)
                        nc.tensor.matmul(psM[:, m % 2, :], qnext[0:ROWS, h // 2, h % 2, :],
                                         kst[0:ROWS, h // 2, c * NS:(c + 1) * NS], start=True,
                                         stop=True).then_inc(s["mxs"], 1)

                def shift(t):
                    wait(pe, "sh", 6, t, 6)
                    wait(pe, "y", 1, t, -1)
                    nc.tensor.transpose(psX[:, 0:P], sh[:, :], C("ident")).then_inc(s["shps"], 1)

                def outputs(t):
                    wait(pe, "o_sb", 1, t, 1)
                    wait(pe, "shT", 1, t, 2)
                    for gr in range(4):
                        ins = nc.tensor.transpose(psX[:, gr * P:(gr + 1) * P], osb[:, gr * P:(gr + 1) * P], C("ident"))
                    ins.then_inc(s["o_ps"], 1)

                def out_transpose(t):
                    wait(pe, "att", 1, t, 1)
                    nc.tensor.transpose(psX[:, 0:P], att[:, :, :].rearrange("p h d -> p (h d)"),
                                        C("ident")).then_inc(s["aT_ps"], 1)

                def out_project(t):
                    wait(pe, "aT", 1, t, 1)
                    nc.tensor.matmul(psX[:, P:2 * P], attT[:, :], C("woT"), start=True, stop=True).then_inc(s["y_ps"], 1)

                def tile(t, first, last):
                    for j in range(T):
                        if j % JC == 0:
                            wait(pe, f"st_in{j // JC}", 32 * BLOCKS, t, 32 * BLOCKS)
                        lo = 6 * (j - 1)
                        if not last and j == 14:
                            shift(t + 1)
                        for n in range(6):
                            if n < 4:
                                scores(t, j, n // 2, n % 2)
                            elif j > 0:
                                times_v(t, j - 1, n - 4)
                            elif not first:
                                times_v(t - 1, T - 1, n - 4)
                            if not last and lo + n == 0:
                                wait(pe, "q_in", 32, t, 64)
                            if not last and 0 <= lo + n < MAXS:
                                maxima(t + 1, lo + n, lo + n + 1)
                        if not first:
                            if j == 2:
                                outputs(t - 1)
                            if j == 4:
                                out_transpose(t - 1)
                            if j == 6:
                                out_project(t - 1)

                pe.wait_ge(s["zero_o"], 1)
                pe.wait_ge(s["q_in"], 32)
                maxima(0, 0, MAXS)
                shift(0)
                tile(0, True, False)
                with pe.Fori(1, T - 1) as t:
                    tile(t, False, False)
                tile(T - 1, False, True)
                for half in range(2):
                    times_v(T - 1, T - 1, half)
                pe.wait_ge(s["o_sb"], T)
                pe.wait_ge(s["y"], T - 1)
                for gr in range(4):
                    ins = nc.tensor.transpose(psX[:, gr * P:(gr + 1) * P], osb[:, gr * P:(gr + 1) * P], C("ident"))
                ins.then_inc(s["o_ps"], 1)
                out_transpose(T - 1)
                out_project(T - 1)


def experts(nc, sb, sem, g):
    C, xs, banks = g["C"], g["xs"], g["banks"]
    stats, mv, rstd, cst = g["stats"], g["mv"], g["rstd"], g["cst"]
    w1, w2, out = g["w1"], g["w2"], g["out"]
    with ExitStack() as ctx:
        xn = sb("xn2", [P, T, D], F32, ctx)
        xT = sb("xT2", [P, S], F32, ctx)
        hr = sb("hr", [P, T, R1], F32, ctx)
        hg = sb("hg", [P, T, R1], F32, ctx)
        hT = sb("hT", [P, T // 2, P], F32, ctx)
        wr2 = sb("wr2", [P, E], F32, ctx)
        lgt = sb("lgt", [P, T, E], F32, ctx)
        row = sb("row", [P, T], F32, ctx)
        pairs = sb("pairs", [P, T, E, E], F32, ctx)
        same = sb("same", [P, T, E, E], F32, ctx)
        wts = sb("wts", [P, T, E], F32, ctx)
        wtT = sb("wtT", [P, P], F32, ctx)
        b2own = sb("b2own", [P, T, D], F32, ctx)
        w1s = sb("w1s", [P, 2, 2 * F], F32, ctx)
        w2s = sb("w2s", [P, 2, FT, D], F32, ctx)
        G = sb("G", [P, 2, NS], F32, ctx)
        hid = sb("hid", [P, 2, FT, NS], F32, ctx)
        b1s = sb("b1s", [P, 2, 2 * FT], F32, ctx)
        b1_dram = g["consts"][:, AT["b1"]]

        names = ["dv", "rs", "xn", "xt_ps", "xt", "h_ps", "h", "hst", "hrs", "hn", "gelu", "hT_ps", "hT",
                 "l_ps", "lg", "ex", "r", "w", "wT_ps", "wT", "own", "b2_ps", "x2",
                 "w_in0", "w_in1", "x2ps", "x1ps", "gl", "hd", "yps", "acc", "out"]
        s = {n: sem("e_" + n, ctx) for n in names}
        UP = FC * FT

        START = {"gl": 3, "hd": 3, "yps": 2, "acc": T}

        def wait(eng, name, per, e, more):
            eng.wait_ge(s[name], e * per + more + START.get(name, 0))

        with nc.Block() as block:

            @block.sync
            def _(sp):
                def load(e, buf):
                    if not isinstance(e, int):
                        wait(sp, "yps", FC, e, -FC)
                    sp.dma_start(w1s[:, buf, :], w1[bass.ds(e, 1), :, :].rearrange("a c f -> c (a f)")).then_inc(s[f"w_in{buf}"], 16)
                    sp.dma_start(w2s[:, buf, :, :],
                                 w2[bass.ds(e, 1), :, :].rearrange("a (n p) d -> p (a n) d", p=P)).then_inc(s[f"w_in{buf}"], 16)
                    sp.dma_start(b1s[:, buf, :], b1_dram[:, bass.ds(e * 2 * FT, 2 * FT)]).then_inc(s[f"w_in{buf}"], 16)

                load(0, 0)
                load(1, 1)
                with sp.Fori(1, E // 2) as p:
                    load(2 * p, 0)
                    load(2 * p + 1, 1)
                wait(sp, "acc", T, E, 0)
                sp.dma_start(out.rearrange("(t p) d -> p t d", p=P), xs[:, :, :]).then_inc(s["out"], 16)
                sp.wait_ge(s["out"], 16)

            @block.gpsimd
            def _(pool):
                nc.gpsimd.tensor_copy(wr2[:, :], C("wr2")).then_inc(s["own"], 1)
                nc.gpsimd.tensor_tensor(b2own[:, :, :], C("b2").rearrange("p (a d) -> p a d", a=1).to_broadcast([P, T, D]),
                                        C("own").rearrange("p (t a) -> p t a", a=1).to_broadcast([P, T, D]),
                                        ALU.mult).then_inc(s["own"], 1)
                pool.wait_ge(s["dv"], 2 * T)
                rstd_first(nc, pool, s["rs"], LN_EPS, g)
                rstd_step(nc, pool, s["rs"], g)
                pool.wait_ge(s["hst"], 2 * T)
                rstd_first(nc, pool, s["hrs"], ROUTER_EPS, g)
                rstd_step(nc, pool, s["hrs"], g)

            @block.vector
            def _(dve):
                for t in range(T):
                    nc.vector.bn_stats(stats[:, t, :], xs[:, t, :]).then_inc(s["dv"], 1)
                for t in range(T):
                    dve.wait_ge(s["dv"], t + 1)
                    nc.vector.bn_aggr(mv[:, t, :], stats[:, t, :]).then_inc(s["dv"], 1)
                dve.wait_ge(s["dv"], 2 * T)
                rstd_reciprocal(nc, dve, s["rs"], g)
                dve.wait_ge(s["rs"], RSTD)
                for t in range(T):
                    nc.vector.tensor_scalar(xn[:, t, :], xs[:, t, :], mv[:, t, 0:1], rstd[:, t:t + 1],
                                            ALU.subtract, ALU.mult).then_inc(s["xn"], 1)
                for c in range(2):
                    dve.wait_ge(s["h_ps"], c + 1)
                    nc.vector.tensor_tensor(hr[:, 8 * c:8 * c + 8, :], banks[4 + c].rearrange("p (t n) -> p t n", n=R1),
                                            C("br1").rearrange("p (a n) -> p a n", a=1).to_broadcast([P, 8, R1]),
                                            ALU.add).then_inc(s["h"], 1)
                dve.wait_ge(s["h"], 2)
                dve.wait_ge(s["xn"], T)
                for t in range(T):
                    nc.vector.bn_stats(stats[:, t, :], hr[:, t, :]).then_inc(s["hst"], 1)
                for t in range(T):
                    dve.wait_ge(s["hst"], t + 1)
                    nc.vector.bn_aggr(mv[:, t, :], stats[:, t, :]).then_inc(s["hst"], 1)
                dve.wait_ge(s["hst"], 2 * T)
                rstd_reciprocal(nc, dve, s["hrs"], g)
                dve.wait_ge(s["hrs"], RSTD)
                for t in range(T):
                    nc.vector.tensor_scalar(hr[:, t, :], hr[:, t, :], mv[:, t, 0:1], rstd[:, t:t + 1],
                                            ALU.subtract, ALU.mult).then_inc(s["hn"], 1)
                dve.wait_ge(s["hn"], T)
                nc.vector.tensor_tensor(hr[:, :, :], hr[:, :, :], C("lns").rearrange("p (a n) -> p a n", a=1).to_broadcast([P, T, R1]),
                                        ALU.mult).then_inc(s["hn"], 1)
                dve.wait_ge(s["hn"], T + 1)
                nc.vector.tensor_tensor(hr[:, :, :], hr[:, :, :], C("lnb").rearrange("p (a n) -> p a n", a=1).to_broadcast([P, T, R1]),
                                        ALU.add).then_inc(s["hn"], 1)
                dve.wait_ge(s["l_ps"], 2)
                for z in range(2):
                    nc.vector.tensor_tensor(lgt[:, z:T:2, :], banks[6 + z][:, 0:T // 2 * E].rearrange("p (t e) -> p t e", e=E),
                                            C("br2").rearrange("p (a e) -> p a e", a=1).to_broadcast([P, T // 2, E]),
                                            ALU.add).then_inc(s["lg"], 1)
                dve.wait_ge(s["lg"], 2)
                nc.vector.reduce_max(row[:, :], lgt[:, :, :], AX_X).then_inc(s["r"], 1)
                dve.wait_ge(s["r"], 1)
                nc.vector.tensor_tensor(lgt[:, :, :], lgt[:, :, :], row[:, :].rearrange("p (t a) -> p t a", a=1).to_broadcast([P, T, E]),
                                        ALU.subtract).then_inc(s["r"], 1)
                dve.wait_ge(s["ex"], 1)
                nc.vector.reduce_sum(row[:, :], lgt[:, :, :], AX_X).then_inc(s["r"], 1)
                dve.wait_ge(s["r"], 3)
                nc.vector.reciprocal(row[:, :], row[:, :]).then_inc(s["r"], 1)
                dve.wait_ge(s["r"], 4)
                nc.vector.tensor_tensor(lgt[:, :, :], lgt[:, :, :], row[:, :].rearrange("p (t a) -> p t a", a=1).to_broadcast([P, T, E]),
                                        ALU.mult).then_inc(s["r"], 1)
                dve.wait_ge(s["r"], 5)
                for t in range(T):
                    mine = lgt[:, t, :].rearrange("p (e a) -> p e a", a=1).to_broadcast([P, E, E])
                    other = lgt[:, t, :].rearrange("p (a e) -> p a e", a=1).to_broadcast([P, E, E])
                    nc.vector.tensor_tensor(pairs[:, t, :, :], other, mine, ALU.is_gt).then_inc(s["r"], 1)
                    nc.vector.tensor_tensor(same[:, t, :, :], other, mine, ALU.is_equal).then_inc(s["r"], 1)
                dve.wait_ge(s["r"], 5 + 2 * T)
                flat = lambda a: a[:, :, :, :].rearrange("p t e f -> p t (e f)")
                nc.vector.tensor_tensor(flat(same), flat(same), C("before").rearrange("p (a n) -> p a n", a=1).to_broadcast([P, T, E * E]),
                                        ALU.mult).then_inc(s["r"], 1)
                dve.wait_ge(s["r"], 6 + 2 * T)
                nc.vector.tensor_tensor(flat(pairs), flat(pairs), flat(same), ALU.add).then_inc(s["r"], 1)
                dve.wait_ge(s["r"], 7 + 2 * T)
                nc.vector.reduce_sum(wts[:, :, :], pairs[:, :, :, :], AX_X).then_inc(s["r"], 1)
                dve.wait_ge(s["r"], 8 + 2 * T)
                nc.vector.tensor_scalar(wts[:, :, :], wts[:, :, :], 1.5, None, ALU.is_lt).then_inc(s["r"], 1)
                dve.wait_ge(s["r"], 9 + 2 * T)
                nc.vector.tensor_tensor(wts[:, :, :], wts[:, :, :], lgt[:, :, :], ALU.mult).then_inc(s["r"], 1)
                dve.wait_ge(s["r"], 10 + 2 * T)
                nc.vector.reduce_sum(row[:, :], wts[:, :, :], AX_X).then_inc(s["r"], 1)
                dve.wait_ge(s["r"], 11 + 2 * T)
                nc.vector.reciprocal(row[:, :], row[:, :]).then_inc(s["r"], 1)
                dve.wait_ge(s["r"], 12 + 2 * T)
                nc.vector.tensor_tensor(wts[:, :, :], wts[:, :, :], row[:, :].rearrange("p (t a) -> p t a", a=1).to_broadcast([P, T, E]),
                                        ALU.mult).then_inc(s["w"], 1)
                dve.wait_ge(s["wT_ps"], 1)
                nc.vector.tensor_copy(wtT[:, :], banks[6][:, P:2 * P]).then_inc(s["wT"], 1)
                for c in range(FC):
                    dve.wait_ge(s["b2_ps"], c + 1)
                    v = xs[:, 4 * c:4 * c + 4, :]
                    nc.vector.tensor_tensor(v, v, banks[c].rearrange("p (t d) -> p t d", t=4), ALU.add).then_inc(s["x2"], 1)
                dve.wait_ge(s["x2"], FC)

                def up(e, buf, n):
                    c, ft = divmod(n, FT)
                    wait(dve, "x1ps", UP, e, n + 1)
                    wait(dve, "gl", UP, e, n + 1)
                    if ft == 0:
                        wait(dve, "yps", FC, e, c - 1)
                    nc.vector.scalar_tensor_tensor(hid[:, c % 2, ft, :], banks[3 + n % 3],
                                                   b1s[:, buf, ft:ft + 1], G[:, n % 2, :],
                                                   ALU.add, ALU.mult).then_inc(s["hd"], 1)

                def gather(e, c):
                    wait(dve, "yps", FC, e, c + 1)
                    for t in range(4):
                        wait(dve, "acc", T, e, 4 * c + t - T + 1)
                        nc.vector.scalar_tensor_tensor(xs[:, 4 * c + t, :], banks[6 + c % 2][:, t * P:(t + 1) * P],
                                                       wts[:, 4 * c + t, bass.ds(e, 1)], xs[:, 4 * c + t, :],
                                                       ALU.mult, ALU.add).then_inc(s["acc"], 1)

                dve.sem_inc(s["hd"], START["hd"])
                dve.sem_inc(s["acc"], START["acc"])
                def expert(e, buf, pair):
                    dve.wait_ge(s[f"w_in{buf}"], pair * 48 + 48)
                    for c in range(FC):
                        for ft in range(FT):
                            up(e, buf, c * FT + ft)
                            if ft == 1 and c > 0:
                                gather(e, c - 1)
                    gather(e, FC - 1)

                with dve.Fori(0, E // 2) as p:
                    expert(2 * p, 0, p)
                    expert(2 * p + 1, 1, p)

            @block.scalar
            def _(act):
                rstd_root(nc, act, s["rs"], g)
                for c in range(FC):
                    act.wait_ge(s["xt_ps"], c + 1)
                    nc.scalar.copy(xT[:, c * NS:(c + 1) * NS], banks[c]).then_inc(s["xt"], 1)
                rstd_root(nc, act, s["hrs"], g)
                act.wait_ge(s["hn"], T + 2)
                nc.scalar.activation(hg[:, :, :], hr[:, :, :], ACT.Gelu_apprx_tanh).then_inc(s["gelu"], 1)
                for c in range(2):
                    act.wait_ge(s["hT_ps"], c + 1)
                    nc.scalar.copy(hT[:, 4 * c:4 * c + 4, :], banks[4 + c].rearrange("p (t n) -> p t n", n=P)).then_inc(s["hT"], 1)
                act.wait_ge(s["r"], 2)
                nc.scalar.activation(lgt[:, :, :], lgt[:, :, :], ACT.Exp).then_inc(s["ex"], 1)

                act.sem_inc(s["gl"], START["gl"])

                def expert(e, buf, pair):
                    act.wait_ge(s[f"w_in{buf}"], pair * 48 + 48)
                    for n in range(UP):
                        wait(act, "x2ps", UP, e, n + 1)
                        wait(act, "hd", UP, e, n - 1)
                        nc.scalar.activation(G[:, n % 2, :], banks[n % 3], ACT.Gelu_apprx_tanh,
                                             bias=b1s[:, buf, FT + n % FT:FT + n % FT + 1]).then_inc(s["gl"], 1)

                with act.Fori(0, E // 2) as p:
                    expert(2 * p, 0, p)
                    expert(2 * p + 1, 1, p)

            @block.tensor
            def _(pe):
                for t in range(T):
                    pe.wait_ge(s["xn"], t + 1)
                    ins = nc.tensor.transpose(banks[t // 4][:, (t % 4) * P:(t % 4 + 1) * P], xn[:, t, :], C("ident"))
                    if t % 4 == 3:
                        ins.then_inc(s["xt_ps"], 1)
                pe.wait_ge(s["xt"], FC)
                for t in range(T):
                    ins = nc.tensor.matmul(banks[4 + t // 8][:, (t % 8) * R1:(t % 8 + 1) * R1], xT[:, t * P:(t + 1) * P],
                                           C("wr1"), start=True, stop=True)
                    if t % 8 == 7:
                        ins.then_inc(s["h_ps"], 1)
                pe.wait_ge(s["gelu"], 1)
                for t in range(T // 2):
                    ins = nc.tensor.transpose(banks[4 + t // 4][:, (t % 4) * P:(t % 4 + 1) * P],
                                              hg[:, 2 * t:2 * t + 2, :].rearrange("p t n -> p (t n)"), C("ident"))
                    if t % 4 == 3:
                        ins.then_inc(s["hT_ps"], 1)
                pe.wait_ge(s["hT"], 2)
                pe.wait_ge(s["own"], 1)
                for t in range(T):
                    z = R1 * (t % 2)
                    ins = nc.tensor.matmul(banks[6 + t % 2][:, t // 2 * E:(t // 2 + 1) * E], hT[z:z + R1, t // 2, :],
                                           wr2[z:z + R1, :], start=True, stop=True)
                    if t >= T - 2:
                        ins.then_inc(s["l_ps"], 1)
                pe.wait_ge(s["w"], 1)
                nc.tensor.transpose(banks[6][:, P:2 * P], wts[:, :, :].rearrange("p t e -> p (t e)"),
                                    C("ident")).then_inc(s["wT_ps"], 1)
                pe.wait_ge(s["wT"], 1)
                pe.wait_ge(s["own"], 2)
                for c in range(FC):
                    nc.tensor.matmul(banks[c], wtT[:, :], b2own[:, 4 * c:4 * c + 4, :].rearrange("p t d -> p (t d)"),
                                     start=True, stop=True).then_inc(s["b2_ps"], 1)
                pe.wait_ge(s["x2"], FC)

                def up(e, buf, n):
                    c, ft = divmod(n, FT)
                    for half, done, used, bank in ((1, "x2ps", "gl", n % 3), (0, "x1ps", "hd", 3 + n % 3)):
                        wait(pe, used, UP, e, n - 2)
                        nc.tensor.matmul(banks[bank], w1s[:, buf, half * F + ft * P:half * F + (ft + 1) * P],
                                         xT[:, c * NS:(c + 1) * NS], start=True, stop=True).then_inc(s[done], 1)

                def down(e, buf, c):
                    wait(pe, "hd", UP, e, FT * (c + 1))
                    wait(pe, "acc", T, e, 4 * (c - 1))
                    for t in range(4):
                        for ft in range(FT):
                            ins = nc.tensor.matmul(banks[6 + c % 2][:, t * P:(t + 1) * P],
                                                   hid[:, c % 2, ft, t * P:(t + 1) * P], w2s[:, buf, ft, :],
                                                   start=ft == 0, stop=ft == FT - 1)
                    ins.then_inc(s["yps"], 1)

                def expert(e, buf, pair):
                    pe.wait_ge(s[f"w_in{buf}"], pair * 48 + 48)
                    for c in range(FC):
                        for ft in range(FT):
                            up(e, buf, c * FT + ft)
                            if ft == 1 and c > 0:
                                down(e, buf, c - 1)
                    down(e, buf, FC - 1)

                pe.sem_inc(s["yps"], START["yps"])
                with pe.Fori(0, E // 2) as p:
                    expert(2 * p, 0, p)
                    expert(2 * p + 1, 1, p)


_NAMES = ["attn_Wq", "attn_bq", "attn_Wk", "attn_bk", "attn_Wv", "attn_bv", "attn_Wo", "attn_bo", "attn_rel_W",
          "attn_rel_b", "attn_logical_bias", "attn_gate_W", "attn_gate_b", "ffn_Wr1", "ffn_br1", "ffn_ln_scale",
          "ffn_ln_bias", "ffn_Wr2", "ffn_br2", "ffn_b1", "ffn_b2"]


def kernel(**inputs):
    import numpy as np
    import concourse.bacc as bacc
    from concourse.bass_utils import run_bass_kernel_spmd

    g = {n: np.asarray(inputs["L0_" + n]) for n in _NAMES}
    packed = np.zeros((P, CW_ALL), np.float32)

    def put(name, a):
        packed[:, AT[name]] = a

    for name, src in (("wvT", "attn_Wv"), ("woT", "attn_Wo"), ("gateT", "attn_gate_W")):
        put(name, g[src].T)
    by_row = np.arange(D).reshape(PAIRS, 2, HD).transpose(1, 2, 0).ravel()
    put("wqT", g["attn_Wq"][by_row].T)
    put("wkT", g["attn_Wk"][by_row].T)
    put("relI", g["attn_rel_W"][:, :D].T)
    put("relJ", g["attn_rel_W"][:, D:].T)
    put("bq", g["attn_bq"][by_row][:, None])
    put("bk", g["attn_bk"][by_row][:, None])
    for name, src in (("bv", "attn_bv"), ("bo", "attn_bo"), ("relb", "attn_rel_b"), ("gateb", "attn_gate_b"),
                      ("br1", "ffn_br1"), ("lns", "ffn_ln_scale"), ("lnb", "ffn_ln_bias"), ("br2", "ffn_br2")):
        put(name, g[src][None, :])
    put("bias", g["attn_logical_bias"].T.reshape(1, -1))
    put("ident", np.eye(P, dtype=np.float32))
    put("diag", np.tile(np.repeat(np.eye(IB, dtype=np.float32), 4, axis=0), (2, 1)))
    put("wr1", g["ffn_Wr1"])
    put("wr2", np.tile(g["ffn_Wr2"], (2, 1)))
    put("b2", np.tile(g["ffn_b2"], (T, 1)))
    put("own", np.repeat(np.eye(T, dtype=np.float32), E, axis=0))
    put("before", np.tri(E, E, -1, dtype=np.float32).reshape(1, -1))
    put("b1", g["ffn_b1"].reshape(E, 2 * FT, P).transpose(2, 0, 1).reshape(P, -1))

    nc = bacc.Bacc("TRN2", target_bir_lowering=False, num_devices=1)
    arrays, aps = {}, []
    for name, a in (("x", np.asarray(inputs["L0_attn_hidden_states"])[0]), ("consts", packed),
                    ("w1", np.asarray(inputs["L0_ffn_W1"])), ("w2", np.asarray(inputs["L0_ffn_W2"]))):
        arrays[name] = np.ascontiguousarray(a)
        aps.append(nc.dram_tensor(name, a.shape, F32, kind="ExternalInput").ap())
    out = nc.dram_tensor("out", (S, D), F32, kind="ExternalOutput").ap()
    build(nc, *aps, out)
    r = run_bass_kernel_spmd(nc, [arrays], core_ids=[0])
    return r.results[0]["out"].reshape(1, S, D)
```

```python
from contextlib import ExitStack

import concourse.bass as bass
from concourse import mybir

F32 = mybir.dt.float32
F16 = mybir.dt.float16
BF16 = mybir.dt.bfloat16
ALU = mybir.AluOpType
ACT = mybir.ActivationFunctionType
AX_X = mybir.AxisListType.X

P = 128
S, D = 2048, 128
H, HD = 16, 8
T = S // P
PAIRS = H // 2
SLOTS = 6
QPART = [0, 0, 1, 0, 2, 1]
KPART = [0, 1, 0, 2, 0, 1]
ROWS = 2 * SLOTS * HD
SROWS = ROWS + 2 * 3
IB = 16
BLOCKS = P // IB
CHUNKS = 2
CW = S // CHUNKS
JC = CW // P
GROUPS, GH = 4, 3
GW = GH * HD + 1
VW = HD + 1
NS = 512
MAXS = S // NS * H
PER_KEY_TILE = 5
E, F = 8, 512
FT = F // P
R1 = 64
FC = S // NS
LN_EPS, ROUTER_EPS = 1e-5, 1e-6
WSCALE = 64.0

CONST = [("wqT", D), ("wkT", D), ("wvT", D), ("woT", D), ("relI", 3), ("relJ", 3), ("gateT", H),
         ("bq", 1), ("bk", 1), ("bv", D), ("bo", D), ("relb", 3), ("gateb", H), ("bias", 3 * H),
         ("ident", P), ("diag", IB), ("wr1", R1), ("br1", R1), ("lns", R1), ("lnb", R1), ("wr2", E),
         ("br2", E), ("b2", D), ("own", T), ("before", E * E), ("b1", E * 2 * FT)]
AT, n = {}, 0
for _name, _w in CONST:
    AT[_name] = slice(n, n + _w)
    n += _w
CW_ALL = n


def build(nc, x, consts, w1, w2, out):
    q_dram = nc.dram_tensor("q_parts", [2, SLOTS, HD * PAIRS, S], BF16, kind="Internal").ap()
    a_dram = nc.dram_tensor("a_parts", [S, 4, H], F16, kind="Internal").ap()

    ctx = ExitStack()
    with ctx:
        def sb(name, shape, dt, c=ctx):
            return c.enter_context(nc.sbuf_tensor(name, shape, dt))

        def sem(name, c=ctx):
            return c.enter_context(nc.semaphore(name))

        psS = ctx.enter_context(nc.psum_tensor("psS", [P, 2, 2 * NS], F32))
        psO = ctx.enter_context(nc.psum_tensor("psO", [P, NS], F32))
        psM = ctx.enter_context(nc.psum_tensor("psM", [P, 2, NS], F32))
        psX = ctx.enter_context(nc.psum_tensor("psX", [P, NS], F32))
        banks = [psS[:, 0, 0:NS], psS[:, 0, NS:], psS[:, 1, 0:NS], psS[:, 1, NS:],
                 psO[:, :], psM[:, 0, :], psM[:, 1, :], psX[:, :]]

        cst = sb("cst", [P, CW_ALL], F32)

        def C(name):
            return cst[:, AT[name]]

        xs = sb("xs", [P, T, D], F32)
        stats = sb("stats", [P, T, 6], F32)
        mv = sb("mv", [P, T, 2], F32)
        rstd = sb("rstd", [P, T], F32)
        var = sb("var", [P, T], F32)
        newton = sb("newton", [P, T], F32)

        attention(nc, ctx, sb, sem, locals())
        experts(nc, sb, sem, locals())


def rstd_of_variance(nc, dve, done, eps, g):
    rstd, var, newton = g["rstd"][:, :], g["var"][:, :], g["newton"][:, :]
    nc.vector.tensor_scalar(var, g["mv"][:, :, 1], eps, None, ALU.add).then_inc(done, 1)
    dve.wait_ge(done, 1)
    nc.vector.reciprocal(rstd, var).then_inc(done, 1)
    dve.wait_ge(done, 3)
    nc.vector.tensor_tensor(newton, rstd, rstd, ALU.mult).then_inc(done, 1)
    dve.wait_ge(done, 4)
    nc.vector.scalar_tensor_tensor(newton, newton, -0.5, var, ALU.mult, ALU.mult).then_inc(done, 1)
    dve.wait_ge(done, 5)
    nc.vector.scalar_tensor_tensor(rstd, newton, 1.5, rstd, ALU.add, ALU.mult).then_inc(done, 1)
    dve.wait_ge(done, 6)


def rstd_root(nc, act, done, g):
    act.wait_ge(done, 2)
    nc.scalar.activation(g["rstd"][:, :], g["rstd"][:, :], ACT.Sqrt).then_inc(done, 1)


def attention(nc, outer, sb, sem, g):
    C, xs, banks = g["C"], g["xs"], g["banks"]
    psS, psO, psM, psX = g["psS"], g["psO"], g["psM"], g["psX"]
    stats, mv, rstd, cst = g["stats"], g["mv"], g["rstd"], g["cst"]
    q_dram, a_dram = g["q_dram"], g["a_dram"]
    with ExitStack() as ctx:
        kst = sb("kst", [SROWS, PAIRS, S], BF16, ctx)
        V = sb("V", [P, T, GROUPS, GW], F32, ctx)
        V1 = sb("V1", [P, T, GROUPS, VW], F32, ctx)
        beta = sb("beta", [P, 2, S], F32, ctx)
        alpha = sb("alpha", [P, T, 2], F32, ctx)
        gtop = sb("gtop", [P, T, H], F32, ctx)
        ast = sb("ast", [P, T * BLOCKS, H], F16, ctx)
        diag = sb("diag", [P, IB], F16, ctx)
        top = [sb(f"top{c}", [P, CW], F32, ctx) for c in range(CHUNKS)]
        rel = [[sb(f"rel{c}{r}", [P, CW], F32, ctx) for r in range(2)] for c in range(CHUNKS)]
        qnext = sb("qnext", [SROWS, PAIRS, 2, P], BF16, ctx)
        q_in = sem("q_in", ctx)
        anow = sb("anow", [P, 2], F32, ctx)
        lg = [sem(f"lg{c}", ctx) for c in range(CHUNKS)]
        al = sem("al", ctx)
        a_in = sem("a_in", ctx)
        prepare(nc, sb, sem, {**g, **locals()})
        attend(nc, sb, sem, {**g, **locals()})


def fetch_q(sp, g, t):
    for z in range(2):
        src = g["q_dram"][z, :, :, :].rearrange("n (d a) s -> (n d) a s", a=PAIRS)
        sp.dma_start(g["qnext"][z * SLOTS * HD:(z + 1) * SLOTS * HD, :, z, :],
                     src[:, :, bass.ds(t * P, P)]).then_inc(g["q_in"], 16)


def largest_logit(nc, g, t, c, r):
    top, b, a = g["top"][c][:, :], g["beta"][:, r, c * CW:(c + 1) * CW], g["alpha"][:, bass.ds(t, 1), r]
    if r == 1:
        return nc.vector.tensor_scalar(top, b, a, 0.0, ALU.add, ALU.max)
    return nc.vector.scalar_tensor_tensor(top, b, a, top, ALU.add, ALU.max)


def current_alpha(nc, g, t):
    return nc.vector.tensor_copy(g["anow"][:, :], g["alpha"][:, bass.ds(t, 1), :].rearrange("p a r -> p (a r)"))


def prepare(nc, sb, sem, g):
    C, xs, banks, x = g["C"], g["xs"], g["banks"], g["x"]
    stats, mv, rstd, cst, consts = g["stats"], g["mv"], g["rstd"], g["cst"], g["consts"]
    q_dram, a_dram = g["q_dram"], g["a_dram"]
    kst, V, V1, beta, alpha, gtop, ast, diag, a_in = (g[n] for n in ("kst", "V", "V1", "beta", "alpha", "gtop",
                                                                     "ast", "diag", "a_in"))
    with ExitStack() as ctx:
        xn = sb("xn", [P, T, D], F32, ctx)
        xT = sb("xT", [P, S], F32, ctx)
        proj = sb("proj", [P, 2, S], F32, ctx)
        rest = sb("rest", [P, 2, S], F32, ctx)
        bqs = sb("bqs", [P, 1], F32, ctx)
        parts = sb("parts", [P, 2, 3, S], BF16, ctx)
        ones = sb("ones", [P, P], F32, ctx)
        dJ = sb("dJ", [P, 2], F32, ctx)
        dJb = sb("dJb", [P, 2, P], F32, ctx)
        wnat = sb("wnat", [P, 2 + H], F32, ctx)
        drb = sb("drb", [P, 2], F32, ctx)
        dL = sb("dL", [P, 3, H], F32, ctx)
        gate = sb("gate", [P, T, H], F32, ctx)
        gated = sb("gated", [P, T, 2, H], F32, ctx)
        gparts = sb("gparts", [P, T, 4, H], F16, ctx)

        names = ["load", "loadx0", "loadx1", "loadx2", "loadx3", "kone", "v_ones", "dv", "rs", "xn_ready", "xt_ps",
                 "xt_ready", "w_ready", "mm_q", "mm_k", "mm_v", "mm_b", "mm_n", "q_evac", "k_evac", "q_rest",
                 "k_rest", "q_parts", "k_parts", "a_parts", "gsum", "gexp", "v_copied", "b_copied", "q_out",
                 "a_out", "k_in", "k_ones", "zero_q"]
        s = {n: sem("p_" + n, ctx) for n in names}
        QSCALE = float(HD) ** -0.5
        with nc.Block() as block:

            @block.sync
            def _(sp):
                xv = x.rearrange("(t p) d -> p t d", p=P)
                for c in range(FC):
                    sp.dma_start(xs[:, 4 * c:4 * c + 4, :], xv[:, 4 * c:4 * c + 4, :]).then_inc(s[f"loadx{c}"], 16)
                sp.wait_ge(s["kone"], 1)
                sp.dma_start(kst[ROWS:SROWS, 1:PAIRS, :],
                             kst[ROWS:SROWS, 0:1, :].to_broadcast([SROWS - ROWS, PAIRS - 1, S])).then_inc(s["k_ones"], 16)
                for part in range(3):
                    sp.wait_ge(s["k_parts"], part + 1)
                    for n in range(SLOTS):
                        if KPART[n] == part:
                            for z in range(2):
                                sp.dma_start(kst[(z * SLOTS + n) * HD:(z * SLOTS + n + 1) * HD, :, :],
                                             parts[z * (P // 2):(z + 1) * (P // 2), 1, part, :]).then_inc(s["k_in"], 16)
                    sp.wait_ge(s["q_parts"], part + 1)
                    for n in range(SLOTS):
                        if QPART[n] == part:
                            sp.dma_start(q_dram[:, n, :, :], parts[:, 0, part, :]).then_inc(s["q_out"], 16)
                sp.wait_ge(s["a_parts"], 2)
                sp.dma_start(a_dram.rearrange("(t p) a h -> p t (a h)", p=P),
                             gparts[:, :, :, :].rearrange("p t a h -> p t (a h)")).then_inc(s["a_out"], 16)
                sp.wait_ge(s["q_out"], 16 * SLOTS)
                sp.wait_ge(s["zero_q"], 1)
                fetch_q(sp, g, 0)
                sp.wait_ge(s["k_in"], 16 * 2 * SLOTS)
                sp.wait_ge(s["k_ones"], 16)
                sp.wait_ge(s["a_out"], 16)

            @block.gpsimd
            def _(pool):
                nc.gpsimd.memset(kst[ROWS:SROWS, 0, :], 1.0).then_inc(s["kone"], 1)
                pool.wait_ge(s["kone"], 1)
                nc.gpsimd.memset(V[:, :, :, GW - 1:GW], 1.0).then_inc(s["v_ones"], 1)
                pool.wait_ge(s["v_ones"], 1)
                nc.gpsimd.memset(V1[:, :, :, HD:VW], 1.0).then_inc(s["v_ones"], 1)
                nc.gpsimd.memset(g["qnext"][:, :, :, :], 0.0).then_inc(s["zero_q"], 1)
                pool.wait_ge(s["q_parts"], 1)
                nc.gpsimd.tensor_tensor(rest[:, 0, :], proj[:, 0, :], parts[:, 0, 0, :],
                                        ALU.subtract).then_inc(s["q_rest"], 1)
                pool.wait_ge(s["q_parts"], 2)
                nc.gpsimd.tensor_tensor(parts[:, 0, 2, :], rest[:, 0, :], parts[:, 0, 1, :],
                                        ALU.subtract).then_inc(s["q_parts"], 1)

            @block.vector
            def _(dve):
                for t in range(T):
                    if t % 4 == 0:
                        dve.wait_ge(s[f"loadx{t // 4}"], 16)
                    nc.vector.bn_stats(stats[:, t, :], xs[:, t, :]).then_inc(s["dv"], 1)
                for t in range(T):
                    dve.wait_ge(s["dv"], t + 1)
                    nc.vector.bn_aggr(mv[:, t, :], stats[:, t, :]).then_inc(s["dv"], 1)
                dve.wait_ge(s["load"], 16)
                L = C("bias").rearrange("p (r h) -> p r h", h=H)
                nc.vector.tensor_tensor(dL[:, 2, :], L[:, 0, :], L[:, 1, :], ALU.max).then_inc(s["w_ready"], 1)
                dve.wait_ge(s["w_ready"], 1)
                nc.vector.tensor_tensor(dL[:, 2, :], dL[:, 2, :], L[:, 2, :], ALU.max).then_inc(s["w_ready"], 1)
                dve.wait_ge(s["w_ready"], 2)
                nc.vector.tensor_tensor(dL[:, 2, :], dL[:, 2, :], L[:, 2, :], ALU.subtract).then_inc(s["w_ready"], 1)
                for r in range(2):
                    nc.vector.tensor_tensor(dL[:, r, :], L[:, 2, :], L[:, r, :], ALU.subtract).then_inc(s["w_ready"], 1)
                nc.vector.tensor_tensor(drb[:, :], C("relb")[:, 0:2], C("relb")[:, 2:3].to_broadcast([P, 2]),
                                        ALU.subtract).then_inc(s["w_ready"], 1)
                nc.vector.tensor_tensor(wnat[:, 0:2], C("relI")[:, 0:2], C("relI")[:, 2:3].to_broadcast([P, 2]),
                                        ALU.subtract).then_inc(s["w_ready"], 1)
                nc.vector.tensor_copy(wnat[:, 2:2 + H], C("gateT")).then_inc(s["w_ready"], 1)
                nc.vector.tensor_copy(diag[:, :], C("diag")).then_inc(s["w_ready"], 1)
                nc.vector.memset(ones[:, :], 1.0).then_inc(s["w_ready"], 1)
                nc.vector.tensor_tensor(dJ[:, :], C("relJ")[:, 0:2], C("relJ")[:, 2:3].to_broadcast([P, 2]),
                                        ALU.subtract).then_inc(s["w_ready"], 1)
                dve.wait_ge(s["w_ready"], 11)
                for r in range(2):
                    nc.vector.tensor_scalar(dJb[:, r, :], ones[:, :], dJ[:, r:r + 1], None,
                                            ALU.mult).then_inc(s["w_ready"], 1)
                nc.vector.tensor_scalar(bqs[:, :], C("bq"), QSCALE, None, ALU.mult).then_inc(s["w_ready"], 1)
                dve.wait_ge(s["dv"], 2 * T)
                rstd_of_variance(nc, dve, s["rs"], LN_EPS, g)
                for t in range(T):
                    nc.vector.tensor_scalar(xn[:, t, :], xs[:, t, :], mv[:, t, 0:1], rstd[:, t:t + 1],
                                            ALU.subtract, ALU.mult).then_inc(s["xn_ready"], 1)
                for c in range(FC):
                    dve.wait_ge(s["mm_k"], c + 1)
                    nc.vector.tensor_scalar(proj[:, 1, c * NS:(c + 1) * NS], banks[4 + c], C("bk"), None,
                                            ALU.add).then_inc(s["k_evac"], 1)
                dve.wait_ge(s["k_evac"], FC)
                nc.vector.tensor_copy(parts[:, 1, 0, :], proj[:, 1, :]).then_inc(s["k_parts"], 1)
                dve.wait_ge(s["k_parts"], 1)
                nc.vector.tensor_tensor(rest[:, 1, :], proj[:, 1, :], parts[:, 1, 0, :],
                                        ALU.subtract).then_inc(s["k_rest"], 1)
                dve.wait_ge(s["k_rest"], 1)
                nc.vector.tensor_copy(parts[:, 1, 1, :], rest[:, 1, :]).then_inc(s["k_parts"], 1)
                dve.wait_ge(s["k_parts"], 2)
                nc.vector.tensor_tensor(parts[:, 1, 2, :], rest[:, 1, :], parts[:, 1, 1, :],
                                        ALU.subtract).then_inc(s["k_parts"], 1)
                dve.wait_ge(s["mm_n"], 1)
                dve.wait_ge(s["w_ready"], 13)
                nat = banks[4][:, 0:T * (2 + H)].rearrange("p (t n) -> p t n", t=T)
                nc.vector.tensor_tensor(alpha[:, :, :], nat[:, :, 0:2],
                                        drb[:, :].rearrange("p (a n) -> p a n", a=1).to_broadcast([P, T, 2]),
                                        ALU.add).then_inc(s["gsum"], 1)
                nc.vector.tensor_tensor(gate[:, :, :], nat[:, :, 2:2 + H],
                                        C("gateb").rearrange("p (a n) -> p a n", a=1).to_broadcast([P, T, H]),
                                        ALU.add).then_inc(s["gsum"], 1)
                for c in range(4):
                    dve.wait_ge(s["mm_v"], c + 1)
                    src = banks[(5, 6, 7, 4)[c]].rearrange("p (t n) -> p t n", t=4)
                    split = GROUPS * GH * HD
                    for t in range(4):
                        for dst, cols, w in ((V[:, 4 * c + t, :, 0:GW - 1], slice(0, split), GH * HD),
                                             (V1[:, 4 * c + t, :, 0:HD], slice(split, D), HD)):
                            nc.vector.tensor_tensor(dst, src[:, t, cols].rearrange("p (g n) -> p g n", n=w),
                                                    C("bv")[:, cols].rearrange("p (g n) -> p g n", n=w),
                                                    ALU.add).then_inc(s["v_copied"], 1)
                dve.wait_ge(s["gexp"], 1)
                nc.vector.tensor_scalar(gate[:, :, :], gate[:, :, :], 1.0, None, ALU.add).then_inc(s["gsum"], 1)
                dve.wait_ge(s["gsum"], 3)
                nc.vector.reciprocal(gate[:, :, :], gate[:, :, :]).then_inc(s["gsum"], 1)
                dve.wait_ge(s["gsum"], 4)
                for r in range(3):
                    dst = gated[:, :, r, :] if r < 2 else gtop[:, :, :]
                    nc.vector.tensor_tensor(dst, gate[:, :, :], dL[:, r:r + 1, :].to_broadcast([P, T, H]),
                                            ALU.mult).then_inc(s["gsum"], 1)
                dve.wait_ge(s["gsum"], 7)
                nc.vector.tensor_copy(gparts[:, :, 0:2, :], gated[:, :, :, :]).then_inc(s["a_parts"], 1)
                dve.wait_ge(s["a_parts"], 1)
                nc.vector.tensor_tensor(gparts[:, :, 2:4, :], gated[:, :, :, :], gparts[:, :, 0:2, :],
                                        ALU.subtract).then_inc(s["a_parts"], 1)
                dve.wait_ge(s["b_copied"], 2 * FC)
                current_alpha(nc, g, 0).then_inc(g["al"], 1)
                for c in range(CHUNKS):
                    largest_logit(nc, g, 0, c, 1).then_inc(g["lg"][c], 1)
                    dve.wait_ge(g["lg"][c], 1)
                    largest_logit(nc, g, 0, c, 0).then_inc(g["lg"][c], 1)

            @block.scalar
            def _(act):
                act.dma_start(cst[:, :], consts).then_inc(s["load"], 16)
                rstd_root(nc, act, s["rs"], g)
                for c in range(FC):
                    act.wait_ge(s["xt_ps"], c + 1)
                    nc.scalar.copy(xT[:, c * NS:(c + 1) * NS], banks[c]).then_inc(s["xt_ready"], 1)
                act.wait_ge(s["w_ready"], 14)
                for c in range(FC):
                    act.wait_ge(s["mm_q"], c + 1)
                    nc.scalar.activation(proj[:, 0, c * NS:(c + 1) * NS], banks[c], ACT.Identity,
                                         bias=bqs[:, 0:1], scale=QSCALE).then_inc(s["q_evac"], 1)
                act.wait_ge(s["q_evac"], FC)
                nc.scalar.copy(parts[:, 0, 0, :], proj[:, 0, :]).then_inc(s["q_parts"], 1)
                for r in range(2):
                    for c in range(FC):
                        n = r * FC + c
                        act.wait_ge(s["mm_b"], n + 1)
                        nc.scalar.copy(beta[:, r, c * NS:(c + 1) * NS], banks[1 + n % 3]).then_inc(s["b_copied"], 1)
                        if n == 2:
                            act.wait_ge(s["gsum"], 2)
                            nc.scalar.activation(gate[:, :, :], gate[:, :, :], ACT.Exp,
                                                 scale=-1.0).then_inc(s["gexp"], 1)
                        if n == 5:
                            act.wait_ge(s["q_rest"], 1)
                            nc.scalar.copy(parts[:, 0, 1, :], rest[:, 0, :]).then_inc(s["q_parts"], 1)

            @block.tensor
            def _(pe):
                pe.wait_ge(s["load"], 16)
                for t in range(T):
                    pe.wait_ge(s["xn_ready"], t + 1)
                    ins = nc.tensor.transpose(banks[t // 4][:, (t % 4) * P:(t % 4 + 1) * P], xn[:, t, :], C("ident"))
                    if t % 4 == 3:
                        ins.then_inc(s["xt_ps"], 1)
                pe.wait_ge(s["xt_ready"], FC)
                for w, mm, first in (("wkT", "mm_k", 4), ("wqT", "mm_q", 0)):
                    for c in range(FC):
                        nc.tensor.matmul(banks[first + c], C(w), xT[:, c * NS:(c + 1) * NS],
                                         start=True, stop=True).then_inc(s[mm], 1)
                pe.wait_ge(s["w_ready"], 13)
                pe.wait_ge(s["k_evac"], FC)
                for t in range(T):
                    ins = nc.tensor.matmul(banks[4][:, t * (2 + H):(t + 1) * (2 + H)], xT[:, t * P:(t + 1) * P],
                                           wnat[:, :], start=True, stop=True)
                ins.then_inc(s["mm_n"], 1)
                def project_v(c):
                    for t in range(4):
                        ins = nc.tensor.matmul(banks[(5, 6, 7, 4)[c]][:, t * P:(t + 1) * P],
                                               xT[:, (4 * c + t) * P:(4 * c + t + 1) * P], C("wvT"), start=True, stop=True)
                    ins.then_inc(s["mm_v"], 1)

                for c in range(3):
                    project_v(c)
                pe.wait_ge(s["q_evac"], FC)
                for r in range(2):
                    for c in range(FC):
                        n = r * FC + c
                        if n >= 3:
                            pe.wait_ge(s["b_copied"], n - 2)
                        if n == 3:
                            pe.wait_ge(s["gsum"], 2)
                            project_v(3)
                        nc.tensor.matmul(banks[1 + n % 3], dJb[:, r, :], xT[:, c * NS:(c + 1) * NS],
                                         start=True, stop=True).then_inc(s["mm_b"], 1)


def attend(nc, sb, sem, g):
    C, xs, stats, mv = g["C"], g["xs"], g["stats"], g["mv"]
    psS, psO, psM, psX = g["psS"], g["psO"], g["psM"], g["psX"]
    kst, V, V1, beta, alpha, gtop, ast, diag, a_in = (g[n] for n in ("kst", "V", "V1", "beta", "alpha", "gtop",
                                                                     "ast", "diag", "a_in"))
    top, rel, anow, qnext = g["top"], g["rel"], g["anow"], g["qnext"]
    with ExitStack() as ctx:
        qcur = sb("qcur", [SROWS, PAIRS, 2, P], BF16, ctx)
        anext = sb("anext", [P, BLOCKS * H, IB], F16, ctx)
        acur = sb("acur", [P, BLOCKS * H, IB], F16, ctx)
        pst = sb("pst", [P, CHUNKS, BLOCKS, CW], F16, ctx)
        pp = sb("pp", [P, CHUNKS, 4, CW], F16, ctx)
        low = [sb(f"low{c}", [P, CW], F32, ctx) for c in range(CHUNKS)]
        tot = [sb(f"tot{c}", [P, CW], F32, ctx) for c in range(CHUNKS)]
        ET = sb("ET", [P, 2, H, P], F32, ctx)
        mx = sb("mx", [P, H, S // NS], F32, ctx)
        mrow = sb("mrow", [P, H], F32, ctx)
        sh = sb("sh", [P, P], F32, ctx)
        shh = sb("shh", [P, 2, H], BF16, ctx)
        shT = sb("shT", [2 * 3 * PAIRS, P], BF16, ctx)
        osb = sb("osb", [P, NS], F32, ctx)
        den = sb("den", [P, GH + 1, GROUPS], F32, ctx)
        att = sb("att", [P, H, HD], F32, ctx)
        attT = sb("attT", [P, P], F32, ctx)

        names = ["zero_sh", "zero_o", "sh_in", "st_in0", "st_in1", "scores", "exps", "av", "cur", "anext", "mxs",
                 "mxused", "ls0", "ls1", "ex0", "ex1", "sm0", "sm1", "ln0", "ln1", "nt0", "nt1",
                 "rc0", "rc1", "pr0", "pr1", "hi0", "hi1", "pd0", "pd1", "sh", "shps", "shT",
                 "o_sb", "o_ps", "den", "att", "aT_ps", "aT", "y_ps", "y", "st", "bo"]
        s = {n: sem("a_" + n, ctx) for n in names}
        s["lg0"], s["lg1"], s["al"], s["q_in"] = *g["lg"], g["al"], g["q_in"]

        shv = sh[:, 0:2 * 3 * PAIRS].rearrange("p (z a n) -> p z a n", z=2, a=3)

        def by_pair(ap):
            return ap.rearrange("p (n z) -> p z n", z=2)

        def wait(eng, name, per, tile, more):
            if isinstance(tile, int) and per * tile + more <= 0:
                return
            eng.wait_ge(s[name], tile * per + more)

        with nc.Block() as block:

            @block.sync
            def _(sp):
                def load_stack(t, c):
                    wait(sp, f"pd{c}", 2, t, 2)
                    wait(sp, "scores", 2 * T, t, -2 * T + 2 * JC * (c + 1))
                    for b in range(BLOCKS):
                        for z in range(2):
                            sp.dma_start(pst[z * (P // 2):(z + 1) * (P // 2), c, b, :],
                                         pp[b * IB:(b + 1) * IB, c, :, :]).then_inc(s[f"st_in{c}"], 16)

                def load_q(t):
                    wait(sp, "cur", 4, t, 0)
                    fetch_q(sp, g, t)

                def load_shift(t):
                    wait(sp, "shT", 1, t, 1)
                    for z in range(2):
                        sp.dma_start(qnext[ROWS + 3 * z:ROWS + 3 * z + 3, :, z, :],
                                     shT[z * 3 * PAIRS:(z + 1) * 3 * PAIRS, :]).then_inc(s["sh_in"], 16)

                def tile(t, last):
                    load_stack(t, 0)
                    load_shift(t)
                    if not last:
                        load_q(t + 1)
                    load_stack(t, 1)

                for n in range(8):
                    part = (n % 4) // 2 + 2 * (n // 4)
                    first = n // 4 * (P // 2)
                    src = g["a_dram"][:, part, :].rearrange("(b i) h -> i b h", i=IB)
                    sp.dma_start(ast[first + n % 4:first + P // 2:4, :, :], src).then_inc(a_in, 16)
                tile(0, False)
                with sp.Fori(1, T - 1) as t:
                    tile(t, False)
                tile(T - 1, True)

            @block.gpsimd
            def _(pool):
                nc.gpsimd.memset(sh[:, :], 0.0).then_inc(s["zero_sh"], 1)

                def less_largest(t, c):
                    wait(pool, f"lg{c}", 2, t, 2)
                    wait(pool, f"pd{c}", 2, t, 0)
                    for r, l in enumerate(rel[c]):
                        nc.gpsimd.tensor_tensor(l[:, :], beta[:, r, c * CW:(c + 1) * CW], top[c][:, :],
                                                ALU.subtract).then_inc(s[f"ls{c}"], 1)

                def total(t, c):
                    wait(pool, f"ex{c}", 3, t, 2)
                    wait(pool, f"rc{c}", 1, t, 0)
                    nc.gpsimd.tensor_tensor(tot[c][:, :], rel[c][0][:, :], rel[c][1][:, :], ALU.add).then_inc(s[f"sm{c}"], 1)
                    wait(pool, f"ex{c}", 3, t, 3)
                    wait(pool, f"sm{c}", 2, t, 1)
                    nc.gpsimd.tensor_tensor(tot[c][:, :], tot[c][:, :], low[c][:, :], ALU.add).then_inc(s[f"sm{c}"], 1)

                def check(t, c):
                    wait(pool, f"ln{c}", 2, t, 2)
                    nc.gpsimd.tensor_tensor(top[c][:, :], tot[c][:, :], low[c][:, :], ALU.mult).then_inc(s[f"nt{c}"], 1)

                def products(t, c):
                    wait(pool, f"rc{c}", 1, t, 1)
                    for l in rel[c]:
                        nc.gpsimd.tensor_tensor(l[:, :], l[:, :], top[c][:, :], ALU.mult).then_inc(s[f"pr{c}"], 1)

                def lows(t, c):
                    for r, l in enumerate(rel[c]):
                        wait(pool, f"hi{c}", 2, t, r + 1)
                        nc.gpsimd.tensor_tensor(pp[:, c, 2 * r + 1, :], l[:, :], pp[:, c, 2 * r, :],
                                                ALU.subtract).then_inc(s[f"pd{c}"], 1)

                def diagonal(t):
                    wait(pool, "cur", 4, t, 0)
                    nc.gpsimd.tensor_tensor(
                        anext[:, :, :],
                        ast[:, bass.ds(t * BLOCKS, BLOCKS), :].rearrange("p b (h a) -> p (b h) a", a=1)
                        .to_broadcast([P, BLOCKS * H, IB]),
                        diag[:, :].rearrange("p (a i) -> p a i", a=1).to_broadcast([P, BLOCKS * H, IB]),
                        ALU.mult).then_inc(s["anext"], 1)

                def ahead(t, first=False):
                    less_largest(t, 0)
                    if not first:
                        diagonal(t)
                    less_largest(t, 1)
                    total(t, 0)
                    check(t, 0)
                    total(t, 1)
                    products(t, 0)
                    lows(t, 0)
                    check(t, 1)
                    products(t, 1)
                    lows(t, 1)

                ahead(0, first=True)
                pool.wait_ge(a_in, 16 * 8)
                diagonal(0)
                nc.gpsimd.tensor_tensor(xs[:, :, :], xs[:, :, :],
                                        C("bo").rearrange("p (a d) -> p a d", a=1).to_broadcast([P, T, D]),
                                        ALU.add).then_inc(s["bo"], 1)
                with pool.Fori(0, T - 1) as t:
                    ahead(t + 1)

            @block.scalar
            def _(act):
                def exps(t, j, u):
                    wait(act, "scores", 2 * T, t, 2 * j + u + 1)
                    if u == 0:
                        wait(act, "av", T, t, j - 1)
                    nc.scalar.activation(
                        ET[:, j % 2, 8 * u:8 * u + 8, :].rearrange("p h (v i) -> p v h i", v=2),
                        psS[:, u, :].rearrange("p (v h i) -> p v h i", v=2, h=8),
                        ACT.Exp).then_inc(s["exps"], 1)

                def rel_exps(t, c, n):
                    if n == 2:
                        wait(act, f"lg{c}", 2, t, 2)
                        wait(act, f"rc{c}", 1, t, 0)
                        ins = nc.scalar.activation(low[c][:, :], top[c][:, :], ACT.Exp, scale=-1.0)
                    else:
                        wait(act, f"ls{c}", 2, t, n + 1)
                        wait(act, "al", 1, t, 1)
                        ins = nc.scalar.activation(rel[c][n][:, :], rel[c][n][:, :], ACT.Exp, bias=anow[:, n:n + 1])
                    ins.then_inc(s[f"ex{c}"], 1)

                def rough_reciprocal(t, c, n):
                    if n == 0:
                        wait(act, f"sm{c}", 2, t, 2)
                        nc.scalar.activation(low[c][:, :], tot[c][:, :], ACT.Ln).then_inc(s[f"ln{c}"], 1)
                    else:
                        wait(act, f"ln{c}", 2, t, 1)
                        nc.scalar.activation(low[c][:, :], low[c][:, :], ACT.Exp, scale=-1.0).then_inc(s[f"ln{c}"], 1)

                def high(t, c, r):
                    wait(act, f"pr{c}", 2, t, r + 1)
                    wait(act, f"st_in{c}", 32 * BLOCKS, t, 0)
                    nc.scalar.copy(pp[:, c, 2 * r, :], rel[c][r][:, :]).then_inc(s[f"hi{c}"], 1)

                def copy_outputs(t):
                    wait(act, "av", T, t, T)
                    wait(act, "o_ps", 1, t, 0)
                    nc.scalar.copy(osb[:, :], psO[:, :]).then_inc(s["o_sb"], 1)

                def copy_transposed(t):
                    wait(act, "aT_ps", 1, t, 1)
                    nc.scalar.copy(attT[:, :], psX[:, 0:P]).then_inc(s["aT"], 1)

                beside = {(2, 0): (rel_exps, 0, 0), (3, 0): (rel_exps, 0, 1), (3, 1): (rel_exps, 0, 2),
                          (5, 0): (rough_reciprocal, 0, 0), (5, 1): (rough_reciprocal, 0, 1),
                          (6, 0): (rel_exps, 1, 0), (7, 0): (rel_exps, 1, 1), (7, 1): (rel_exps, 1, 2),
                          (9, 0): (high, 0, 0), (9, 1): (high, 0, 1),
                          (10, 0): (rough_reciprocal, 1, 0), (10, 1): (rough_reciprocal, 1, 1),
                          (12, 1): (high, 1, 0), (13, 0): (high, 1, 1)}

                def tile(t, first, last):
                    for j in range(T):
                        for u in range(2):
                            exps(t, j, u)
                            if not first and (j, u) == (1, 0):
                                copy_outputs(t - 1)
                            if not last and (j, u) in beside:
                                step, c, n = beside[j, u]
                                step(t + 1, c, n)
                        if not first and j == 5:
                            copy_transposed(t - 1)

                act.preload_act_table_set("natural_log_exp_and_others")
                for c in range(CHUNKS):
                    for n in range(3):
                        rel_exps(0, c, n)
                    for n in range(2):
                        rough_reciprocal(0, c, n)
                for c in range(CHUNKS):
                    for r in range(2):
                        high(0, c, r)
                tile(0, True, False)
                with act.Fori(1, T - 1) as t:
                    tile(t, False, False)
                tile(T - 1, False, True)
                copy_outputs(T - 1)
                copy_transposed(T - 1)

            @block.vector
            def _(dve):
                nc.vector.memset(psO[:, :], 0.0).then_inc(s["zero_o"], 1)

                def logits_top(t, c, r):
                    if r == 1:
                        wait(dve, f"pr{c}", 2, t, 0)
                    else:
                        wait(dve, f"lg{c}", 2, t, 1)
                    largest_logit(nc, g, t, c, r).then_inc(s[f"lg{c}"], 1)

                def take_alpha(t):
                    for c in range(CHUNKS):
                        wait(dve, f"ex{c}", 3, t, -1)
                    current_alpha(nc, g, t).then_inc(s["al"], 1)

                def newton(t, c):
                    wait(dve, f"nt{c}", 1, t, 1)
                    nc.vector.scalar_tensor_tensor(top[c][:, :], top[c][:, :], -2.0, low[c][:, :], ALU.add,
                                                   ALU.mult).then_inc(s[f"rc{c}"], 1)

                def maxima(t, lo, hi):
                    for m in range(lo, hi):
                        wait(dve, "mxs", MAXS, t, m + 1)
                        h, c = divmod(m, S // NS)
                        nc.vector.reduce_max(mx[:, h, c:c + 1], psM[:, m % 2, :], AX_X).then_inc(s["mxused"], 1)

                def shift(t):
                    wait(dve, "mxused", MAXS, t, MAXS)
                    wait(dve, "shps", 1, t, 0)
                    nc.vector.reduce_max(mrow[:, :], mx[:, :, :], AX_X).then_inc(s["sh"], 1)
                    wait(dve, "sh", 6, t, 1)
                    nc.vector.scalar_tensor_tensor(
                        shv[:, :, 0, :], by_pair(mrow[:, :]), -1.0,
                        gtop[:, bass.ds(t, 1), :].rearrange("p a (n z) -> p z (a n)", z=2),
                        ALU.mult, ALU.subtract).then_inc(s["sh"], 1)
                    wait(dve, "sh", 6, t, 2)
                    hv = [shh[:, n, :].rearrange("p (z n) -> p z n", z=2) for n in range(2)]
                    for n in range(2):
                        nc.vector.tensor_copy(hv[n], shv[:, :, n, :]).then_inc(s["sh"], 1)
                        wait(dve, "sh", 6, t, 3 + 2 * n)
                        nc.vector.tensor_tensor(shv[:, :, n + 1, :], shv[:, :, n, :], hv[n],
                                                ALU.subtract).then_inc(s["sh"], 1)
                        if n == 0:
                            wait(dve, "sh", 6, t, 4)

                def shift_rows(t):
                    wait(dve, "shps", 1, t, 1)
                    wait(dve, "sh_in", 32, t, 0)
                    nc.vector.tensor_copy(shT[:, :], psX[0:2 * 3 * PAIRS, 0:P]).then_inc(s["shT"], 1)

                def to_current(t):
                    wait(dve, "q_in", 32, t, 32)
                    wait(dve, "sh_in", 32, t, 32)
                    wait(dve, "anext", 1, t, 1)
                    for u in range(2):
                        wait(dve, "scores", 2 * T, t, u - 1)
                        nc.vector.tensor_copy(qcur[:, 4 * u:4 * u + 4, :, :],
                                              qnext[:, 4 * u:4 * u + 4, :, :]).then_inc(s["cur"], 1)
                        ac, an = (m[:, :, :].rearrange("p (b h) i -> p b (h i)", h=H)[:, :, u * P:(u + 1) * P]
                                  for m in (acur, anext))
                        nc.vector.tensor_copy(ac, an).then_inc(s["cur"], 1)

                def normalize(t):
                    v = psX[:, :].rearrange("p (k r w) -> p k r w", k=GH + 1, w=32)
                    heads = [att[:, 0:GROUPS * GH, :].rearrange("p (r k) d -> p k r d", k=GH)[:, k] for k in range(GH)]
                    heads.append(att[:, GROUPS * GH:H, :])
                    wait(dve, "o_ps", 1, t, 1)
                    wait(dve, "aT_ps", 1, t, 0)
                    nc.vector.reciprocal(den[:, 0:GH, :], v[:, 0:GH, :, GW - 1]).then_inc(s["den"], 1)
                    nc.vector.reciprocal(den[:, GH, :], v[:, GH, :, HD]).then_inc(s["den"], 1)
                    wait(dve, "den", 2, t, 2)
                    for k in range(GH + 1):
                        first = k * HD if k < GH else 0
                        nc.vector.tensor_tensor(heads[k], v[:, k, :, first:first + HD],
                                                den[:, k, :].rearrange("p (r a) -> p r a", a=1)
                                                .to_broadcast([P, GROUPS, HD]), ALU.mult).then_inc(s["att"], 1)

                def residual(t):
                    wait(dve, "y_ps", 1, t, 1)
                    dve.wait_ge(s["bo"], 1)
                    nc.vector.tensor_tensor(xs[:, bass.ds(t, 1), :], xs[:, bass.ds(t, 1), :],
                                            psX[:, P:2 * P].rearrange("p (a d) -> p a d", a=1),
                                            ALU.add).then_inc(s["y"], 1)
                    wait(dve, "y", 1, t, 1)
                    nc.vector.bn_stats(stats[:, bass.ds(t, 1), :].rearrange("p a n -> p (a n)"),
                                       xs[:, bass.ds(t, 1), :].rearrange("p a d -> p (a d)")).then_inc(s["st"], 1)

                beside = {(0, 0): ((take_alpha,), (logits_top, 0, 1), (logits_top, 0, 0)), (1, 4): ((logits_top, 1, 1),),
                          (2, 3): ((logits_top, 1, 0),), (7, 4): ((newton, 0),), (11, 4): ((newton, 1),)}

                def tile(t, first, last):
                    for j in range(T):
                        if not last:
                            for n in range(PER_KEY_TILE + 1):
                                for step, *which in beside.get((j, n), ()):
                                    step(t + 1, *which)
                                m = PER_KEY_TILE * (j - 1) + n
                                if j > 0 and n < PER_KEY_TILE and m < MAXS:
                                    maxima(t + 1, m, m + 1)
                        if not last and j == 13:
                            shift(t + 1)
                        if not last and j == 14:
                            shift_rows(t + 1)
                        if not first:
                            if j == 3:
                                normalize(t - 1)
                            if j == 7:
                                residual(t - 1)
                    if not last:
                        to_current(t + 1)

                maxima(0, 0, 20)
                newton(0, 0)
                maxima(0, 20, 40)
                newton(0, 1)
                maxima(0, 40, MAXS)
                dve.wait_ge(s["zero_sh"], 1)
                shift(0)
                shift_rows(0)
                to_current(0)
                tile(0, True, False)
                with dve.Fori(1, T - 1) as t:
                    tile(t, False, False)
                tile(T - 1, False, True)
                normalize(T - 1)
                residual(T - 1)

            @block.tensor
            def _(pe):
                def scores(t, j, u, v):
                    c, jj = divmod(j, JC)
                    if j == 0 and v == 0:
                        wait(pe, "cur", 4, t, 2 * u + 2)
                    if v == 0:
                        wait(pe, "exps", 2 * T, t, 2 * j + u - 1)
                    out = psS[:, u, v * NS:(v + 1) * NS]
                    for n in range(4):
                        a = 4 * u + n
                        nc.tensor.matmul(out[:, n * P:(n + 1) * P], kst[:, a, j * P:(j + 1) * P],
                                         qcur[:, a, :, v * 64:(v + 1) * 64], start=n == 0, stop=False,
                                         skip_group_check=True)
                    for n in range(4):
                        b = 4 * v + n
                        ins = nc.tensor.matmul(
                            out.rearrange("p (h i) -> p h i", h=8)[:, :, n * IB:(n + 1) * IB],
                            pst[:, c, b, jj * P:(jj + 1) * P],
                            acur[:, b * H + 8 * u:b * H + 8 * u + 8, :], start=False, stop=n == 3,
                            skip_group_check=True)
                    if v == 1:
                        ins.then_inc(s["scores"], 1)

                def times_v(t, j, half):
                    if half == 0:
                        wait(pe, "exps", 2 * T, t, 2 * j + 2)
                    if j == 0 and half == 0:
                        wait(pe, "o_sb", 1, t, 0)
                    for r in (2 * half, 2 * half + 1):
                        nc.tensor.matmul(psO[32 * r:32 * r + GW, 0:GH * P], V[:, j, r, :],
                                         ET[:, j % 2, GH * r:GH * (r + 1), :].rearrange("p h i -> p (h i)"),
                                         start=j == 0, stop=j == T - 1, skip_group_check=True)
                        ins = nc.tensor.matmul(psO[32 * r:32 * r + VW, GH * P:(GH + 1) * P], V1[:, j, r, :],
                                               ET[:, j % 2, GH * GROUPS + r, :], start=False, stop=j == T - 1,
                                               skip_group_check=True)
                    if half == 1:
                        ins.then_inc(s["av"], 1)

                def maxima(t, lo, hi):
                    for m in range(lo, hi):
                        h, c = divmod(m, S // NS)
                        wait(pe, "mxused", MAXS, t, m - 1)
                        nc.tensor.matmul(psM[:, m % 2, :], qnext[0:ROWS, h // 2, h % 2, :],
                                         kst[0:ROWS, h // 2, c * NS:(c + 1) * NS], start=True,
                                         stop=True).then_inc(s["mxs"], 1)

                def shift(t):
                    wait(pe, "sh", 6, t, 6)
                    wait(pe, "y", 1, t, -1)
                    nc.tensor.transpose(psX[:, 0:P], sh[:, :], C("ident")).then_inc(s["shps"], 1)

                def outputs(t):
                    wait(pe, "o_sb", 1, t, 1)
                    wait(pe, "shT", 1, t, 2)
                    for gr in range(4):
                        ins = nc.tensor.transpose(psX[:, gr * P:(gr + 1) * P], osb[:, gr * P:(gr + 1) * P], C("ident"))
                    ins.then_inc(s["o_ps"], 1)

                def out_transpose(t):
                    wait(pe, "att", GH + 1, t, GH + 1)
                    nc.tensor.transpose(psX[:, 0:P], att[:, :, :].rearrange("p h d -> p (h d)"),
                                        C("ident")).then_inc(s["aT_ps"], 1)

                def out_project(t):
                    wait(pe, "aT", 1, t, 1)
                    nc.tensor.matmul(psX[:, P:2 * P], attT[:, :], C("woT"), start=True, stop=True).then_inc(s["y_ps"], 1)

                def tile(t, first, last):
                    for j in range(T):
                        if j % JC == 0:
                            wait(pe, f"st_in{j // JC}", 32 * BLOCKS, t, 32 * BLOCKS)
                        lo = PER_KEY_TILE * (j - 1)
                        for n in range(6):
                            if not last and (j, n) == (14, 3):
                                shift(t + 1)
                            if n < 4:
                                scores(t, j, n // 2, n % 2)
                            elif j > 0:
                                times_v(t, j - 1, n - 4)
                            elif not first:
                                times_v(t - 1, T - 1, n - 4)
                            if not last and (j, n) == (1, 0):
                                wait(pe, "q_in", 32, t, 64)
                            if not last and j > 0 and n < PER_KEY_TILE and lo + n < MAXS:
                                maxima(t + 1, lo + n, lo + n + 1)
                        if not first:
                            if j == 2:
                                outputs(t - 1)
                            if j == 4:
                                out_transpose(t - 1)
                            if j == 6:
                                out_project(t - 1)

                pe.wait_ge(s["zero_o"], 1)
                pe.wait_ge(s["q_in"], 32)
                maxima(0, 0, MAXS)
                shift(0)
                tile(0, True, False)
                with pe.Fori(1, T - 1) as t:
                    tile(t, False, False)
                tile(T - 1, False, True)
                for half in range(2):
                    times_v(T - 1, T - 1, half)
                pe.wait_ge(s["o_sb"], T)
                pe.wait_ge(s["y"], T - 1)
                for gr in range(4):
                    ins = nc.tensor.transpose(psX[:, gr * P:(gr + 1) * P], osb[:, gr * P:(gr + 1) * P], C("ident"))
                ins.then_inc(s["o_ps"], 1)
                out_transpose(T - 1)
                out_project(T - 1)


def experts(nc, sb, sem, g):
    C, xs, banks = g["C"], g["xs"], g["banks"]
    stats, mv, rstd, cst = g["stats"], g["mv"], g["rstd"], g["cst"]
    w1, w2, out = g["w1"], g["w2"], g["out"]
    with ExitStack() as ctx:
        xn = sb("xn2", [P, T, D], F32, ctx)
        xT = sb("xT2", [P, S], F32, ctx)
        hr = sb("hr", [P, T, R1], F32, ctx)
        hg = sb("hg", [P, T, R1], F32, ctx)
        hT = sb("hT", [P, T // 2, P], F32, ctx)
        wr2 = sb("wr2", [P, E], F32, ctx)
        lgt = sb("lgt", [P, T, E], F32, ctx)
        row = sb("row", [P, T], F32, ctx)
        pairs = sb("pairs", [P, T, E, E], F32, ctx)
        same = sb("same", [P, T, E, E], F32, ctx)
        wts = sb("wts", [P, T, E], F32, ctx)
        wtT = sb("wtT", [P, P], F32, ctx)
        b2own = sb("b2own", [P, T, D], F32, ctx)
        w1s = sb("w1s", [P, 2, 2 * F], F32, ctx)
        w1p = sb("w1p", [P, 2, 2, 2 * F], F16, ctx)
        xp = sb("xp", [P, 2, S], F16, ctx)
        wscale = sb("wscale", [P, 1], F32, ctx)
        down_wts = sb("down_wts", [P, T, E], F32, ctx)
        w2s = sb("w2s", [P, 2, FT, D], F32, ctx)
        G = sb("G", [P, 2, NS], F32, ctx)
        hid = sb("hid", [P, 2, FT, NS], F32, ctx)
        b1s = sb("b1s", [P, 2, 2 * FT], F32, ctx)
        b1_dram = g["consts"][:, AT["b1"]]

        names = ["dv", "wsc", "rs", "xn", "xt_ps", "xt", "h_ps", "h", "hst", "hrs", "hn", "gelu", "hT_ps", "hT",
                 "l_ps", "lg", "ex", "r", "w", "wT_ps", "wT", "own", "b2_ps", "x2",
                 "w_in0", "w_in1", "w_hi0", "w_hi1", "w_lo0", "w_lo1", "b1_sc0", "b1_sc1", "x_hi", "x_lo", "wd", "x2ps", "x1ps", "gl", "hd", "yps", "acc", "out"]
        s = {n: sem("e_" + n, ctx) for n in names}
        UP = FC * FT

        RING = [n % 3 for n in range(UP - 1)] + [1]

        def last_user(n):
            return max(m for m in range(-UP, n) if RING[m % UP] == RING[n])

        AHEAD = 3
        START = {"gl": 3, "hd": 3, "yps": 2, "acc": T}

        def wait(eng, name, per, e, more):
            if isinstance(e, int) and e * per + more <= 0:
                return
            eng.wait_ge(s[name], e * per + more + START.get(name, 0))

        with nc.Block() as block:

            @block.sync
            def _(sp):
                def load(e, buf):
                    if not isinstance(e, int):
                        wait(sp, "yps", FC, e, -FC)
                    sp.dma_start(w1s[:, buf, :], w1[bass.ds(e, 1), :, :].rearrange("a c f -> c (a f)")).then_inc(s[f"w_in{buf}"], 16)
                    sp.dma_start(w2s[:, buf, :, :],
                                 w2[bass.ds(e, 1), :, :].rearrange("a (n p) d -> p (a n) d", p=P)).then_inc(s[f"w_in{buf}"], 16)
                    sp.dma_start(b1s[:, buf, :], b1_dram[:, bass.ds(e * 2 * FT, 2 * FT)]).then_inc(s[f"w_in{buf}"], 16)

                load(0, 0)
                load(1, 1)
                with sp.Fori(1, E // 2) as p:
                    load(2 * p, 0)
                    load(2 * p + 1, 1)
                for c in range(FC):
                    wait(sp, "acc", T, E - 1, 4 * (c + 1))
                    sp.dma_start(out.rearrange("(t p) d -> p t d", p=P)[:, 4 * c:4 * c + 4, :],
                                 xs[:, 4 * c:4 * c + 4, :]).then_inc(s["out"], 16)
                sp.wait_ge(s["out"], 16 * FC)

            @block.gpsimd
            def _(pool):
                def split(e, buf, pair):
                    pool.wait_ge(s[f"w_in{buf}"], pair * 48 + 48)
                    if not isinstance(e, int):
                        wait(pool, "x1ps", UP, e, -UP)
                    by = wscale[:, :].to_broadcast([P, 2 * F])
                    nc.gpsimd.tensor_tensor(w1p[:, buf, 0, :], w1s[:, buf, :], by, ALU.mult).then_inc(s[f"w_hi{buf}"], 1)
                    nc.gpsimd.tensor_tensor(w1s[:, buf, :], w1s[:, buf, :], by, ALU.mult).then_inc(s[f"w_hi{buf}"], 1)
                    pool.wait_ge(s[f"w_hi{buf}"], pair * 2 + 2)
                    nc.gpsimd.tensor_tensor(w1p[:, buf, 1, :], w1s[:, buf, :], w1p[:, buf, 0, :],
                                            ALU.subtract).then_inc(s[f"w_lo{buf}"], 1)
                    nc.gpsimd.tensor_tensor(b1s[:, buf, 0:FT], b1s[:, buf, 0:FT],
                                            wscale[:, :].to_broadcast([P, FT]), ALU.mult).then_inc(s[f"b1_sc{buf}"], 1)

                nc.gpsimd.memset(wscale[:, :], WSCALE).then_inc(s["wsc"], 1)
                pool.wait_ge(s["wsc"], 1)
                nc.gpsimd.tensor_copy(wr2[:, :], C("wr2")).then_inc(s["own"], 1)
                split(0, 0, 0)
                for c in range(FC):
                    cols = slice(c * NS, (c + 1) * NS)
                    pool.wait_ge(s["x_hi"], c + 1)
                    nc.gpsimd.tensor_tensor(xp[:, 1, cols], xT[:, cols], xp[:, 0, cols],
                                            ALU.subtract).then_inc(s["x_lo"], 1)
                nc.gpsimd.tensor_tensor(b2own[:, :, :], C("b2").rearrange("p (a d) -> p a d", a=1).to_broadcast([P, T, D]),
                                        C("own").rearrange("p (t a) -> p t a", a=1).to_broadcast([P, T, D]),
                                        ALU.mult).then_inc(s["own"], 1)
                split(1, 1, 0)
                with pool.Fori(1, E // 2) as p:
                    split(2 * p, 0, p)
                    split(2 * p + 1, 1, p)

            @block.vector
            def _(dve):
                for t in range(T):
                    nc.vector.bn_aggr(mv[:, t, :], stats[:, t, :]).then_inc(s["dv"], 1)
                dve.wait_ge(s["dv"], T)
                rstd_of_variance(nc, dve, s["rs"], LN_EPS, g)
                for t in range(T):
                    nc.vector.tensor_scalar(xn[:, t, :], xs[:, t, :], mv[:, t, 0:1], rstd[:, t:t + 1],
                                            ALU.subtract, ALU.mult).then_inc(s["xn"], 1)
                for c in range(2):
                    dve.wait_ge(s["h_ps"], c + 1)
                    nc.vector.tensor_tensor(hr[:, 8 * c:8 * c + 8, :], banks[6 + c].rearrange("p (t n) -> p t n", n=R1),
                                            C("br1").rearrange("p (a n) -> p a n", a=1).to_broadcast([P, 8, R1]),
                                            ALU.add).then_inc(s["h"], 1)
                dve.wait_ge(s["h"], 2)
                dve.wait_ge(s["xn"], T)
                for t in range(T):
                    nc.vector.bn_stats(stats[:, t, :], hr[:, t, :]).then_inc(s["hst"], 1)
                for t in range(T):
                    dve.wait_ge(s["hst"], t + 1)
                    nc.vector.bn_aggr(mv[:, t, :], stats[:, t, :]).then_inc(s["hst"], 1)
                dve.wait_ge(s["hst"], 2 * T)
                rstd_of_variance(nc, dve, s["hrs"], ROUTER_EPS, g)
                for t in range(T):
                    nc.vector.tensor_scalar(hr[:, t, :], hr[:, t, :], mv[:, t, 0:1], rstd[:, t:t + 1],
                                            ALU.subtract, ALU.mult).then_inc(s["hn"], 1)
                dve.wait_ge(s["hn"], T)
                nc.vector.tensor_tensor(hr[:, :, :], hr[:, :, :], C("lns").rearrange("p (a n) -> p a n", a=1).to_broadcast([P, T, R1]),
                                        ALU.mult).then_inc(s["hn"], 1)
                dve.wait_ge(s["hn"], T + 1)
                nc.vector.tensor_tensor(hr[:, :, :], hr[:, :, :], C("lnb").rearrange("p (a n) -> p a n", a=1).to_broadcast([P, T, R1]),
                                        ALU.add).then_inc(s["hn"], 1)
                def up(e, buf, n):
                    c, ft = divmod(n, FT)
                    wait(dve, "x1ps", UP, e, n + 1)
                    wait(dve, "gl", UP, e, n + 1)
                    if ft == 0:
                        wait(dve, "yps", FC, e, c - 1)
                    nc.vector.scalar_tensor_tensor(hid[:, c % 2, ft, :], banks[3 + RING[n]],
                                                   b1s[:, buf, ft:ft + 1], G[:, n % 2, :],
                                                   ALU.add, ALU.mult).then_inc(s["hd"], 1)

                dve.sem_inc(s["hd"], START["hd"])
                dve.wait_ge(s["b1_sc0"], 1)
                for n in range(AHEAD):
                    up(0, 0, n)
                dve.wait_ge(s["l_ps"], 2)
                for z in range(2):
                    nc.vector.tensor_tensor(lgt[:, z:T:2, :], banks[6 + z][:, 0:T // 2 * E].rearrange("p (t e) -> p t e", e=E),
                                            C("br2").rearrange("p (a e) -> p a e", a=1).to_broadcast([P, T // 2, E]),
                                            ALU.add).then_inc(s["lg"], 1)
                dve.wait_ge(s["lg"], 2)
                nc.vector.reduce_max(row[:, :], lgt[:, :, :], AX_X).then_inc(s["r"], 1)
                dve.wait_ge(s["r"], 1)
                nc.vector.tensor_tensor(lgt[:, :, :], lgt[:, :, :], row[:, :].rearrange("p (t a) -> p t a", a=1).to_broadcast([P, T, E]),
                                        ALU.subtract).then_inc(s["r"], 1)
                dve.wait_ge(s["ex"], 1)
                nc.vector.reduce_sum(row[:, :], lgt[:, :, :], AX_X).then_inc(s["r"], 1)
                dve.wait_ge(s["r"], 3)
                nc.vector.reciprocal(row[:, :], row[:, :]).then_inc(s["r"], 1)
                dve.wait_ge(s["r"], 4)
                nc.vector.tensor_tensor(lgt[:, :, :], lgt[:, :, :], row[:, :].rearrange("p (t a) -> p t a", a=1).to_broadcast([P, T, E]),
                                        ALU.mult).then_inc(s["r"], 1)
                dve.wait_ge(s["r"], 5)
                mine = lgt[:, :, :].rearrange("p t (e a) -> p t e a", a=1).to_broadcast([P, T, E, E])
                other = lgt[:, :, :].rearrange("p t (a e) -> p t a e", a=1).to_broadcast([P, T, E, E])
                nc.vector.tensor_tensor(pairs[:, :, :, :], other, mine, ALU.is_gt).then_inc(s["r"], 1)
                nc.vector.tensor_tensor(same[:, :, :, :], other, mine, ALU.is_equal).then_inc(s["r"], 1)
                dve.wait_ge(s["r"], 7)
                flat = lambda a: a[:, :, :, :].rearrange("p t e f -> p t (e f)")
                nc.vector.tensor_tensor(flat(same), flat(same), C("before").rearrange("p (a n) -> p a n", a=1).to_broadcast([P, T, E * E]),
                                        ALU.mult).then_inc(s["r"], 1)
                dve.wait_ge(s["r"], 8)
                nc.vector.tensor_tensor(flat(pairs), flat(pairs), flat(same), ALU.add).then_inc(s["r"], 1)
                dve.wait_ge(s["r"], 9)
                nc.vector.reduce_sum(wts[:, :, :], pairs[:, :, :, :], AX_X).then_inc(s["r"], 1)
                dve.wait_ge(s["r"], 10)
                nc.vector.tensor_scalar(wts[:, :, :], wts[:, :, :], 1.5, None, ALU.is_lt).then_inc(s["r"], 1)
                dve.wait_ge(s["r"], 11)
                nc.vector.tensor_tensor(wts[:, :, :], wts[:, :, :], lgt[:, :, :], ALU.mult).then_inc(s["r"], 1)
                dve.wait_ge(s["r"], 12)
                nc.vector.reduce_sum(row[:, :], wts[:, :, :], AX_X).then_inc(s["r"], 1)
                dve.wait_ge(s["r"], 13)
                nc.vector.reciprocal(row[:, :], row[:, :]).then_inc(s["r"], 1)
                dve.wait_ge(s["r"], 14)
                nc.vector.tensor_tensor(wts[:, :, :], wts[:, :, :], row[:, :].rearrange("p (t a) -> p t a", a=1).to_broadcast([P, T, E]),
                                        ALU.mult).then_inc(s["w"], 1)
                dve.wait_ge(s["w"], 1)
                nc.vector.tensor_scalar(down_wts[:, :, :], wts[:, :, :], 1.0 / WSCALE, None, ALU.mult).then_inc(s["wd"], 1)
                dve.wait_ge(s["wT_ps"], 1)
                nc.vector.tensor_copy(wtT[:, :], banks[6][:, P:2 * P]).then_inc(s["wT"], 1)
                for c in range(FC):
                    dve.wait_ge(s["b2_ps"], c + 1)
                    v = xs[:, 4 * c:4 * c + 4, :]
                    nc.vector.tensor_tensor(v, v, banks[7 - c % 2].rearrange("p (t d) -> p t d", t=4), ALU.add).then_inc(s["x2"], 1)
                dve.wait_ge(s["x2"], FC)

                def gather(e, c, back=0):
                    wait(dve, "yps", FC, e, c + 1 - back * FC)
                    for t in range(4):
                        wait(dve, "acc", T, e, 4 * c + t - T + 1 - back * T)
                        nc.vector.scalar_tensor_tensor(xs[:, 4 * c + t, :], banks[6 + c % 2][:, t * P:(t + 1) * P],
                                                       down_wts[:, 4 * c + t, bass.ds(e - back, 1)], xs[:, 4 * c + t, :],
                                                       ALU.mult, ALU.add).then_inc(s["acc"], 1)

                dve.wait_ge(s["wd"], 1)
                dve.sem_inc(s["acc"], START["acc"])

                def expert(e, buf, pair, first=False):
                    dve.wait_ge(s[f"b1_sc{buf}"], pair + 1)
                    for c in range(FC):
                        for ft in range(FT):
                            if not (first and c * FT + ft < AHEAD):
                                up(e, buf, c * FT + ft)
                            if ft == 1 and c > 0:
                                gather(e, c - 1)
                            elif ft == 1 and not first:
                                gather(e, FC - 1, back=1)

                expert(0, 0, 0, first=True)
                expert(1, 1, 0)
                with dve.Fori(1, E // 2) as p:
                    expert(2 * p, 0, p)
                    expert(2 * p + 1, 1, p)
                gather(E - 1, FC - 1)

            @block.scalar
            def _(act):
                rstd_root(nc, act, s["rs"], g)
                for c in range(FC):
                    act.wait_ge(s["xt_ps"], c + 1)
                    nc.scalar.copy(xT[:, c * NS:(c + 1) * NS], banks[c]).then_inc(s["xt"], 1)
                for c in range(FC):
                    act.wait_ge(s["xt"], c + 1)
                    nc.scalar.copy(xp[:, 0, c * NS:(c + 1) * NS], xT[:, c * NS:(c + 1) * NS]).then_inc(s["x_hi"], 1)
                rstd_root(nc, act, s["hrs"], g)
                act.wait_ge(s["hn"], T + 2)
                nc.scalar.activation(hg[:, :, :], hr[:, :, :], ACT.Gelu_apprx_tanh).then_inc(s["gelu"], 1)
                for c in range(2):
                    act.wait_ge(s["hT_ps"], c + 1)
                    nc.scalar.copy(hT[:, 4 * c:4 * c + 4, :], banks[6 + c].rearrange("p (t n) -> p t n", n=P)).then_inc(s["hT"], 1)
                def up(e, buf, n):
                    wait(act, "x2ps", UP, e, n + 1)
                    wait(act, "hd", UP, e, n - 1)
                    nc.scalar.activation(G[:, n % 2, :], banks[RING[n]], ACT.Gelu_apprx_tanh,
                                         bias=b1s[:, buf, FT + n % FT:FT + n % FT + 1],
                                         scale=1.0 / WSCALE).then_inc(s["gl"], 1)

                act.sem_inc(s["gl"], START["gl"])
                act.wait_ge(s["w_in0"], 48)
                for n in range(AHEAD):
                    up(0, 0, n)
                act.wait_ge(s["r"], 2)
                nc.scalar.activation(lgt[:, :, :], lgt[:, :, :], ACT.Exp).then_inc(s["ex"], 1)

                def expert(e, buf, pair, first=0):
                    act.wait_ge(s[f"w_in{buf}"], pair * 48 + 48)
                    for n in range(first, UP):
                        up(e, buf, n)

                expert(0, 0, 0, first=AHEAD)
                expert(1, 1, 0)
                with act.Fori(1, E // 2) as p:
                    expert(2 * p, 0, p)
                    expert(2 * p + 1, 1, p)

            @block.tensor
            def _(pe):
                for t in range(T):
                    pe.wait_ge(s["xn"], t + 1)
                    ins = nc.tensor.transpose(banks[t // 4][:, (t % 4) * P:(t % 4 + 1) * P], xn[:, t, :], C("ident"))
                    if t % 4 == 3:
                        ins.then_inc(s["xt_ps"], 1)
                pe.wait_ge(s["xt"], FC)
                for t in range(T):
                    ins = nc.tensor.matmul(banks[6 + t // 8][:, (t % 8) * R1:(t % 8 + 1) * R1], xT[:, t * P:(t + 1) * P],
                                           C("wr1"), start=True, stop=True)
                    if t % 8 == 7:
                        ins.then_inc(s["h_ps"], 1)
                def up(e, buf, n):
                    c, ft = divmod(n, FT)
                    for half, done, used, bank in ((1, "x2ps", "gl", RING[n]), (0, "x1ps", "hd", 3 + RING[n])):
                        wait(pe, used, UP, e, last_user(n) + 1)
                        for k, (wpart, xpart) in enumerate(((0, 0), (0, 1), (1, 0))):
                            ins = nc.tensor.matmul(banks[bank], w1p[:, buf, wpart, half * F + ft * P:half * F + (ft + 1) * P],
                                                   xp[:, xpart, c * NS:(c + 1) * NS], start=k == 0, stop=k == 2)
                        ins.then_inc(s[done], 1)

                pe.wait_ge(s["w_lo0"], 1)
                pe.wait_ge(s["x_lo"], FC)
                for n in range(AHEAD):
                    up(0, 0, n)
                pe.wait_ge(s["gelu"], 1)
                for t in range(T // 2):
                    ins = nc.tensor.transpose(banks[6 + t // 4][:, (t % 4) * P:(t % 4 + 1) * P],
                                              hg[:, 2 * t:2 * t + 2, :].rearrange("p t n -> p (t n)"), C("ident"))
                    if t % 4 == 3:
                        ins.then_inc(s["hT_ps"], 1)
                pe.wait_ge(s["hT"], 2)
                pe.wait_ge(s["own"], 1)
                for t in range(T):
                    z = R1 * (t % 2)
                    ins = nc.tensor.matmul(banks[6 + t % 2][:, t // 2 * E:(t // 2 + 1) * E], hT[z:z + R1, t // 2, :],
                                           wr2[z:z + R1, :], start=True, stop=True)
                    if t >= T - 2:
                        ins.then_inc(s["l_ps"], 1)
                for n in range(AHEAD, 2 * AHEAD):
                    up(0, 0, n)
                pe.wait_ge(s["w"], 1)
                nc.tensor.transpose(banks[6][:, P:2 * P], wts[:, :, :].rearrange("p t e -> p (t e)"),
                                    C("ident")).then_inc(s["wT_ps"], 1)
                pe.wait_ge(s["wT"], 1)
                pe.wait_ge(s["own"], 2)
                for c in range(FC):
                    if c >= 2:
                        pe.wait_ge(s["x2"], c - 1)
                    nc.tensor.matmul(banks[7 - c % 2], wtT[:, :], b2own[:, 4 * c:4 * c + 4, :].rearrange("p t d -> p (t d)"),
                                     start=True, stop=True).then_inc(s["b2_ps"], 1)

                def down(e, buf, c, back=0):
                    wait(pe, "hd", UP, e, FT * (c + 1) - back * UP)
                    wait(pe, "acc", T, e, 4 * (c - 1) - back * T)
                    for t in range(4):
                        for ft in range(FT):
                            ins = nc.tensor.matmul(banks[6 + c % 2][:, t * P:(t + 1) * P],
                                                   hid[:, c % 2, ft, t * P:(t + 1) * P], w2s[:, buf, ft, :],
                                                   start=ft == 0, stop=ft == FT - 1)
                    ins.then_inc(s["yps"], 1)

                def expert(e, buf, pair, first=False):
                    pe.wait_ge(s[f"w_lo{buf}"], pair + 1)
                    for c in range(FC):
                        for ft in range(FT):
                            n = c * FT + ft
                            if not (first and n < 2 * AHEAD):
                                up(e, buf, n)
                            if ft == 1 and c > 0:
                                down(e, buf, c - 1)
                            elif ft == 1 and not first:
                                down(e, 1 - buf, FC - 1, back=1)

                pe.sem_inc(s["yps"], START["yps"])
                pe.wait_ge(s["x2"], FC)
                expert(0, 0, 0, first=True)
                expert(1, 1, 0)
                with pe.Fori(1, E // 2) as p:
                    expert(2 * p, 0, p)
                    expert(2 * p + 1, 1, p)
                down(E - 1, 1, FC - 1)


_NAMES = ["attn_Wq", "attn_bq", "attn_Wk", "attn_bk", "attn_Wv", "attn_bv", "attn_Wo", "attn_bo", "attn_rel_W",
          "attn_rel_b", "attn_logical_bias", "attn_gate_W", "attn_gate_b", "ffn_Wr1", "ffn_br1", "ffn_ln_scale",
          "ffn_ln_bias", "ffn_Wr2", "ffn_br2", "ffn_b1", "ffn_b2"]


def kernel(**inputs):
    import numpy as np
    import concourse.bacc as bacc
    from concourse.bass_utils import run_bass_kernel_spmd

    g = {n: np.asarray(inputs["L0_" + n]) for n in _NAMES}
    packed = np.zeros((P, CW_ALL), np.float32)

    def put(name, a):
        packed[:, AT[name]] = a

    for name, src in (("wvT", "attn_Wv"), ("woT", "attn_Wo"), ("gateT", "attn_gate_W")):
        put(name, g[src].T)
    by_row = np.arange(D).reshape(PAIRS, 2, HD).transpose(1, 2, 0).ravel()
    put("wqT", g["attn_Wq"][by_row].T)
    put("wkT", g["attn_Wk"][by_row].T)
    put("relI", g["attn_rel_W"][:, :D].T)
    put("relJ", g["attn_rel_W"][:, D:].T)
    put("bq", g["attn_bq"][by_row][:, None])
    put("bk", g["attn_bk"][by_row][:, None])
    for name, src in (("bv", "attn_bv"), ("bo", "attn_bo"), ("relb", "attn_rel_b"), ("gateb", "attn_gate_b"),
                      ("br1", "ffn_br1"), ("lns", "ffn_ln_scale"), ("lnb", "ffn_ln_bias"), ("br2", "ffn_br2")):
        put(name, g[src][None, :])
    put("bias", g["attn_logical_bias"].T.reshape(1, -1))
    put("ident", np.eye(P, dtype=np.float32))
    put("diag", np.tile(np.repeat(np.eye(IB, dtype=np.float32), 4, axis=0), (2, 1)))
    put("wr1", g["ffn_Wr1"])
    put("wr2", np.tile(g["ffn_Wr2"], (2, 1)))
    put("b2", np.tile(g["ffn_b2"], (T, 1)))
    put("own", np.repeat(np.eye(T, dtype=np.float32), E, axis=0))
    put("before", np.tri(E, E, -1, dtype=np.float32).reshape(1, -1))
    put("b1", g["ffn_b1"].reshape(E, 2 * FT, P).transpose(2, 0, 1).reshape(P, -1))

    nc = bacc.Bacc("TRN2", target_bir_lowering=False, num_devices=1)
    arrays, aps = {}, []
    for name, a in (("x", np.asarray(inputs["L0_attn_hidden_states"])[0]), ("consts", packed),
                    ("w1", np.asarray(inputs["L0_ffn_W1"])), ("w2", np.asarray(inputs["L0_ffn_W2"]))):
        arrays[name] = np.ascontiguousarray(a)
        aps.append(nc.dram_tensor(name, a.shape, F32, kind="ExternalInput").ap())
    out = nc.dram_tensor("out", (S, D), F32, kind="ExternalOutput").ap()
    build(nc, *aps, out)
    r = run_bass_kernel_spmd(nc, [arrays], core_ids=[0])
    return r.results[0]["out"].reshape(1, S, D)
```
